# Optimizing a Trainium2 kernel written in Bass

```python
import numpy as np
import jax
import jax.numpy as jnp

def _softmax(x, axis=-1):
    return jax.nn.softmax(x, axis=axis)

def _gelu(x):
    return jax.nn.gelu(x, approximate=True)

def _silu(x):
    return jax.nn.silu(x)

def _sigmoid(x):
    return jax.nn.sigmoid(x)

def _layernorm(x, axis=-1, eps=1e-05):
    m = jnp.mean(x, axis=axis, keepdims=True)
    v = jnp.var(x, axis=axis, keepdims=True)
    return (x - m) / jnp.sqrt(v + eps)

def _scatter_add(tgt, idx, src, axis=0):
    return tgt.at[idx].add(src)

def _segment_sum(src, seg, n):
    return jax.ops.segment_sum(src, seg, n)
kernel_name = 'mk_seq_preln_d2_jaxref_r4_7e42b8'

def setup_inputs(seed: int=0):
    np.random.seed(seed)
    _w = jnp.asarray

    def _L0_attn_setup():
        import jax, jax.numpy as jnp
        import numpy as np
        N_HEADS = 16
        D_MODEL = 256
        D_HEAD = D_MODEL // N_HEADS
        key = jax.random.key(seed)
        k1, k2, k3 = jax.random.split(key, 3)
        b, t, d = (2, 512, D_MODEL)
        x = jax.random.normal(k1, (b, t, d), dtype=jnp.float32)
        w_qkv = jax.random.normal(k2, (d, 3 * d), dtype=jnp.float32) * (1.0 / np.sqrt(d))
        w_out = jax.random.normal(k3, (d, d), dtype=jnp.float32) * (1.0 / np.sqrt(d))
        return {'x': x, 'w_qkv': w_qkv, 'w_out': w_out}
    _L0_attn_in = _L0_attn_setup()

    def _L0_ffn_setup():
        import jax, jax.numpy as jnp
        import numpy as np
        LN_EPS = 1e-05

        def entmax15(z):
            z = z / 2.0
            z = z - jnp.max(z, axis=-1, keepdims=True)
            zs = -jnp.sort(-z, axis=-1)
            k = jnp.arange(1, z.shape[-1] + 1, dtype=z.dtype)
            mean = jnp.cumsum(zs, axis=-1) / k
            meansq = jnp.cumsum(zs * zs, axis=-1) / k
            ss = k * (meansq - jnp.square(mean))
            delta = (1.0 - ss) / k
            tau = mean - jnp.sqrt(jnp.clip(delta, 0.0))
            support = jnp.sum((tau <= zs).astype(jnp.int32), axis=-1, keepdims=True)
            tau_star = jnp.take_along_axis(tau, support - 1, axis=-1)
            return jnp.square(jnp.clip(z - tau_star, 0.0))

        def layernorm_noaffine(v):
            m = jnp.mean(v, axis=-1, keepdims=True)
            var = jnp.mean(jnp.square(v - m), axis=-1, keepdims=True)
            return (v - m) / jnp.sqrt(var + LN_EPS)

        def cp_mumoe(x, gate, Win, Wout):
            ones = jnp.ones(x.shape[:-1] + (1,), x.dtype)
            xb = jnp.concatenate([x, ones], axis=-1)
            z = jnp.einsum('btd,dr->btr', xb, Win) * gate
            return jnp.einsum('btr,or->bto', z, Wout)
        key = jax.random.key(seed)
        ks = jax.random.split(key, 8)
        B, T, D, O, D2, E, R = (8, 512, 256, 1024, 256, 16, 128)
        s = lambda k, shape, scale: jax.random.normal(k, shape, jnp.float32) * scale
        return {'x': s(ks[0], (B, T, D), 1.0), 'proj': s(ks[1], (D, E), D ** (-0.5)), 'C1': s(ks[2], (E, R), E ** (-0.5)), 'Win1': s(ks[3], (D + 1, R), D ** (-0.5)), 'Wout1': s(ks[4], (O, R), R ** (-0.5)), 'C2': s(ks[5], (E, R), E ** (-0.5)), 'Win2': s(ks[6], (O + 1, R), O ** (-0.5)), 'Wout2': s(ks[7], (D2, R), R ** (-0.5))}
    _L0_ffn_in = _L0_ffn_setup()

    def _L1_attn_setup():
        import jax, jax.numpy as jnp
        import numpy as np
        import math
        B, T, C = (2, 512, 256)
        H, L = (16, 64)
        DH = C // H
        DHE = DH // 2
        THETA = 10000.0

        def _rope_cache(t, dim):
            inv_freq = 1.0 / THETA ** (jnp.arange(0, dim, 2, dtype=jnp.float32) / dim)
            freqs = jnp.arange(t, dtype=jnp.float32)[:, None] * inv_freq[None, :]
            emb = jnp.concatenate((freqs, freqs), axis=-1)
            return (jnp.cos(emb), jnp.sin(emb))

        def _apply_rope(x, cos, sin):
            x1 = x[..., 0::2]
            x2 = x[..., 1::2]
            rot = jnp.stack((-x2, x1), axis=-1).reshape(x.shape)
            return x * cos[None, None] + rot * sin[None, None]
        key = jax.random.key(seed)
        ks = jax.random.split(key, 10)
        s = 0.02
        return {'x': jax.random.normal(ks[0], (B, T, C), jnp.float32), 'Wq_down': jax.random.normal(ks[1], (C, H * L), jnp.float32) * s, 'Wk_down': jax.random.normal(ks[2], (C, H * L), jnp.float32) * s, 'Wv_down': jax.random.normal(ks[3], (C, H * L), jnp.float32) * s, 'Wq_up_c': jax.random.normal(ks[4], (L, DHE), jnp.float32) * s, 'Wq_up_e': jax.random.normal(ks[5], (L, DHE), jnp.float32) * s, 'Wk_up_c': jax.random.normal(ks[6], (L, DHE), jnp.float32) * s, 'Wk_up_e': jax.random.normal(ks[7], (L, DHE), jnp.float32) * s, 'Wv_up': jax.random.normal(ks[8], (L, DH), jnp.float32) * s, 'Wc': jax.random.normal(ks[9], (C, C), jnp.float32) * s}
    _L1_attn_in = _L1_attn_setup()

    def _L1_ffn_setup():
        import jax, jax.numpy as jnp
        import numpy as np
        D_MODEL = 256
        EXPERT_DIM = 128
        N_EXPERTS = 8
        TOP_K = 2

        def _sq_relu(h):
            return jnp.square(jax.nn.relu(h))
        key = jax.random.key(seed)
        ks = jax.random.split(key, 6)
        s = 0.02
        x = jax.random.normal(ks[0], (2, 512, D_MODEL), dtype=jnp.float32)
        Ws1 = jax.random.normal(ks[1], (D_MODEL, EXPERT_DIM), dtype=jnp.float32) * s
        Ws2 = jax.random.normal(ks[2], (EXPERT_DIM, D_MODEL), dtype=jnp.float32) * s
        W1 = jax.random.normal(ks[3], (N_EXPERTS, D_MODEL, EXPERT_DIM), dtype=jnp.float32) * s
        W2 = jax.random.normal(ks[4], (N_EXPERTS, EXPERT_DIM, D_MODEL), dtype=jnp.float32) * s
        Wr = jax.random.normal(ks[5], (D_MODEL, N_EXPERTS), dtype=jnp.float32) * s
        return {'x': x, 'Ws1': Ws1, 'Ws2': Ws2, 'W1': W1, 'W2': W2, 'Wr': Wr}
    _L1_ffn_in = _L1_ffn_setup()
    _d = {'L0_attn_x': _L0_attn_in['x'], 'L0_attn_w_qkv': _L0_attn_in['w_qkv'], 'L0_attn_w_out': _L0_attn_in['w_out'], 'L0_ffn_proj': _L0_ffn_in['proj'], 'L0_ffn_C1': _L0_ffn_in['C1'], 'L0_ffn_Win1': _L0_ffn_in['Win1'], 'L0_ffn_Wout1': _L0_ffn_in['Wout1'], 'L0_ffn_C2': _L0_ffn_in['C2'], 'L0_ffn_Win2': _L0_ffn_in['Win2'], 'L0_ffn_Wout2': _L0_ffn_in['Wout2'], 'L1_attn_Wq_down': _L1_attn_in['Wq_down'], 'L1_attn_Wk_down': _L1_attn_in['Wk_down'], 'L1_attn_Wv_down': _L1_attn_in['Wv_down'], 'L1_attn_Wq_up_c': _L1_attn_in['Wq_up_c'], 'L1_attn_Wq_up_e': _L1_attn_in['Wq_up_e'], 'L1_attn_Wk_up_c': _L1_attn_in['Wk_up_c'], 'L1_attn_Wk_up_e': _L1_attn_in['Wk_up_e'], 'L1_attn_Wv_up': _L1_attn_in['Wv_up'], 'L1_attn_Wc': _L1_attn_in['Wc'], 'L1_ffn_Ws1': _L1_ffn_in['Ws1'], 'L1_ffn_Ws2': _L1_ffn_in['Ws2'], 'L1_ffn_W1': _L1_ffn_in['W1'], 'L1_ffn_W2': _L1_ffn_in['W2'], 'L1_ffn_Wr': _L1_ffn_in['Wr']}
    _x0 = _d['L0_attn_x']
    _d['L0_attn_x'] = jax.random.normal(jax.random.fold_in(jax.random.key(seed), 1), (8, 1024, 256), dtype=_x0.dtype)
    del _x0
    return _d

def reference(L0_attn_x, L0_attn_w_qkv, L0_attn_w_out, L0_ffn_proj, L0_ffn_C1, L0_ffn_Win1, L0_ffn_Wout1, L0_ffn_C2, L0_ffn_Win2, L0_ffn_Wout2, L1_attn_Wq_down, L1_attn_Wk_down, L1_attn_Wv_down, L1_attn_Wq_up_c, L1_attn_Wq_up_e, L1_attn_Wk_up_c, L1_attn_Wk_up_e, L1_attn_Wv_up, L1_attn_Wc, L1_ffn_Ws1, L1_ffn_Ws2, L1_ffn_W1, L1_ffn_W2, L1_ffn_Wr):

    def _L0_attn_ref(x, w_qkv, w_out):
        import jax, jax.numpy as jnp
        import numpy as np
        N_HEADS = 16
        D_MODEL = 256
        D_HEAD = D_MODEL // N_HEADS
        b, t, d = x.shape
        h, dh = (N_HEADS, D_HEAD)
        qkv = x @ w_qkv
        q, k, v = jnp.split(qkv, 3, axis=-1)
        q = q.reshape(b, t, h, dh).transpose(0, 2, 1, 3)
        k = k.reshape(b, t, h, dh).transpose(0, 2, 1, 3)
        v = v.reshape(b, t, h, dh).transpose(0, 2, 1, 3)
        scale = 1.0 / np.sqrt(dh).astype(np.float32)
        att = jnp.einsum('bhqd,bhkd->bhqk', q, k) * scale
        causal = jnp.tril(jnp.ones((t, t), dtype=bool))
        att = jnp.where(causal, att, -jnp.inf)
        att = jax.nn.softmax(att, axis=-1)
        y = jnp.einsum('bhqk,bhkd->bhqd', att, v)
        y = y.transpose(0, 2, 1, 3).reshape(b, t, d)
        return y @ w_out

    def _L0_ffn_ref(x, proj, C1, Win1, Wout1, C2, Win2, Wout2):
        import jax, jax.numpy as jnp
        import numpy as np
        LN_EPS = 1e-05

        def entmax15(z):
            z = z / 2.0
            z = z - jnp.max(z, axis=-1, keepdims=True)
            zs = -jnp.sort(-z, axis=-1)
            k = jnp.arange(1, z.shape[-1] + 1, dtype=z.dtype)
            mean = jnp.cumsum(zs, axis=-1) / k
            meansq = jnp.cumsum(zs * zs, axis=-1) / k
            ss = k * (meansq - jnp.square(mean))
            delta = (1.0 - ss) / k
            tau = mean - jnp.sqrt(jnp.clip(delta, 0.0))
            support = jnp.sum((tau <= zs).astype(jnp.int32), axis=-1, keepdims=True)
            tau_star = jnp.take_along_axis(tau, support - 1, axis=-1)
            return jnp.square(jnp.clip(z - tau_star, 0.0))

        def layernorm_noaffine(v):
            m = jnp.mean(v, axis=-1, keepdims=True)
            var = jnp.mean(jnp.square(v - m), axis=-1, keepdims=True)
            return (v - m) / jnp.sqrt(var + LN_EPS)

        def cp_mumoe(x, gate, Win, Wout):
            ones = jnp.ones(x.shape[:-1] + (1,), x.dtype)
            xb = jnp.concatenate([x, ones], axis=-1)
            z = jnp.einsum('btd,dr->btr', xb, Win) * gate
            return jnp.einsum('btr,or->bto', z, Wout)
        a = entmax15(layernorm_noaffine(jnp.einsum('btd,de->bte', x, proj)))
        g1 = jnp.einsum('bte,er->btr', a, C1)
        h = cp_mumoe(x, g1, Win1, Wout1)
        h = jax.nn.gelu(h, approximate=False)
        g2 = jnp.einsum('bte,er->btr', a, C2)
        return cp_mumoe(h, g2, Win2, Wout2)

    def _L1_attn_ref(x, Wq_down, Wk_down, Wv_down, Wq_up_c, Wq_up_e, Wk_up_c, Wk_up_e, Wv_up, Wc):
        import jax, jax.numpy as jnp
        import numpy as np
        import math
        B, T, C = (2, 512, 256)
        H, L = (16, 64)
        DH = C // H
        DHE = DH // 2
        THETA = 10000.0

        def _rope_cache(t, dim):
            inv_freq = 1.0 / THETA ** (jnp.arange(0, dim, 2, dtype=jnp.float32) / dim)
            freqs = jnp.arange(t, dtype=jnp.float32)[:, None] * inv_freq[None, :]
            emb = jnp.concatenate((freqs, freqs), axis=-1)
            return (jnp.cos(emb), jnp.sin(emb))

        def _apply_rope(x, cos, sin):
            x1 = x[..., 0::2]
            x2 = x[..., 1::2]
            rot = jnp.stack((-x2, x1), axis=-1).reshape(x.shape)
            return x * cos[None, None] + rot * sin[None, None]
        b, t, c = x.shape
        q_lat = (x @ Wq_down).reshape(b, t, H, L)
        k_lat = (x @ Wk_down).reshape(b, t, H, L)
        v_lat = (x @ Wv_down).reshape(b, t, H, L)
        q_c = jnp.einsum('bthl,ld->bhtd', q_lat, Wq_up_c)
        q_e = jnp.einsum('bthl,ld->bhtd', q_lat, Wq_up_e)
        k_c = jnp.einsum('bthl,ld->bhtd', k_lat, Wk_up_c)
        k_e = jnp.einsum('bthl,ld->bhtd', k_lat, Wk_up_e)
        v = jnp.einsum('bthl,ld->bhtd', v_lat, Wv_up)
        cos, sin = _rope_cache(t, DHE)
        q = jnp.concatenate([q_c, _apply_rope(q_e, cos, sin)], axis=-1)
        k = jnp.concatenate([k_c, _apply_rope(k_e, cos, sin)], axis=-1)
        scale = 1.0 / math.sqrt(DH)
        scores = jnp.einsum('bhqd,bhkd->bhqk', q, k) * scale
        causal = jnp.tril(jnp.ones((t, t), dtype=bool))
        scores = jnp.where(causal[None, None], scores, -jnp.inf)
        att = jax.nn.softmax(scores, axis=-1)
        y = jnp.einsum('bhqk,bhkd->bhqd', att, v)
        y = y.transpose(0, 2, 1, 3).reshape(b, t, c)
        return y @ Wc

    def _L1_ffn_ref(x, Ws1, Ws2, W1, W2, Wr):
        import jax, jax.numpy as jnp
        import numpy as np
        D_MODEL = 256
        EXPERT_DIM = 128
        N_EXPERTS = 8
        TOP_K = 2

        def _sq_relu(h):
            return jnp.square(jax.nn.relu(h))
        shape = x.shape
        xf = x.reshape(-1, D_MODEL)
        out_shared = _sq_relu(xf @ Ws1) @ Ws2
        logits = xf @ Wr
        top_vals, top_idx = jax.lax.top_k(logits, TOP_K)
        rw = jax.nn.softmax(top_vals.astype(jnp.float32), axis=-1).astype(x.dtype)
        onehot = jax.nn.one_hot(top_idx, N_EXPERTS, dtype=x.dtype)
        prob = jnp.einsum('tk,tke->te', rw, onehot)
        prob = jnp.trunc(prob)
        h = _sq_relu(jnp.einsum('td,edf->tef', xf, W1))
        y = jnp.einsum('tef,efd->ted', h, W2)
        out_routed = jnp.einsum('ted,te->td', y, prob)
        return (out_shared + out_routed).reshape(shape)
    x = L0_attn_x
    x = x + _L0_attn_ref(_layernorm(x, axis=-1), L0_attn_w_qkv, L0_attn_w_out)
    x = x + _L0_ffn_ref(_layernorm(x, axis=-1), L0_ffn_proj, L0_ffn_C1, L0_ffn_Win1, L0_ffn_Wout1, L0_ffn_C2, L0_ffn_Win2, L0_ffn_Wout2)
    x = x + _L1_attn_ref(_layernorm(x, axis=-1), L1_attn_Wq_down, L1_attn_Wk_down, L1_attn_Wv_down, L1_attn_Wq_up_c, L1_attn_Wq_up_e, L1_attn_Wk_up_c, L1_attn_Wk_up_e, L1_attn_Wv_up, L1_attn_Wc)
    x = x + _L1_ffn_ref(_layernorm(x, axis=-1), L1_ffn_Ws1, L1_ffn_Ws2, L1_ffn_W1, L1_ffn_W2, L1_ffn_Wr)
    return x

_drawn_inputs = setup_inputs


def setup_inputs(seed=0):
    import zlib

    import numpy as np

    out = dict(_drawn_inputs(seed))
    spreads = {}
    factors = {'L0_ffn_proj': 3.75,
     'L0_ffn_C1': 3.802,
     'L0_ffn_Win1': 3.835,
     'L0_ffn_Wout1': 3.845,
     'L0_ffn_C2': 3.507,
     'L0_ffn_Win2': 3.585,
     'L0_ffn_Wout2': 3.627,
     'L1_attn_Wq_down': 8.0,
     'L1_attn_Wk_down': 8.0,
     'L1_attn_Wv_down': 8.0,
     'L1_attn_Wq_up_c': 8.0,
     'L1_attn_Wq_up_e': 8.0,
     'L1_attn_Wk_up_c': 8.0,
     'L1_attn_Wk_up_e': 8.0,
     'L1_attn_Wv_up': 8.0,
     'L1_attn_Wc': 8.0,
     'L1_ffn_Ws1': 8.0,
     'L1_ffn_Ws2': 8.0}
    for name, (base, spread) in spreads.items():
        noise = np.random.default_rng([zlib.crc32(name.encode()), seed]).standard_normal(out[name].shape)
        drawn = base * np.exp(spread * noise) if base else spread * noise
        out[name] = jnp.asarray(drawn.astype(out[name].dtype))
    for name, factor in factors.items():
        out[name] = (out[name] * factor).astype(out[name].dtype)
    return out
```

```python
import concourse.bass as bass
from concourse import mybir
from concourse.alu_op_type import AluOpType as ALU
from contextlib import ExitStack

F32 = mybir.dt.float32
BF16 = mybir.dt.bfloat16
ACT = mybir.ActivationFunctionType
AX = mybir.AxisListType

P = 128
BANK = 512
LN_EPS = 1e-5
NEG = -1.0e30
LOWEST = -3.0e38

B, T, D = 8, 1024, 256
H = 16
DH = D // H
TT = T // P
KD = D // P
NC = T // BANK
TPC = TT // NC
L = 64
E0, R, O = 16, 128, 1024
OC = O // P
NE, FE = 8, 128
HG = 4
NG = H // HG
MH = P // DH
SCALE = DH ** -0.5

NP = 3
ROWS_A = DH * 2 * NP
ROWS_S = ROWS_A + DH
ROWS = ROWS_S + NP
STACK_DMAS = 5
NBUF = 3

MAX_AT_STEP = [[7], [6], [5], [4], [3, 2], [1, 0], [], []]
MT_STEP = 6
NORM_STEP = 1


def score_parts(i):
    return [(p, min(BANK, P * (i + 1) - BANK * p)) for p in range(NC) if P * (i + 1) > BANK * p]


def query_range(j, c):
    return max(P * j, BANK * c), BANK * (c + 1)


def plan_banks():
    place, used = {}, [0] * 8

    def put(key, bank):
        place[key] = (bank, used[bank])
        used[bank] += 1

    turn = 0

    def ring(*key):
        nonlocal turn
        put(key, turn % 4)
        turn += 1

    totals = {}
    for l in range(2):
        for s in (2 * l,):
            for c in range(NC):
                for kd in range(KD):
                    ring("xt", s, c, kd)
        for c in range(NC):
            for w in range(2):
                ring("qk", l, 0, c, w)
        for tp in range(TT // 2):
            ring("v", l, tp)
        for c in range(NC):
            for w in range(2):
                ring("qk", l, 1, c, w)
        totals[l] = list(used)
        for c in range(NC):
            for kd in range(KD):
                ring("yt", l, c, kd)
        for tp in range(TT // 2):
            ring("ao", l, tp)
        for c in range(NC):
            for kd in range(KD):
                ring("xt", 2 * l + 1, c, kd)
        if l == 0:
            ring("logit")
            for c in range(NC):
                put(("h1", c), 4 + c)
            for c in range(NC):
                ring("at", c)
            for c in range(NC):
                ring("g1", c)
                ring("g2", c)
            for c in range(NC):
                for o in range(OC):
                    ring("hid", c, o)
                put(("z2", c), 6 + c)
                for tp in range(TPC // 2):
                    ring("fo", c, tp)
        else:
            ring("route")
            for c in range(NC):
                ring("he", NE, c)
                for tp in range(TPC // 2):
                    ring("eo", NE, c, tp)
            for e in range(NE):
                for c in range(NC):
                    ring("he", e, c)
                    for tp in range(TPC // 2):
                        ring("eo", e, c, tp)
    return place, totals


def plan_scores():
    index, n = {}, 0

    def put(*key):
        nonlocal n
        index[key] = n
        n += 1

    for l in range(2):
        for i in reversed(range(TT)):
            for h in range(HG):
                for p, _ in score_parts(i):
                    put("s", l, 0, i, h, p)
        put("mt", l, 0)
        for g in range(NG):
            for j in range(TT):
                if g + 1 < NG:
                    for h in range(HG):
                        for i in MAX_AT_STEP[j]:
                            for p, _ in score_parts(i):
                                put("s", l, g + 1, i, h, p)
                    if j == MT_STEP:
                        put("mt", l, g + 1)
                if g > 0 and j == NORM_STEP:
                    for c in range(NC):
                        put("nm", l, g - 1, c)
        for c in range(NC):
            put("nm", l, NG - 1, c)
    return index, n


def transformer_kernel(nc, x_d, w_qkv_d, w_out_d, proj_d, c1_d, win1_d, wout1_d, c2_d, win2_d, wout2_d,
                       wqd_d, wkd_d, wvd_d, wquc_d, wque_d, wkuc_d, wkue_d, wvu_d, wc_d,
                       ws1_d, ws2_d, w1_d, w2_d, wr_d, cos_d, sin_d, kidx_d, out_d):
    place, ring_before_main = plan_banks()
    sidx, n_scores = plan_scores()
    ctx = ExitStack()
    with ctx:
        def sb(name, shape, dt=F32):
            return ctx.enter_context(nc.sbuf_tensor(name, shape, dt))

        x_in = sb("x_in", [P, TT, D])
        x = sb("x", [P, TT, D])
        xn = sb("xn", [P, TT, D])
        xnT = sb("xnT", [P, KD, T])
        y, yT = xn, xnT
        parts = sb("parts", [P, 2, 2, NP, T], BF16)
        stk = sb("stk", [P, NBUF, 2, HG, T], BF16)
        probs = sb("probs", [P, 2, HG, T])
        vaug = sb("vaug", [P, TT, H, DH + 1])
        oT = sb("oT", [P, T])
        mx = sb("mx", [P, HG, TT, 2])
        negm = sb("negm", [P, HG * TT])
        negr = sb("negr", [P, HG * TT])
        mparts = sb("mparts", [P, NP, HG * TT], BF16)
        mT = sb("mT", [P, P], BF16)
        rec = sb("rec", [P, TPC, HG])
        st6 = sb("st6", [P, TT, 6])
        mv = sb("mv", [P, TT, 2])
        veps = sb("veps", [P, TT])
        rstd = sb("rstd", [P, TT])
        neg_half = sb("neg_half", [P, TT])
        wqkv = [sb(f"wqkv{l}", [P, KD, 3 * D]) for l in range(2)]
        wo = [sb(f"wo{l}", [P, KD, D]) for l in range(2)]
        projw = sb("projw", [P, KD, E0])
        c12 = sb("c12", [E0, 2, R])
        win1 = sb("win1", [P, KD, R])
        bias1 = sb("bias1", [P, 1])
        wout1T = sb("wout1T", [R, O])
        win2 = sb("win2", [P, OC, R])
        bias2 = sb("bias2", [P, 1])
        wout2T = sb("wout2T", [R, D])
        wr = sb("wr", [P, KD, NE])
        w1 = sb("w1", [P, NE + 1, KD, FE])
        w2 = sb("w2", [P, NE + 1, D])
        cos = sb("cos", [P, T])
        sin = sb("sin", [P, T])
        ident = sb("ident", [P, P])
        ident_b = sb("ident_b", [P, P], BF16)
        mask_b = sb("mask_b", [P, P], BF16)
        kidx = sb("kidx", [P, 2, E0])
        zsm = sb("zsm", [P, 4, TT])
        zc = sb("zc", [P, TT, E0])
        zt = sb("zt", [P, TT, E0])
        zu = sb("zu", [P, TT, E0])
        cum = oT[:, 0:3 * 2 * TT * E0].rearrange("p (a t k) -> p a t k", a=3, k=E0)
        gate = sb("gate", [P, TT, NE])
        flat = probs[:, :, :, :].rearrange("p a h t -> p (a h t)")
        scratch = [flat[:, BANK * i:BANK * (i + 1)] for i in range(16)]
        qf, qs, qc, qr = (scratch[2 * i:2 * i + 2] for i in range(4))
        aT = flat[0:E0, 0:T]
        gsb = [scratch[2 + i] for i in range(4)]
        z1 = scratch[6:8]
        hsb = scratch[8:12]
        z2 = scratch[12:14]
        hr = scratch[0:4]
        hq = scratch[4:8]
        down = flat[:, 0:3 * KD * H * L].rearrange("p (w k n) -> p w k n", w=3, k=KD)
        stage = stk[:, :, :, :, :].rearrange("p b w h t -> p (b w h t)").bitcast(F32)
        dT = stage[:, 0:3 * 8 * D].rearrange("p (w b d) -> p w b d", w=3, b=8)
        up = stage[:, 6144:6144 + 3 * DH].rearrange("p (w d) -> p w d", w=3)
        wo1_s = stage[:, 6400:6400 + OC * R].rearrange("p (o r) -> p o r", o=OC)
        wo2_s = stage[:, 7424:7424 + KD * R].rearrange("p (o r) -> p o r", o=KD)

        ps = ctx.enter_context(nc.psum_tensor("ps", [P, 8 * BANK], F32))
        bank = [ps[:, BANK * b:BANK * (b + 1)] for b in range(8)]
        st_pair = [ps[:, 2 * BANK * i:2 * BANK * (i + 1)] for i in range(2)]
        s_bank = bank[4:6]
        o_bank = bank[6:8]

        def sem(name):
            return ctx.enter_context(nc.semaphore(name))

        w_loaded = sem("w_loaded")
        w_const = sem("w_const")
        w_full = sem("w_full")
        w_drained = sem("w_drained")
        x_loaded = sem("x_loaded")
        stored = sem("stored")
        next_pass = sem("next_pass")
        first = part_done = sem("part_done")
        begun = sem("begun")
        full = [sem("full0")] + [sem(f"full{b}") for b in range(1, 8)]
        drained = [sem(f"drained{b}") for b in range(8)]
        ln_var = sem("ln_var")
        ln_rstd = sem("ln_rstd")
        xn_ready = sem("xn_ready")
        part0_ready = sem("part0_ready")
        rest_ready = sem("rest_ready")
        part1_ready = sem("part1_ready")
        parts_ready = sem("parts_ready")
        qcos_ready = sem("qcos_ready")
        rope_ready = sem("rope_ready")
        stk_loaded = [[sem(f"stk_loaded{b}_{h}") for h in range(HG)] for b in range(NBUF)]
        m_loaded = [sem(f"m_loaded{b}") for b in range(NBUF)]
        s_full = sem("s_full")
        s_drained = sem("s_drained")
        mx_ready = sem("mx_ready")
        st_full = sem("st_full")
        exp_done = sem("exp_done")
        p_ready = sem("p_ready")
        pv_done = sem("pv_done")
        o_drained = sem("o_drained")
        ent_var = sem("ent_var")
        ent_rstd = sem("ent_rstd")
        delta_ready = sem("delta_ready")
        sqrt_ready = sem("sqrt_ready")
        a_ready = sem("a_ready")
        h_used = sem("h_used")
        gap_ready = sem("gap_ready")
        egap_ready = sem("egap_ready")
        relu_ready = sem("relu_ready")
        hq_ready = sem("hq_ready")
        x_done = sem("x_done")
        act_chain = sem("act_chain")
        last = dve_chain = sem("dve_chain")
        pass_sems = range(first.num, last.num + 1)

        def arrived(eng, *key):
            b, n = place[key]
            eng.wait_ge(full[b], n + 1)
            return bank[b]

        def begin_pass(eng, b):
            eng.wait_ge(next_pass, b + 1)
            eng.sem_inc(begun, 1)

        def read_out(*key):
            return drained[place[key][0]]

        block = ctx.enter_context(nc.Block())

        @block.sync
        def _(sp):
            loads = [
                (wqkv[0][:], w_qkv_d.rearrange("(k p) n -> p k n", p=P)),
                (wo[0][:], w_out_d.rearrange("(k p) n -> p k n", p=P)),
                (down[:, 0], wqd_d.rearrange("(k p) n -> p k n", p=P)),
                (down[:, 1], wkd_d.rearrange("(k p) n -> p k n", p=P)),
                (down[:, 2], wvd_d.rearrange("(k p) n -> p k n", p=P)),
                (wo1_s, wout1_d.rearrange("(o p) r -> p o r", p=P)),
                (wo2_s, wout2_d.rearrange("(o p) r -> p o r", p=P)),
                (projw[:], proj_d.rearrange("(k p) n -> p k n", p=P)),
                (c12[:, 0], c1_d), (c12[:, 1], c2_d),
                (win1[:], win1_d[0:D, :].rearrange("(k p) r -> p k r", p=P)),
                (bias1[:], win1_d[D:D + 1, :].rearrange("a r -> r a")),
                (win2[:], win2_d[0:O, :].rearrange("(o p) r -> p o r", p=P)),
                (bias2[:], win2_d[O:O + 1, :].rearrange("a r -> r a")),
                (wo[1][:], wc_d.rearrange("(k p) n -> p k n", p=P)),
                (wr[:], wr_d.rearrange("(k p) n -> p k n", p=P)),
                (w1[:, NE], ws1_d.rearrange("(k p) f -> p k f", p=P)),
                (w2[:, NE], ws2_d),
                (cos[:], cos_d), (sin[:], sin_d), (kidx[:], kidx_d),
            ]
            for e in range(NE):
                loads.append((w1[:, e], w1_d[e].rearrange("(k p) f -> p k f", p=P)))
                loads.append((w2[:, e], w2_d[e]))
            half = DH // 2
            for r in range(2):
                rows = slice(L * r, L * (r + 1))
                loads += [(up[rows, 0, 0:half], wquc_d), (up[rows, 0, half:DH], wque_d),
                          (up[rows, 1, 0:half], wkuc_d), (up[rows, 1, half:DH], wkue_d),
                          (up[rows, 2], wvu_d)]
            sp.dma_start(x_in[:], x_d[0].rearrange("(t p) d -> p t d", p=P)).then_inc(x_loaded, 16)
            for dst, src in loads:
                sp.dma_start(dst, src).then_inc(w_loaded, 16)
            sp.wait_ge(w_loaded, 16 * len(loads))
            sp.sem_inc(w_const, 1)
            sp.sem_inc(stored, 16)
            sp.wait_ge(part_done, 4)
            sp.sem_clear(pass_sems)
            sp.sem_inc(next_pass, 1)

            def load_stack(l, g):
                m, buf = g // 2, g % NBUF
                sp.wait_ge(parts_ready, 8 * l + 4 * (m + 1))
                if NG * l + g >= NBUF:
                    sp.wait_ge(st_full, HG * TT * (NG * l + max(g - NBUF + 1, 0)))
                for h in range(HG):
                    rows = slice(DH * ((g % 2) * HG + h), DH * ((g % 2) * HG + h + 1))
                    ends = parts[rows, m].rearrange("d w p t -> d (w p) t")[:, 0:2 * NP:2 * NP - 1, :]
                    for t in range(2):
                        block = slice(DH * NP * t, DH * NP * (t + 1))
                        k = parts[rows, m, 1, t:t + 1, :].broadcast_to([DH, NP, T])
                        sp.dma_start(stk[block, buf, 0, h, :], parts[rows, m, 0, :, :]).then_inc(stk_loaded[buf][h], 16)
                        sp.dma_start(stk[block, buf, 1, h, :], k).then_inc(stk_loaded[buf][h], 16)
                    sp.dma_start(stk[ROWS_A:ROWS_S, buf, :, h, :], ends).then_inc(stk_loaded[buf][h], 16)

            def load_max(l, g):
                sp.wait_ge(s_drained, sidx["mt", l, g] + 1)
                sp.dma_start(stk[ROWS_S:ROWS, g % NBUF, 0, :, :].rearrange("r h t -> r (h t)"),
                             mT[0:NP * HG * TT, :]).then_inc(m_loaded[g % NBUF], 16)

            with sp.Fori(0, B) as b:
                for l in range(2):
                    load_stack(l, 0)
                    load_stack(l, 1)
                    load_max(l, 0)
                    load_stack(l, 2)
                    load_max(l, 1)
                    load_stack(l, 3)
                    load_max(l, 2)
                    load_max(l, 3)
                    if l == 0:
                        for tp in range(TT // 2):
                            bk, n = place["ao", 0, tp]
                            sp.wait_ge(drained[bk], n + 1)
                        sp.dma_start(x_in[:], x_d[(b + 1) % B].rearrange("(t p) d -> p t d", p=P)).then_inc(x_loaded, 16)
                sp.wait_ge(x_done, 1)
                sp.dma_start(out_d[b].rearrange("(t p) d -> p t d", p=P), x[:]).then_inc(stored, 16)
                sp.wait_ge(part_done, 4)
                sp.sem_clear(pass_sems)
                sp.sem_inc(next_pass, 1)
            sp.wait_ge(stored, 16 * (B + 1))
            sp.wait_ge(x_loaded, 16 * (B + 1))

        @block.tensor
        def _(pe):
            def claim(*key):
                b, n = place[key]
                if n:
                    pe.wait_ge(drained[b], n)
                return bank[b], full[b]

            def in_sbuf(*key):
                b, n = place[key]
                pe.wait_ge(drained[b], n + 1)

            pe.wait_ge(w_const, 2)
            unit = 0

            def setup_bank():
                nonlocal unit
                if unit >= 4:
                    pe.wait_ge(w_drained, unit - 3)
                unit += 1
                return bank[(unit - 1) % 4]

            for u in range(2):
                pt = setup_bank()
                for i in range(4):
                    ins = pe.transpose(pt[:, P * i:P * (i + 1)], wo1_s[:, 4 * u + i, :], ident[:])
                ins.then_inc(w_full, 1)
            pt = setup_bank()
            for i in range(KD):
                ins = pe.transpose(pt[:, P * i:P * (i + 1)], wo2_s[:, i, :], ident[:])
            ins.then_inc(w_full, 1)
            for w in range(3):
                for u in range(4):
                    pt = setup_bank()
                    for i in range(4):
                        blk = 2 * u + i // KD
                        ins = pe.transpose(pt[:, P * i:P * (i + 1)], down[:, w, i % KD, P * blk:P * (blk + 1)], ident[:])
                    ins.then_inc(w_full, 1)
            for w in range(3):
                pe.wait_ge(w_drained, 3 + 4 * (w + 1))
                for odd in range(2):
                    pt = setup_bank()
                    rows = slice(L * odd, L * (odd + 1))
                    for kd in range(KD):
                        for i in range(H // 2):
                            col = DH * (H // 2 * kd + i)
                            ins = pe.matmul(pt[:, col:col + DH], dT[rows, w, i, P * kd:P * (kd + 1)], up[rows, w, :],
                                            start=True, stop=True)
                    ins.then_inc(w_full, 1)
            pe.drain().then_inc(part_done, 1)

            def transposed_x(s):
                for c in range(NC):
                    pe.wait_ge(xn_ready, NC * s + c + 1)
                    for kd in range(KD):
                        pt, done = claim("xt", s, c, kd)
                        for i in range(TPC):
                            ins = pe.transpose(pt[:, P * i:P * (i + 1)], xn[:, TPC * c + i, P * kd:P * (kd + 1)], ident[:])
                        ins.then_inc(done, 1)

            def need_xT(s, c):
                for kd in range(KD):
                    in_sbuf("xt", s, c, kd)

            def project_qk(l, m, c, w):
                pt, done = claim("qk", l, m, c, w)
                for kd in range(KD):
                    ins = pe.matmul(pt, wqkv[l][:, kd, D * w + P * m:D * w + P * (m + 1)],
                                    xnT[:, kd, BANK * c:BANK * (c + 1)], start=kd == 0, stop=kd == KD - 1)
                ins.then_inc(done, 1)

            def by_token(pt, left, right, tiles, n_k):
                for i, t in enumerate(tiles):
                    for kd in range(n_k):
                        ins = pe.matmul(pt[:, D * i:D * (i + 1)], left(kd, t), right(kd), start=kd == 0, stop=kd == n_k - 1)
                return ins

            def score_unit(l, g, i, h, p, width):
                n, buf = sidx["s", l, g, i, h, p], g % NBUF
                if n >= 2:
                    pe.wait_ge(s_drained, n - 1)
                out = s_bank[n % 2][:, 0:width]
                lhsT = stk[0:ROWS_S, buf, 0, h, P * i:P * (i + 1)]
                diagonal = BANK * p + width == P * (i + 1)
                ins = pe.matmul(out, lhsT, stk[0:ROWS_S, buf, 1, h, BANK * p:BANK * p + width], start=True, stop=not diagonal)
                if diagonal:
                    ins = pe.matmul(out[:, width - P:width], ident_b[:], mask_b[:], start=False, stop=True)
                ins.then_inc(s_full, 1)

            def stack_ready(l, g, h):
                uses = 1 + (g >= NBUF) + l * (1 + (g % NBUF + NBUF < NG))
                pe.wait_ge(stk_loaded[g % NBUF][h], STACK_DMAS * 16 * uses)

            def max_rows(l, g):
                n = sidx["mt", l, g]
                pe.wait_ge(s_drained, n - 1)
                pe.wait_ge(mx_ready, NG * l + g + 1)
                rows = NP * HG * TT
                pe.transpose(s_bank[n % 2][0:rows, 0:P // 2].bitcast(BF16),
                             mparts[:].rearrange("q p m -> q (p m)"), ident_b[:]).then_inc(s_full, 1)

            def normalise(l, g):
                for c in range(NC):
                    n = sidx["nm", l, g, c]
                    pe.wait_ge(s_drained, n - 1)
                    pe.wait_ge(o_drained, NC * (NG * l + g) + c + 1)
                    for i in range(TPC):
                        t = TPC * c + i
                        ins = pe.transpose(s_bank[n % 2][:, P * i:P * (i + 1)], oT[:, P * t:P * (t + 1)], ident[:])
                    ins.then_inc(s_full, 1)

            def scores_t(l, g, j, h):
                n, buf = HG * (TT * (NG * l + g) + j) + h, g % NBUF
                if n >= 2:
                    pe.wait_ge(exp_done, n - 1)
                for c in range(NC):
                    a, z = query_range(j, c)
                    if a < z:
                        ins = pe.matmul(st_pair[n % 2][:, a:z], stk[0:ROWS, buf, 1, h, P * j:P * (j + 1)],
                                        stk[0:ROWS, buf, 0, h, a:z], start=True, stop=True)
                ins.then_inc(st_full, 1)

            def weigh_values(l, g, j, c):
                step = TT * (NG * l + g) + j
                a, z = query_range(j, c)
                if a < z:
                    pe.wait_ge(p_ready, HG * (step + 1))
                    if j == 0 and NG * l + g > 0:
                        pe.wait_ge(o_drained, NC * (NG * l + g - 1) + c + 1)
                    for h in range(HG):
                        ins = pe.matmul(o_bank[c][32 * h:32 * h + DH + 1, a - BANK * c:z - BANK * c],
                                        vaug[:, j, HG * g + h, :], probs[:, step % 2, h, a:z],
                                        start=j == 0, stop=j == TPC * (c + 1) - 1)
                if c == NC - 1:
                    ins.then_inc(pv_done, 1)

            def attention(l):
                s = 2 * l
                transposed_x(s)
                for c in range(NC):
                    need_xT(s, c)
                    for w in range(2):
                        project_qk(l, 0, c, w)
                for tp in range(TT // 2):
                    pt, done = claim("v", l, tp)
                    by_token(pt, lambda kd, t: xnT[:, kd, P * t:P * (t + 1)], lambda kd: wqkv[l][:, kd, 2 * D:3 * D],
                             (2 * tp, 2 * tp + 1), KD).then_inc(done, 1)
                if l:
                    for c in range(NC):
                        in_sbuf("h1", c)
                        in_sbuf("z2", c)
                for i in reversed(range(TT)):
                    for h in range(HG):
                        if i == TT - 1:
                            stack_ready(l, 0, h)
                        for p, width in score_parts(i):
                            score_unit(l, 0, i, h, p, width)
                    if i % 2 == 0:
                        project_qk(l, 1, (TT - 2 - i) // 2 // 2, (TT - 2 - i) // 2 % 2)
                max_rows(l, 0)
                for b in range(4):
                    if ring_before_main[l][b]:
                        pe.wait_ge(drained[b], ring_before_main[l][b])
                before = None
                for g in range(NG):
                    pe.wait_ge(m_loaded[g % NBUF], 16 * (1 + (g >= NBUF) + l * (1 + (g % NBUF + NBUF < NG))))
                    for j in range(TT):
                        for h in range(HG):
                            if g + 1 < NG:
                                if j == 0:
                                    stack_ready(l, g + 1, h)
                                for i in MAX_AT_STEP[j]:
                                    for p, width in score_parts(i):
                                        score_unit(l, g + 1, i, h, p, width)
                            scores_t(l, g, j, h)
                            if before and h % 2:
                                weigh_values(l, *before, h // 2)
                        before = (g, j)
                        if g + 1 < NG and j == MT_STEP:
                            max_rows(l, g + 1)
                        if g > 0 and j == NORM_STEP:
                            normalise(l, g - 1)
                for c in range(NC):
                    weigh_values(l, *before, c)
                normalise(l, NG - 1)
                pe.wait_ge(exp_done, HG * TT * NG * (l + 1))
                pe.wait_ge(s_drained, sidx["nm", l, NG - 1, NC - 1] + 1)
                for c in range(NC):
                    for kd in range(KD):
                        pt, done = claim("yt", l, c, kd)
                        for i in range(TPC):
                            ins = pe.transpose(pt[:, P * i:P * (i + 1)], y[:, TPC * c + i, P * kd:P * (kd + 1)], ident[:])
                        ins.then_inc(done, 1)
                for tp in range(TT // 2):
                    for kd in range(KD):
                        in_sbuf("yt", l, 2 * tp // TPC, kd)
                    pt, done = claim("ao", l, tp)
                    by_token(pt, lambda kd, t: yT[:, kd, P * t:P * (t + 1)], lambda kd: wo[l][:, kd, :],
                             (2 * tp, 2 * tp + 1), KD).then_inc(done, 1)

            def first_ffn():
                transposed_x(1)
                pt, done = claim("logit")
                for t in range(TT):
                    need_xT(1, t // TPC)
                    for kd in range(KD):
                        ins = pe.matmul(pt[:, E0 * t:E0 * (t + 1)], xnT[:, kd, P * t:P * (t + 1)], projw[:, kd, :],
                                        start=kd == 0, stop=kd == KD - 1)
                ins.then_inc(done, 1)
                for c in range(NC):
                    pt, done = claim("h1", c)
                    for kd in range(KD):
                        ins = pe.matmul(pt, win1[:, kd, :], xnT[:, kd, BANK * c:BANK * (c + 1)], start=kd == 0, stop=kd == KD - 1)
                    ins.then_inc(done, 1)
                pe.wait_ge(a_ready, 1)
                for c in range(NC):
                    pt, done = claim("at", c)
                    for i in range(TPC):
                        ins = pe.transpose(pt[0:E0, P * i:P * (i + 1)], zu[:, TPC * c + i, :], ident[:])
                    ins.then_inc(done, 1)
                for c in range(NC):
                    in_sbuf("at", c)
                    for n, name in enumerate(("g1", "g2")):
                        pt, done = claim(name, c)
                        pe.matmul(pt, c12[:, n, :], aT[:, BANK * c:BANK * (c + 1)], start=True, stop=True).then_inc(done, 1)

                def hidden(c, o):
                    pt, done = claim("hid", c, o)
                    pe.matmul(pt, wout1T[:, P * o:P * (o + 1)], z1[c], start=True, stop=True).then_inc(done, 1)

                for c in range(NC):
                    in_sbuf("h1", c)
                    acc, done = claim("z2", c)
                    lag = 3
                    for o in range(OC + lag):
                        if o < OC:
                            hidden(c, o)
                        if o >= lag:
                            in_sbuf("hid", c, o - lag)
                            ins = pe.matmul(acc, win2[:, o - lag, :], hsb[(o - lag) % 4], start=o == lag, stop=o == OC + lag - 1)
                            if o < OC + lag - 1:
                                ins.then_inc(h_used, 1)
                    ins.then_inc(done, 1)
                    in_sbuf("z2", c)
                    for tp in range(TPC // 2):
                        pt, done = claim("fo", c, tp)
                        by_token(pt, lambda kd, t: z2[c][:, P * t:P * (t + 1)], lambda kd: wout2T[:],
                                 (2 * tp, 2 * tp + 1), 1).then_inc(done, 1)

            def second_ffn():
                transposed_x(3)
                pt, done = claim("route")
                for t in range(TT):
                    need_xT(3, t // TPC)
                    for kd in range(KD):
                        ins = pe.matmul(pt[:, NE * t:NE * (t + 1)], xnT[:, kd, P * t:P * (t + 1)], wr[:, kd, :],
                                        start=kd == 0, stop=kd == KD - 1)
                ins.then_inc(done, 1)

                units = [(e, c) for e in [NE, *range(NE)] for c in range(NC)]

                def up_unit(e, c):
                    pt, done = claim("he", e, c)
                    for kd in range(KD):
                        ins = pe.matmul(pt, w1[:, e, kd, :], xnT[:, kd, BANK * c:BANK * (c + 1)], start=kd == 0, stop=kd == KD - 1)
                    ins.then_inc(done, 1)

                def down_unit(u, e, c):
                    in_sbuf("he", e, c)
                    for tp in range(TPC // 2):
                        pt, done = claim("eo", e, c, tp)
                        by_token(pt, lambda kd, t: hq[u % 4][:, P * t:P * (t + 1)], lambda kd: w2[:, e, :],
                                 (2 * tp, 2 * tp + 1), 1).then_inc(done, 1)

                for u, (e, c) in enumerate(units):
                    up_unit(e, c)
                    down_unit(u, e, c)

            with pe.Fori(0, B) as b:
                begin_pass(pe, b)
                attention(0)
                first_ffn()
                attention(1)
                second_ffn()
                pe.drain().then_inc(part_done, 1)

        @block.scalar
        def _(act):
            unit = 0

            def setup_copy(dst, n=BANK):
                nonlocal unit
                act.wait_ge(w_full, unit + 1)
                src = bank[unit % 4][:, 0:n]
                if len(dst.shape) == 3:
                    src = src.rearrange("p (a n) -> p a n", a=dst.shape[1])
                act.activation(dst, src, ACT.Copy).then_inc(w_drained, 1)
                unit += 1

            for u in range(2):
                setup_copy(wout1T[:, BANK * u:BANK * (u + 1)])
            setup_copy(wout2T[:], D)
            for w in range(3):
                for u in range(4):
                    setup_copy(dT[:, w, 2 * u:2 * u + 2, :])
            for w in range(3):
                for odd in range(2):
                    act.wait_ge(w_full, unit + 1)
                    src = bank[unit % 4][:, 0:KD * D // 2].rearrange("p (k i d) -> p k i d", k=KD, d=DH)
                    dst = wqkv[1][:, :, D * w:D * (w + 1)].rearrange("p k (i o d) -> p k i o d", o=2, d=DH)[:, :, :, odd, :]
                    act.activation(dst, src, ACT.Copy).then_inc(w_drained, 1)
                    unit += 1
            act.drain().then_inc(part_done, 1)

            def copy_xT(name, s, c, kd):
                pt = arrived(act, name, s, c, kd)
                act.activation(xnT[:, kd, BANK * c:BANK * (c + 1)], pt, ACT.Copy).then_inc(read_out(name, s, c, kd), 1)

            def part0(l, u, m, c, w):
                dst = parts[:, m, w, 0, BANK * c:BANK * (c + 1)]
                if l == 0:
                    pt = arrived(act, "qk", l, m, c, w)
                    act.activation(dst, pt, ACT.Copy).then_inc(part0_ready, 1)
                else:
                    act.wait_ge(rope_ready, u + 1)
                    act.activation(dst, qs[u % 2], ACT.Copy).then_inc(part0_ready, 1)

            def copy_q(u, m, c, w):
                pt = arrived(act, "qk", 1, m, c, w)
                if u >= 2:
                    act.wait_ge(parts_ready, 8 + u - 1)
                act.activation(qf[u % 2], pt, ACT.Copy).then_inc(read_out("qk", 1, m, c, w), 1)

            def part1(l, u, m, c, w):
                act.wait_ge(rest_ready, 8 * l + u + 1)
                act.activation(parts[:, m, w, 1, BANK * c:BANK * (c + 1)], qr[u % 2], ACT.Copy).then_inc(part1_ready, 1)

            def split(l, m):
                units = [(4 * m + 2 * c + w, m, c, w) for c in range(NC) for w in range(2)]
                if l == 0 and m == 0:
                    for i, u in enumerate(units):
                        part0(l, *u)
                        if i:
                            part1(l, *units[i - 1])
                    part1(l, *units[-1])
                else:
                    for u in units:
                        if l:
                            copy_q(*u)
                        part0(l, *u)
                        part1(l, *u)

            def attention(l):
                for c in range(NC):
                    for kd in range(KD):
                        copy_xT("xt", 2 * l, c, kd)
                split(l, 0)
                for tp in range(TT // 2):
                    pt = arrived(act, "v", l, tp)
                    act.activation(vaug[:, 2 * tp:2 * tp + 2, :, 0:DH], pt.rearrange("p (t h d) -> p t h d", t=2, h=H),
                                   ACT.Copy).then_inc(read_out("v", l, tp), 1)
                split(l, 1)

                def copy_o(g):
                    act.wait_ge(pv_done, TT * (NG * l + g + 1))
                    if NG * l + g > 0:
                        key = ("nm", l, g - 1, NC - 1) if g else ("nm", l - 1, NG - 1, NC - 1)
                        act.wait_ge(s_drained, sidx[key] + 1)
                    for c in range(NC):
                        act.activation(oT[:, BANK * c:BANK * (c + 1)], o_bank[c], ACT.Copy).then_inc(o_drained, 1)

                for g in range(NG):
                    for j in range(TT):
                        step = TT * (NG * l + g) + j
                        for h in range(HG):
                            n = HG * step + h
                            act.wait_ge(st_full, n + 1)
                            if step >= 2:
                                act.wait_ge(pv_done, step - 1)
                            act.activation(probs[:, step % 2, h, P * j:T], st_pair[n % 2][:, P * j:T], ACT.Exp,
                                           scale=SCALE).then_inc(exp_done, 1)
                        if g > 0 and j == 0:
                            copy_o(g - 1)
                copy_o(NG - 1)
                for c in range(NC):
                    for kd in range(KD):
                        copy_xT("yt", l, c, kd)

            def first_ffn():
                for c in range(NC):
                    for kd in range(KD):
                        copy_xT("xt", 1, c, kd)
                act.wait_ge(delta_ready, 1)
                act.activation(zt[:], zt[:], ACT.Sqrt).then_inc(sqrt_ready, 1)
                for c in range(NC):
                    pt = arrived(act, "at", c)
                    act.activation(aT[:, BANK * c:BANK * (c + 1)], pt[0:E0, :], ACT.Copy).then_inc(read_out("at", c), 1)
                for c in range(NC):
                    for n, name in enumerate(("g1", "g2")):
                        pt = arrived(act, name, c)
                        act.activation(gsb[2 * c + n], pt, ACT.Copy).then_inc(read_out(name, c), 1)
                for c in range(NC):
                    for o in range(OC):
                        pt = arrived(act, "hid", c, o)
                        n = OC * c + o
                        if o >= 4:
                            act.wait_ge(h_used, (OC - 1) * c + o - 3)
                        elif c:
                            bk, k = place["z2", c - 1]
                            act.wait_ge(full[bk], k + 1)
                        act.activation(hsb[n % 4], pt, ACT.Gelu).then_inc(read_out("hid", c, o), 1)

            def second_ffn():
                for c in range(NC):
                    for kd in range(KD):
                        copy_xT("xt", 3, c, kd)
                units = [(e, c) for e in [NE, *range(NE)] for c in range(NC)]

                def relu(u):
                    pt = arrived(act, "he", *units[u])
                    if u >= 4:
                        act.wait_ge(hq_ready, u - 3)
                    act.activation(hr[u % 4], pt, ACT.Relu).then_inc(relu_ready, 1)

                act.wait_ge(gap_ready, 1)
                act.activation(zsm[:, 1, :], zsm[:, 0, :], ACT.Exp).then_inc(egap_ready, 1)
                for u in range(len(units)):
                    relu(u)

            with act.Fori(0, B) as b:
                begin_pass(act, b)
                attention(0)
                first_ffn()
                attention(1)
                second_ffn()
                act.drain().then_inc(part_done, 1)

        @block.gpsimd
        def _(pool):
            n = 0

            def done(ins):
                nonlocal n
                n += 1
                ins.then_inc(act_chain, 1)
                pool.wait_ge(act_chain, n)

            done(pool.memset(ident[:], 0.0))
            done(pool.memset(ident_b[:], 0.0))
            done(pool.memset(mask_b[:], 0.0))
            done(pool.memset(neg_half[:], -0.5))
            for t in (ident, ident_b):
                done(pool.affine_select(out=t[:], in_=t[:], compare_op=ALU.not_equal, fill=1.0, base=0,
                                        pattern=[[-1, P]], channel_multiplier=1))
            pool.affine_select(out=mask_b[:], in_=mask_b[:], compare_op=ALU.is_ge, fill=NEG, base=0,
                               pattern=[[-1, P]], channel_multiplier=1).then_inc(w_const, 1)
            pool.drain().then_inc(part_done, 1)

            def inverse_root(s):
                for c in range(NC):
                    pool.wait_ge(ln_var, NC * s + c + 1)
                    tiles = slice(TPC * c, TPC * (c + 1))
                    pool.tensor_tensor(rstd[:, tiles], veps[:, tiles], neg_half[:, tiles], ALU.pow).then_inc(ln_rstd, 1)

            def attention(l):
                inverse_root(2 * l)
                if l:
                    for m in range(2):
                        for c in range(NC):
                            for w in range(2):
                                u = 4 * m + 2 * c + w
                                bk, k = place["qk", 1, m, c, w]
                                pool.wait_ge(drained[bk], k + 1)
                                pool.tensor_tensor(qc[u % 2], qf[u % 2], cos[:, BANK * c:BANK * (c + 1)], ALU.mult)\
                                    .then_inc(qcos_ready, 1)
                for step in range(TT * NG * l, TT * NG * (l + 1)):
                    j = step % TT
                    for h in range(HG):
                        pool.wait_ge(exp_done, HG * step + h + 1)
                        diag = probs[:, step % 2, h, P * j:P * (j + 1)]
                        pool.affine_select(out=diag, in_=diag, compare_op=ALU.is_ge, fill=0.0, base=0,
                                           pattern=[[1, P]], channel_multiplier=-1).then_inc(p_ready, 1)

            with pool.Fori(0, B) as b:
                begin_pass(pool, b)
                attention(0)
                inverse_root(1)
                pool.wait_ge(ent_var, 1)
                pool.tensor_tensor(zsm[:, 2, :], zsm[:, 1, :], neg_half[:], ALU.pow).then_inc(ent_rstd, 1)
                attention(1)
                inverse_root(3)
                pool.drain().then_inc(part_done, 1)

        @block.vector
        def _(dve):
            links = 0

            def link(ins):
                nonlocal links
                links += 1
                ins.then_inc(dve_chain, 1)
                dve.wait_ge(dve_chain, links)

            dve.memset(vaug[:], 1.0)
            dve.memset(mx[:], LOWEST)
            dve.wait_ge(w_drained, 21)
            for buf in range(NBUF):
                dve.memset(stk[ROWS_A:P, buf, 1, :, :], 1.0)
            for c in range(NC):
                dve.memset(o_bank[c], 0.0)
            dve.drain().then_inc(part_done, 1)

            def layer_norm(s, src):
                for c in range(NC):
                    tiles = range(TPC * c, TPC * (c + 1))
                    for t in tiles:
                        ins = dve.bn_stats(st6[:, t, :], src[:, t, :])
                    link(ins)
                    for t in tiles:
                        ins = dve.bn_aggr(mv[:, t, :], st6[:, t, :])
                    link(ins)
                    cs = slice(TPC * c, TPC * (c + 1))
                    dve.tensor_scalar(veps[:, cs], mv[:, cs, 1], LN_EPS, None, ALU.add).then_inc(ln_var, 1)
                for c in range(NC):
                    dve.wait_ge(ln_rstd, NC * s + c + 1)
                    for t in range(TPC * c, TPC * (c + 1)):
                        ins = dve.tensor_scalar(xn[:, t, :], src[:, t, :], mv[:, t, 0:1], rstd[:, t:t + 1],
                                                ALU.subtract, ALU.mult)
                    ins.then_inc(xn_ready, 1)

            def rest(l, m, c, w):
                u = 4 * m + 2 * c + w
                part = parts[:, m, w, 0, BANK * c:BANK * (c + 1)]
                if l == 0:
                    dve.wait_ge(part0_ready, u + 1)
                    pt = arrived(dve, "qk", l, m, c, w)
                    if u >= 2:
                        dve.wait_ge(parts_ready, u - 1)
                    dve.tensor_tensor(qr[u % 2], pt, part, ALU.subtract).then_inc(rest_ready, 1)
                    bk, k = place["qk", l, m, c, w]
                    dve.wait_ge(rest_ready, u + 1)
                    dve.sem_inc(drained[bk], 1)
                else:
                    bk, k = place["qk", l, m, c, w]
                    dve.wait_ge(drained[bk], k + 1)
                    swap = [i ^ 1 for i in range(32)]
                    link(dve.stream_shuffle(qs[u % 2], qf[u % 2], swap))
                    link(dve.tensor_tensor(qs[u % 2], qs[u % 2], sin[:, BANK * c:BANK * (c + 1)], ALU.mult))
                    dve.wait_ge(qcos_ready, u + 1)
                    dve.tensor_tensor(qs[u % 2], qs[u % 2], qc[u % 2], ALU.add).then_inc(rope_ready, 1)
                    dve.wait_ge(part0_ready, 8 + u + 1)
                    dve.tensor_tensor(qr[u % 2], qs[u % 2], part, ALU.subtract).then_inc(rest_ready, 1)

            def part2(l, m, c, w):
                u = 4 * m + 2 * c + w
                dve.wait_ge(part1_ready, 8 * l + u + 1)
                cols = slice(BANK * c, BANK * (c + 1))
                dve.tensor_tensor(parts[:, m, w, 2, cols], qr[u % 2], parts[:, m, w, 1, cols], ALU.subtract).then_inc(parts_ready, 1)

            def maximum(l, g, i, h, p, width):
                n = sidx["s", l, g, i, h, p]
                dve.wait_ge(s_full, n + 1)
                dve.tensor_reduce(mx[:, h, i, p:p + 1], s_bank[n % 2][:, 0:width], AX.X, ALU.max).then_inc(s_drained, 1)

            def split_max(l, g):
                n = sidx["mt", l, g]
                dve.wait_ge(s_drained, n)
                link(dve.tensor_reduce(negm[:], mx[:].rearrange("q h i p -> q (h i) p"), AX.X, ALU.max, negate=True))
                link(dve.tensor_copy(mparts[:, 0, :], negm[:]))
                link(dve.tensor_tensor(negr[:], negm[:], mparts[:, 0, :], ALU.subtract))
                link(dve.tensor_copy(mparts[:, 1, :], negr[:]))
                dve.tensor_tensor(mparts[:, 2, :], negr[:], mparts[:, 1, :], ALU.subtract).then_inc(mx_ready, 1)
                dve.wait_ge(s_full, n + 1)
                if NG * l + g:
                    loads = NG * l + g
                    before = (loads - 1) % NG
                    dve.wait_ge(m_loaded[before % NBUF], 16 * (1 + (before >= NBUF) + (loads > NG) * (1 + (before % NBUF + NBUF < NG))))
                rows = NP * HG * TT
                dve.tensor_copy(mT[0:rows, :], s_bank[n % 2][0:rows, 0:P // 2].bitcast(BF16)).then_inc(s_drained, 1)

            def normalise(l, g):
                for c in range(NC):
                    n = sidx["nm", l, g, c]
                    dve.wait_ge(s_full, n + 1)
                    dve.wait_ge(s_drained, n)
                    src = s_bank[n % 2].rearrange("q (t h v) -> q t h v", t=TPC, h=HG)
                    link(dve.reciprocal(rec[:], src[:, :, :, DH]))
                    dst = y[:, TPC * c:TPC * (c + 1), HG * DH * g:HG * DH * (g + 1)].rearrange("q t (h d) -> q t h d", h=HG)
                    w = rec[:].rearrange("q t (h a) -> q t h a", a=1).broadcast_to([P, TPC, HG, DH])
                    dve.tensor_tensor(dst, src[:, :, :, 0:DH], w, ALU.mult).then_inc(s_drained, 1)

            def add_to_x(tiles, pt, base, key):
                dve.tensor_tensor(x[:, tiles, :], pt.rearrange("p (t d) -> p t d", t=2), base[:, tiles, :], ALU.add)\
                    .then_inc(read_out(*key), 1)

            def settled(*keys):
                for key in keys:
                    bk, k = place[key]
                    dve.wait_ge(drained[bk], k + 1)

            def attention(l, src, pass_index):
                layer_norm(2 * l, src)
                units = [(c, w) for c in range(NC) for w in range(2)]
                for i, u in enumerate(units):
                    rest(l, 0, *u)
                    if i:
                        part2(l, 0, *units[i - 1])
                part2(l, 0, *units[-1])
                pending = None
                for i in reversed(range(TT)):
                    for h in range(HG):
                        for p, width in score_parts(i):
                            maximum(l, 0, i, h, p, width)
                    if pending:
                        part2(l, 1, *pending)
                        pending = None
                    if i % 2 == 0:
                        pending = units[(TT - 2 - i) // 2]
                        rest(l, 1, *pending)
                part2(l, 1, *pending)
                split_max(l, 0)
                for g in range(NG):
                    for j in range(TT):
                        if g + 1 < NG:
                            for h in range(HG):
                                for i in MAX_AT_STEP[j]:
                                    for p, width in score_parts(i):
                                        maximum(l, g + 1, i, h, p, width)
                            if j == MT_STEP:
                                split_max(l, g + 1)
                        if g > 0 and j == NORM_STEP:
                            normalise(l, g - 1)
                normalise(l, NG - 1)
                if l == 0:
                    dve.wait_ge(stored, 16 * pass_index + 16)
                for tp in range(TT // 2):
                    pt = arrived(dve, "ao", l, tp)
                    add_to_x(slice(2 * tp, 2 * tp + 2), pt, src, ("ao", l, tp))
                settled(*[("ao", l, tp) for tp in range(TT // 2)])

            def entmax():
                def wide(v):
                    return v.rearrange("p (t a) -> p t a", a=1).broadcast_to([P, TT, E0])

                def every(v):
                    return v.rearrange("p (a k) -> p a k", a=1).broadcast_to([P, TT, E0])

                pt = arrived(dve, "logit")[:, 0:TT * E0].rearrange("p (t e) -> p t e", t=TT)
                link(dve.tensor_reduce(zsm[:, 0, :], pt, AX.X, ALU.add))
                link(dve.tensor_scalar(zsm[:, 0, :], zsm[:, 0, :], 1.0 / E0, None, ALU.mult))
                dve.tensor_tensor(zc[:], pt, wide(zsm[:, 0, :]), ALU.subtract).then_inc(read_out("logit"), 1)
                settled(("logit",))
                link(dve.tensor_tensor(zt[:], zc[:], zc[:], ALU.mult))
                link(dve.tensor_reduce(zsm[:, 1, :], zt[:], AX.X, ALU.add))
                ins = dve.tensor_scalar(zsm[:, 1, :], zsm[:, 1, :], 1.0 / E0, LN_EPS, ALU.mult, ALU.add)
                ins.then_inc(ent_var, 1)
                dve.wait_ge(ent_rstd, 1)
                link(dve.scalar_tensor_tensor(zc[:], zc[:], 0.5, wide(zsm[:, 2, :]), ALU.mult, ALU.mult))
                link(dve.tensor_reduce(zsm[:, 0, :], zc[:], AX.X, ALU.max))
                link(dve.tensor_tensor(zc[:], zc[:], wide(zsm[:, 0, :]), ALU.subtract))
                zs = cum[:, 0, 0:TT, :]
                for t in range(TT):
                    ins = dve.max(zs[:, t, 0:8], zc[:, t, :])
                link(ins)
                for t in range(TT):
                    ins = dve.match_replace(zt[:, t, :], zs[:, t, 0:8], zc[:, t, :], LOWEST)
                link(ins)
                for t in range(TT):
                    ins = dve.max(zs[:, t, 8:16], zt[:, t, :])
                link(ins)
                link(dve.tensor_tensor(cum[:, 0, TT:2 * TT, :], zs, zs, ALU.mult))
                a, nxt = cum[:, 0], (cum[:, 1], cum[:, 2])
                for r, s in enumerate((1, 2, 4, 8)):
                    z = nxt[r % 2]
                    dve.tensor_copy(z[:, :, 0:s], a[:, :, 0:s])
                    link(dve.tensor_tensor(z[:, :, s:E0], a[:, :, s:E0], a[:, :, 0:E0 - s], ALU.add))
                    a = z
                inv = kidx[:, 1, :].rearrange("p (a k) -> p a k", a=1).broadcast_to([P, 2 * TT, E0])
                m = cum[:, 1]
                link(dve.tensor_tensor(m, a, inv, ALU.mult))
                link(dve.tensor_tensor(zt[:], m[:, 0:TT, :], m[:, 0:TT, :], ALU.mult))
                link(dve.tensor_tensor(zt[:], zt[:], m[:, TT:2 * TT, :], ALU.subtract))
                link(dve.tensor_tensor(zt[:], zt[:], every(kidx[:, 1, :]), ALU.add))
                dve.tensor_scalar(zt[:], zt[:], 1e-34, None, ALU.max).then_inc(delta_ready, 1)
                dve.wait_ge(sqrt_ready, 1)
                tau = cum[:, 2, 0:TT, :]
                link(dve.tensor_tensor(tau, m[:, 0:TT, :], zt[:], ALU.subtract))
                link(dve.tensor_tensor(zu[:], tau, zs, ALU.is_le))
                link(dve.tensor_reduce(zsm[:, 3, :], zu[:], AX.X, ALU.add))
                link(dve.tensor_tensor(zu[:], every(kidx[:, 0, :]), wide(zsm[:, 3, :]), ALU.is_equal))
                link(dve.tensor_tensor(zu[:], zu[:], tau, ALU.mult))
                link(dve.tensor_reduce(zsm[:, 3, :], zu[:], AX.X, ALU.add))
                link(dve.tensor_tensor(zc[:], zc[:], wide(zsm[:, 3, :]), ALU.subtract))
                link(dve.tensor_scalar(zc[:], zc[:], 0.0, None, ALU.max))
                dve.tensor_tensor(zu[:], zc[:], zc[:], ALU.mult).then_inc(a_ready, 1)

            def gated(pt, bias, key, c, n, dst, src_key):
                settled((key, c))
                dve.scalar_tensor_tensor(dst, pt, bias[:, 0:1], gsb[2 * c + n], ALU.add, ALU.mult).then_inc(read_out(*src_key), 1)

            def first_ffn():
                layer_norm(1, x)
                entmax()
                for c in range(NC):
                    pt = arrived(dve, "h1", c)
                    gated(pt, bias1, "g1", c, 0, z1[c], ("h1", c))
                for c in range(NC):
                    pt = arrived(dve, "z2", c)
                    gated(pt, bias2, "g2", c, 1, z2[c], ("z2", c))
                    for tp in range(TPC // 2):
                        pt = arrived(dve, "fo", c, tp)
                        add_to_x(slice(TPC * c + 2 * tp, TPC * c + 2 * tp + 2), pt, x, ("fo", c, tp))
                settled(*[("fo", c, tp) for c in range(NC) for tp in range(TPC // 2)])

            def second_ffn():
                layer_norm(3, x)
                pt = arrived(dve, "route")[:, 0:TT * NE].rearrange("p (t e) -> p t e", t=TT)
                dve.tensor_copy(zc[:, :, 0:NE], pt).then_inc(read_out("route"), 1)
                settled(("route",))
                for t in range(TT):
                    ins = dve.max(zt[:, t, 0:8], zc[:, t, 0:NE])
                link(ins)
                dve.tensor_tensor(zsm[:, 0, :], zt[:, :, 1], zt[:, :, 0], ALU.subtract).then_inc(gap_ready, 1)
                dve.wait_ge(egap_ready, 1)
                link(dve.tensor_scalar(zsm[:, 1, :], zsm[:, 1, :], 1.0, None, ALU.add))
                link(dve.reciprocal(zsm[:, 2, :], zsm[:, 1, :]))
                link(dve.tensor_scalar(zsm[:, 2, :], zsm[:, 2, :], 1.0, None, ALU.is_ge))
                link(dve.tensor_tensor(gate[:], zc[:, :, 0:NE], zt[:, :, 0:1].broadcast_to([P, TT, NE]), ALU.is_ge))
                link(dve.tensor_tensor(gate[:], gate[:], zsm[:, 2, :].rearrange("p (t a) -> p t a", a=1)
                                       .broadcast_to([P, TT, NE]), ALU.mult))
                units = [(e, c) for e in [NE, *range(NE)] for c in range(NC)]

                def square(u):
                    e, c = units[u]
                    dve.wait_ge(relu_ready, u + 1)
                    pt = arrived(dve, "he", e, c)
                    dve.scalar_tensor_tensor(hq[u % 4], pt, 0.0, hr[u % 4], ALU.max, ALU.mult).then_inc(hq_ready, 1)
                    dve.wait_ge(hq_ready, u + 1)
                    dve.sem_inc(read_out("he", e, c), 1)

                for u, (e, c) in enumerate(units):
                    square(u)
                    for tp in range(TPC // 2):
                        key = ("eo", e, c, tp)
                        pt = arrived(dve, *key)
                        t = TPC * c + 2 * tp
                        if u >= NC:
                            settled(("eo", units[u - NC][0], c, tp))
                        if e == NE:
                            add_to_x(slice(t, t + 2), pt, x, key)
                        else:
                            dve.scalar_tensor_tensor(x[:, t, :], pt[:, 0:D], gate[:, t, e:e + 1], x[:, t, :], ALU.mult, ALU.add)
                            dve.scalar_tensor_tensor(x[:, t + 1, :], pt[:, D:2 * D], gate[:, t + 1, e:e + 1], x[:, t + 1, :],
                                                     ALU.mult, ALU.add).then_inc(read_out(*key), 1)
                dve.drain().then_inc(x_done, 1)

            with dve.Fori(0, B) as b:
                links = 0
                begin_pass(dve, b)
                dve.wait_ge(x_loaded, 16 * b + 16)
                attention(0, x_in, b)
                first_ffn()
                attention(1, x, b)
                second_ffn()
                dve.drain().then_inc(part_done, 1)


_INS = ['L0_attn_x', 'L0_attn_w_qkv', 'L0_attn_w_out', 'L0_ffn_proj', 'L0_ffn_C1', 'L0_ffn_Win1', 'L0_ffn_Wout1',
        'L0_ffn_C2', 'L0_ffn_Win2', 'L0_ffn_Wout2', 'L1_attn_Wq_down', 'L1_attn_Wk_down', 'L1_attn_Wv_down',
        'L1_attn_Wq_up_c', 'L1_attn_Wq_up_e', 'L1_attn_Wk_up_c', 'L1_attn_Wk_up_e', 'L1_attn_Wv_up', 'L1_attn_Wc',
        'L1_ffn_Ws1', 'L1_ffn_Ws2', 'L1_ffn_W1', 'L1_ffn_W2', 'L1_ffn_Wr']


def rope_tables():
    import numpy as np
    half = DH // 2
    inv = (1.0 / np.float32(10000.0) ** (np.arange(0, half, 2, dtype=np.float32) / np.float32(half))).astype(np.float32)
    freqs = np.arange(T, dtype=np.float32)[:, None] * inv[None, :]
    emb = np.concatenate((freqs, freqs), axis=-1).T
    cos = np.ones((DH, T), np.float32)
    sin = np.zeros((DH, T), np.float32)
    cos[half:] = np.cos(emb)
    sin[half:] = np.sin(emb)
    sin[half::2] *= -1.0
    return np.tile(cos, (MH, 1)), np.tile(sin, (MH, 1))


def kernel(**inputs):
    import numpy as np
    import concourse.bacc as bacc
    from concourse.bass_utils import run_bass_kernel_spmd

    nc = bacc.Bacc("TRN2", target_bir_lowering=False, num_devices=1)
    cos, sin = rope_tables()
    k = np.arange(1, E0 + 1, dtype=np.float32)
    arrays = {f"in_{name}": np.ascontiguousarray(inputs[name]) for name in _INS}
    arrays["cos_table"] = cos
    arrays["sin_table"] = sin
    arrays["k_table"] = np.ascontiguousarray(np.broadcast_to(np.stack([k, 1.0 / k]).astype(np.float32), (P, 2, E0)))
    args = [nc.dram_tensor(name, a.shape, mybir.dt.from_np(a.dtype), kind="ExternalInput").ap() for name, a in arrays.items()]
    out = nc.dram_tensor("out", (B, T, D), F32, kind="ExternalOutput").ap()
    transformer_kernel(nc, *args, out)
    r = run_bass_kernel_spmd(nc, [arrays], core_ids=[0])
    return r.results[0]["out"]
```

```python
import concourse.bass as bass
from concourse import mybir
from concourse.alu_op_type import AluOpType as ALU
from contextlib import ExitStack

F32 = mybir.dt.float32
BF16 = mybir.dt.bfloat16
ACT = mybir.ActivationFunctionType
AX = mybir.AxisListType

P = 128
BANK = 512
LN_EPS = 1e-5
NEG = -1.0e30
LOWEST = -3.0e38

B, T, D = 8, 1024, 256
H = 16
DH = D // H
TT = T // P
KD = D // P
NC = T // BANK
TPC = TT // NC
L = 64
E0, R, O = 16, 128, 1024
OC = O // P
NE, FE = 8, 128
HG = 4
NG = H // HG
MH = P // DH
SCALE = DH ** -0.5

NP = 3
ROWS_A = DH * 2 * NP
ROWS_S = ROWS_A + DH
ROWS = ROWS_S + NP
STACK_DMAS = 5
NBUF = 3

MAX_STEPS = 5
MT_STEP = 5
NORM_STEP = 1

PROJ_BANKS = (0, 1, 2)
FFN_BANKS = (0, 1, 2, 3)
S_BANKS = (3, 4, 5)
O_BANKS = (6, 7)


def score_parts(i):
    return [(p, min(BANK, P * (i + 1) - BANK * p)) for p in range(NC) if P * (i + 1) > BANK * p]


def query_range(j, c):
    return max(P * j, BANK * c), BANK * (c + 1)


def plan_banks():
    place, used, before = {}, [0] * 8, {}

    def put(key, bank):
        place[key] = (bank, used[bank])
        used[bank] += 1

    turn = 0

    def ring(banks, *key):
        nonlocal turn
        put(key, banks[turn % len(banks)])
        turn += 1

    for l in range(2):
        for c in range(NC):
            for kd in range(KD):
                ring(PROJ_BANKS, "xt", 2 * l, c, kd)
            for w in range(2):
                ring(PROJ_BANKS, "qk", l, 0, c, w)
        for tp in range(TT // 2):
            ring(PROJ_BANKS, "v", l, tp)
        for c in range(NC):
            for w in range(2):
                ring(PROJ_BANKS, "qk", l, 1, c, w)
        before[l] = list(used)
        for c in range(NC):
            for kd in range(KD):
                ring(PROJ_BANKS, "yt", l, c, kd)
        for tp in range(TT // 2):
            ring(PROJ_BANKS, "ao", l, tp)
        for c in range(NC):
            for kd in range(KD):
                ring(FFN_BANKS, "xt", 2 * l + 1, c, kd)
        if l == 0:
            ring(FFN_BANKS, "logit")
            for c in range(NC):
                put(("h1", c), 4 + c)
            for c in range(NC):
                ring(FFN_BANKS, "at", c)
            for c in range(NC):
                ring(FFN_BANKS, "g1", c)
                ring(FFN_BANKS, "g2", c)
            for c in range(NC):
                for o in range(OC):
                    ring(FFN_BANKS, "hid", c, o)
                put(("z2", c), 6 + c)
                for tp in range(TPC // 2):
                    ring(FFN_BANKS, "fo", c, tp)
        else:
            ring(FFN_BANKS, "route")
            put(("any",), 4)
            for experts in ([NE], range(NE)):
                units = [(e, c) for e in experts for c in range(NC)]
                for u in range(len(units) + 1):
                    if u < len(units):
                        ring(FFN_BANKS, "he", *units[u])
                    if u:
                        for tp in range(TPC // 2):
                            ring(FFN_BANKS, "eo", *units[u - 1], tp)
    return place, before


def first_scores():
    order = [("qk", 0, 0), ("qk", 0, 1)]
    for h in range(HG):
        order += [("s", 0, i, h, p) for i in reversed(range(TT)) for p, _ in score_parts(i)]
        if h < 2:
            order.append(("qk", 1, h))
    return order + [("mt", 0)]


def group_order(g):
    rest, weight = [], []
    for j in range(TT):
        for half in range(2):
            for h in range(2 * half, 2 * half + 2):
                rest.append(("st", j, h))
                weight.append((T - P * j) if j < MAX_STEPS else 0)
            rest.append(("pv", j, half))
            weight.append(4 * BANK if j < MAX_STEPS else 0)
        if j == NORM_STEP and g > 0:
            rest += [("nm", g - 1, c) for c in range(NC)]
            weight += [0] * NC
        if j == MT_STEP and g + 1 < NG:
            rest.append(("mt", g + 1))
            weight.append(0)
    scores = [("s", g + 1, i, h, p) for i in reversed(range(TT)) for h in range(HG) for p, _ in score_parts(i)] if g + 1 < NG else []
    order, done, passed = [], 0, 0
    for item, w in zip(rest, weight):
        passed += w
        upto = -(-len(scores) * passed // sum(weight))
        order += scores[done:upto]
        done = upto
        order.append(item)
    return order


def plan_scores():
    index, t_index = {}, {}
    for l in range(2):
        order = first_scores()
        for g in range(NG):
            order += group_order(g)
        order += [("nm", NG - 1, c) for c in range(NC)]
        for kind, *key in order:
            if kind in ("s", "mt", "nm"):
                index[(kind, l, *key)] = len(index)
        for g in range(NG):
            for j in range(TT):
                for h in range(HG):
                    for c in range(j // TPC, NC):
                        t_index[l, g, j, h, c] = len(t_index)
    return index, t_index


def transformer_kernel(nc, x_d, w_qkv_d, w_out_d, proj_d, c1_d, win1_d, wout1_d, c2_d, win2_d, wout2_d,
                       wqd_d, wkd_d, wvd_d, wquc_d, wque_d, wkuc_d, wkue_d, wvu_d, wc_d,
                       ws1_d, ws2_d, w1_d, w2_d, wr_d, cos_d, sin_d, kidx_d, out_d):
    place, before_scores = plan_banks()
    sidx, tidx = plan_scores()
    ctx = ExitStack()
    with ctx:
        def sb(name, shape, dt=F32):
            return ctx.enter_context(nc.sbuf_tensor(name, shape, dt))

        x_in = sb("x_in", [P, TT, D])
        x = sb("x", [P, TT, D])
        xn = sb("xn", [P, TT, D])
        xnT = sb("xnT", [P, KD, T])
        y, yT = xn, xnT
        parts = sb("parts", [P, 2, 2, NP, T], BF16)
        stk = sb("stk", [P, NBUF, 2, HG, T], BF16)
        probs = sb("probs", [P, 2, HG, T])
        vaug = sb("vaug", [P, TT, H, DH + 1])
        oT = sb("oT", [P, T])
        mx = sb("mx", [P, HG, TT, 2])
        negm = sb("negm", [P, HG * TT])
        negr = sb("negr", [P, HG * TT])
        mparts = sb("mparts", [P, NP, HG * TT], BF16)
        mT = sb("mT", [P, P], BF16)
        rec = sb("rec", [P, TPC, HG])
        st6 = sb("st6", [P, TT, 6])
        mv = sb("mv", [P, TT, 2])
        veps = sb("veps", [P, TT])
        rstd = sb("rstd", [P, TT])
        neg_half = sb("neg_half", [P, TT])
        wqkv = [sb(f"wqkv{l}", [P, KD, 3 * D]) for l in range(2)]
        wo = [sb(f"wo{l}", [P, KD, D]) for l in range(2)]
        projw = sb("projw", [P, KD, E0])
        c12 = sb("c12", [E0, 2, R])
        win1 = sb("win1", [P, KD, R])
        bias1 = sb("bias1", [P, 1])
        wout1T = sb("wout1T", [R, O])
        win2 = sb("win2", [P, OC, R])
        bias2 = sb("bias2", [P, 1])
        wout2T = sb("wout2T", [R, D])
        wr = sb("wr", [P, KD, NE])
        w1 = sb("w1", [P, NE + 1, KD, FE])
        w2 = sb("w2", [P, NE + 1, D])
        cos = sb("cos", [P, T])
        sin = sb("sin", [P, T])
        ident = sb("ident", [P, P])
        ident_b = sb("ident_b", [P, P], BF16)
        mask_b = sb("mask_b", [P, P], BF16)
        kidx = sb("kidx", [P, 2, E0])
        zsm = sb("zsm", [P, 4, TT])
        zc = sb("zc", [P, TT, E0])
        zt = sb("zt", [P, TT, E0])
        zu = sb("zu", [P, TT, E0])
        cum = oT[:, 0:3 * 2 * TT * E0].rearrange("p (a t k) -> p a t k", a=3, k=E0)
        gate = sb("gate", [P, TT, NE])
        gmax = sb("gmax", [P, 1])
        flag = sb("flag", [1, 1])
        flag_i = sb("flag_i", [1, 1], mybir.dt.int32)
        flat = probs[:, :, :, :].rearrange("p a h t -> p (a h t)")
        scratch = [flat[:, BANK * i:BANK * (i + 1)] for i in range(16)]
        qf, qs, qc, qr = (scratch[2 * i:2 * i + 2] for i in range(4))
        aT = flat[0:E0, 0:T]
        gsb = [scratch[2 + i] for i in range(4)]
        z1 = scratch[6:8]
        hsb = scratch[8:12]
        z2 = scratch[12:14]
        hr = scratch[0:4]
        hq = scratch[4:8]
        down = flat[:, 0:3 * KD * H * L].rearrange("p (w k n) -> p w k n", w=3, k=KD)
        stage = stk[:, :, :, :, :].rearrange("p b w h t -> p (b w h t)").bitcast(F32)
        dT = stage[:, 0:3 * 8 * D].rearrange("p (w b d) -> p w b d", w=3, b=8)
        up = stage[:, 6144:6144 + 3 * DH].rearrange("p (w d) -> p w d", w=3)
        wo1_s = stage[:, 6400:6400 + OC * R].rearrange("p (o r) -> p o r", o=OC)
        wo2_s = stage[:, 7424:7424 + KD * R].rearrange("p (o r) -> p o r", o=KD)

        ps = ctx.enter_context(nc.psum_tensor("ps", [P, 8 * BANK], F32))
        bank = [ps[:, BANK * b:BANK * (b + 1)] for b in range(8)]
        st_bank = [bank[b] for b in PROJ_BANKS]
        s_bank = [bank[b] for b in S_BANKS]
        o_bank = [bank[b] for b in O_BANKS]

        def sem(name):
            return ctx.enter_context(nc.semaphore(name))

        w_loaded = sem("w_loaded")
        w_const = sem("w_const")
        w_full = sem("w_full")
        w_drained = sem("w_drained")
        x_loaded = sem("x_loaded")
        stored = sem("stored")
        next_pass = sem("next_pass")
        first = part_done = sem("part_done")
        begun = sem("begun")
        full = [sem("full0")] + [sem(f"full{b}") for b in range(1, 8)]
        drained = [sem(f"drained{b}") for b in range(8)]
        ln_var = sem("ln_var")
        ln_rstd = sem("ln_rstd")
        xn_ready = sem("xn_ready")
        part0_ready = sem("part0_ready")
        rest_ready = sem("rest_ready")
        part1_ready = sem("part1_ready")
        parts_ready = sem("parts_ready")
        swap_ready = sem("swap_ready")
        rotated_ready = sem("rotated_ready")
        gmax_ready = sem("gmax_ready")
        flag_ready = sem("flag_ready")
        rope_ready = sem("rope_ready")
        stk_loaded = [[sem(f"stk_loaded{b}_{h}") for h in range(HG)] for b in range(NBUF)]
        m_loaded = [sem(f"m_loaded{b}") for b in range(NBUF)]
        s_full = sem("s_full")
        s_drained = sem("s_drained")
        mx_ready = sem("mx_ready")
        st_full = sem("st_full")
        exp_done = sem("exp_done")
        p_ready = sem("p_ready")
        pv_done = sem("pv_done")
        o_drained = sem("o_drained")
        ent_var = sem("ent_var")
        ent_rstd = sem("ent_rstd")
        delta_ready = sem("delta_ready")
        sqrt_ready = sem("sqrt_ready")
        a_ready = sem("a_ready")
        h_used = sem("h_used")
        gap_ready = sem("gap_ready")
        egap_ready = sem("egap_ready")
        relu_ready = sem("relu_ready")
        hq_ready = sem("hq_ready")
        x_done = sem("x_done")
        act_chain = sem("act_chain")
        last = dve_chain = sem("dve_chain")
        pass_sems = range(first.num, last.num + 1)

        def arrived(eng, *key):
            b, n = place[key]
            eng.wait_ge(full[b], n + 1)
            return bank[b]

        def begin_pass(eng, b):
            eng.wait_ge(next_pass, b + 1)
            eng.sem_inc(begun, 1)

        def buffer_of(e, c):
            return (NC * (0 if e == NE else e + 1) + c) % 4

        def read_out(*key):
            return drained[place[key][0]]

        block = ctx.enter_context(nc.Block())

        @block.sync
        def _(sp):
            loads = [
                (wqkv[0][:], w_qkv_d.rearrange("(k p) n -> p k n", p=P)),
                (wo[0][:], w_out_d.rearrange("(k p) n -> p k n", p=P)),
                (down[:, 0], wqd_d.rearrange("(k p) n -> p k n", p=P)),
                (down[:, 1], wkd_d.rearrange("(k p) n -> p k n", p=P)),
                (down[:, 2], wvd_d.rearrange("(k p) n -> p k n", p=P)),
                (wo1_s, wout1_d.rearrange("(o p) r -> p o r", p=P)),
                (wo2_s, wout2_d.rearrange("(o p) r -> p o r", p=P)),
                (projw[:], proj_d.rearrange("(k p) n -> p k n", p=P)),
                (c12[:, 0], c1_d), (c12[:, 1], c2_d),
                (win1[:], win1_d[0:D, :].rearrange("(k p) r -> p k r", p=P)),
                (bias1[:], win1_d[D:D + 1, :].rearrange("a r -> r a")),
                (win2[:], win2_d[0:O, :].rearrange("(o p) r -> p o r", p=P)),
                (bias2[:], win2_d[O:O + 1, :].rearrange("a r -> r a")),
                (wo[1][:], wc_d.rearrange("(k p) n -> p k n", p=P)),
                (wr[:], wr_d.rearrange("(k p) n -> p k n", p=P)),
                (w1[:, NE], ws1_d.rearrange("(k p) f -> p k f", p=P)),
                (w2[:, NE], ws2_d),
                (cos[:], cos_d), (sin[:], sin_d), (kidx[:], kidx_d),
            ]
            for e in range(NE):
                loads.append((w1[:, e], w1_d[e].rearrange("(k p) f -> p k f", p=P)))
                loads.append((w2[:, e], w2_d[e]))
            half = DH // 2
            for r in range(2):
                rows = slice(L * r, L * (r + 1))
                loads += [(up[rows, 0, 0:half], wquc_d), (up[rows, 0, half:DH], wque_d),
                          (up[rows, 1, 0:half], wkuc_d), (up[rows, 1, half:DH], wkue_d),
                          (up[rows, 2], wvu_d)]
            sp.dma_start(x_in[:], x_d[0].rearrange("(t p) d -> p t d", p=P)).then_inc(x_loaded, 16)
            for dst, src in loads:
                sp.dma_start(dst, src).then_inc(w_loaded, 16)
            sp.wait_ge(w_loaded, 16 * len(loads))
            sp.sem_inc(w_const, 1)
            sp.sem_inc(stored, 16)
            sp.wait_ge(part_done, 4)
            sp.sem_clear(pass_sems)
            sp.sem_inc(next_pass, 1)

            def load_stack(l, g):
                m, buf = g // 2, g % NBUF
                sp.wait_ge(parts_ready, 8 * l + 4 * (m + 1))
                if NG * l + g >= NBUF:
                    done = NG * l + g - NBUF
                    sp.wait_ge(st_full, tidx[done // NG, done % NG, TT - 1, HG - 1, NC - 1] + 1)
                for h in range(HG):
                    rows = slice(DH * ((g % 2) * HG + h), DH * ((g % 2) * HG + h + 1))
                    ends = parts[rows, m].rearrange("d w p t -> d (w p) t")[:, 0:2 * NP:2 * NP - 1, :]
                    for t in range(2):
                        block = slice(DH * NP * t, DH * NP * (t + 1))
                        k = parts[rows, m, 1, t:t + 1, :].broadcast_to([DH, NP, T])
                        sp.dma_start(stk[block, buf, 0, h, :], parts[rows, m, 0, :, :]).then_inc(stk_loaded[buf][h], 16)
                        sp.dma_start(stk[block, buf, 1, h, :], k).then_inc(stk_loaded[buf][h], 16)
                    sp.dma_start(stk[ROWS_A:ROWS_S, buf, :, h, :], ends).then_inc(stk_loaded[buf][h], 16)

            def load_max(l, g):
                sp.wait_ge(s_drained, sidx["mt", l, g] + 1)
                sp.dma_start(stk[ROWS_S:ROWS, g % NBUF, 0, :, :].rearrange("r h t -> r (h t)"),
                             mT[0:NP * HG * TT, :]).then_inc(m_loaded[g % NBUF], 16)

            with sp.Fori(0, B) as b:
                for l in range(2):
                    load_stack(l, 0)
                    load_stack(l, 1)
                    load_max(l, 0)
                    load_stack(l, 2)
                    load_max(l, 1)
                    load_stack(l, 3)
                    load_max(l, 2)
                    load_max(l, 3)
                    if l == 0:
                        for tp in range(TT // 2):
                            bk, n = place["ao", 0, tp]
                            sp.wait_ge(drained[bk], n + 1)
                        sp.dma_start(x_in[:], x_d[(b + 1) % B].rearrange("(t p) d -> p t d", p=P)).then_inc(x_loaded, 16)
                sp.wait_ge(x_done, 1)
                sp.dma_start(out_d[b].rearrange("(t p) d -> p t d", p=P), x[:]).then_inc(stored, 16)
                sp.wait_ge(part_done, 4)
                sp.sem_clear(pass_sems)
                sp.sem_inc(next_pass, 1)
            sp.wait_ge(stored, 16 * (B + 1))
            sp.wait_ge(x_loaded, 16 * (B + 1))

        @block.tensor
        def _(pe):
            def claim(*key):
                b, n = place[key]
                if n:
                    pe.wait_ge(drained[b], n)
                return bank[b], full[b]

            def in_sbuf(*key):
                b, n = place[key]
                pe.wait_ge(drained[b], n + 1)

            pe.wait_ge(w_const, 2)
            unit = 0

            def setup_bank():
                nonlocal unit
                if unit >= 4:
                    pe.wait_ge(w_drained, unit - 3)
                unit += 1
                return bank[(unit - 1) % 4]

            for u in range(2):
                pt = setup_bank()
                for i in range(4):
                    ins = pe.transpose(pt[:, P * i:P * (i + 1)], wo1_s[:, 4 * u + i, :], ident[:])
                ins.then_inc(w_full, 1)
            pt = setup_bank()
            for i in range(KD):
                ins = pe.transpose(pt[:, P * i:P * (i + 1)], wo2_s[:, i, :], ident[:])
            ins.then_inc(w_full, 1)
            for w in range(3):
                for u in range(4):
                    pt = setup_bank()
                    for i in range(4):
                        blk = 2 * u + i // KD
                        ins = pe.transpose(pt[:, P * i:P * (i + 1)], down[:, w, i % KD, P * blk:P * (blk + 1)], ident[:])
                    ins.then_inc(w_full, 1)
            for w in range(3):
                pe.wait_ge(w_drained, 3 + 4 * (w + 1))
                for odd in range(2):
                    pt = setup_bank()
                    rows = slice(L * odd, L * (odd + 1))
                    for kd in range(KD):
                        for i in range(H // 2):
                            col = DH * (H // 2 * kd + i)
                            ins = pe.matmul(pt[:, col:col + DH], dT[rows, w, i, P * kd:P * (kd + 1)], up[rows, w, :],
                                            start=True, stop=True)
                    ins.then_inc(w_full, 1)
            pe.drain().then_inc(part_done, 1)

            def transposed_x(s, c):
                pe.wait_ge(xn_ready, NC * s + c + 1)
                for kd in range(KD):
                    pt, done = claim("xt", s, c, kd)
                    for i in range(TPC):
                        ins = pe.transpose(pt[:, P * i:P * (i + 1)], xn[:, TPC * c + i, P * kd:P * (kd + 1)], ident[:])
                    ins.then_inc(done, 1)

            def need_xT(s, c):
                for kd in range(KD):
                    in_sbuf("xt", s, c, kd)

            def project_qk(l, m, c, w):
                pt, done = claim("qk", l, m, c, w)
                for kd in range(KD):
                    ins = pe.matmul(pt, wqkv[l][:, kd, D * w + P * m:D * w + P * (m + 1)],
                                    xnT[:, kd, BANK * c:BANK * (c + 1)], start=kd == 0, stop=kd == KD - 1)
                ins.then_inc(done, 1)

            def by_token(pt, left, right, tiles, n_k):
                for i, t in enumerate(tiles):
                    for kd in range(n_k):
                        ins = pe.matmul(pt[:, D * i:D * (i + 1)], left(kd, t), right(kd), start=kd == 0, stop=kd == n_k - 1)
                return ins

            def score_unit(l, g, i, h, p, width):
                n, buf = sidx["s", l, g, i, h, p], g % NBUF
                if n >= len(S_BANKS):
                    pe.wait_ge(s_drained, n - len(S_BANKS) + 1)
                out = s_bank[n % len(S_BANKS)][:, 0:width]
                lhsT = stk[0:ROWS_S, buf, 0, h, P * i:P * (i + 1)]
                diagonal = BANK * p + width == P * (i + 1)
                ins = pe.matmul(out, lhsT, stk[0:ROWS_S, buf, 1, h, BANK * p:BANK * p + width], start=True, stop=not diagonal)
                if diagonal:
                    ins = pe.matmul(out[:, width - P:width], ident_b[:], mask_b[:], start=False, stop=True)
                ins.then_inc(s_full, 1)

            def stack_ready(l, g, h):
                uses = 1 + (g >= NBUF) + l * (1 + (g % NBUF + NBUF < NG))
                pe.wait_ge(stk_loaded[g % NBUF][h], STACK_DMAS * 16 * uses)

            def max_rows(l, g):
                n = sidx["mt", l, g]
                pe.wait_ge(s_drained, n - len(S_BANKS) + 1)
                pe.wait_ge(mx_ready, NG * l + g + 1)
                rows = NP * HG * TT
                pe.transpose(s_bank[n % len(S_BANKS)][0:rows, 0:P // 2].bitcast(BF16),
                             mparts[:].rearrange("q p m -> q (p m)"), ident_b[:]).then_inc(s_full, 1)

            def normalise(l, g, c):
                n = sidx["nm", l, g, c]
                pe.wait_ge(s_drained, n - len(S_BANKS) + 1)
                pe.wait_ge(o_drained, NC * (NG * l + g) + c + 1)
                for i in range(TPC):
                    t = TPC * c + i
                    ins = pe.transpose(s_bank[n % len(S_BANKS)][:, P * i:P * (i + 1)], oT[:, P * t:P * (t + 1)], ident[:])
                ins.then_inc(s_full, 1)

            def scores_t(l, g, j, h):
                buf = g % NBUF
                for c in range(j // TPC, NC):
                    n = tidx[l, g, j, h, c]
                    if n >= len(st_bank):
                        pe.wait_ge(exp_done, n - len(st_bank) + 1)
                    a, z = query_range(j, c)
                    pe.matmul(st_bank[n % len(st_bank)][:, a - BANK * c:z - BANK * c], stk[0:ROWS, buf, 1, h, P * j:P * (j + 1)],
                              stk[0:ROWS, buf, 0, h, a:z], start=True, stop=True).then_inc(st_full, 1)

            def weigh_values(l, g, j, c):
                step = TT * (NG * l + g) + j
                a, z = query_range(j, c)
                if a >= z:
                    return
                if c == j // TPC:
                    pe.wait_ge(p_ready, HG * (step + 1))
                else:
                    pe.wait_ge(exp_done, tidx[l, g, j, HG - 1, c] + 1)
                if j == 0 and NG * l + g > 0:
                    pe.wait_ge(o_drained, NC * (NG * l + g - 1) + c + 1)
                for h in range(HG):
                    ins = pe.matmul(o_bank[c][32 * h:32 * h + DH + 1, a - BANK * c:z - BANK * c],
                                    vaug[:, j, HG * g + h, :], probs[:, step % 2, h, a:z],
                                    start=j == 0, stop=j == TPC * (c + 1) - 1)
                if c == NC - 1:
                    ins.then_inc(pv_done, 1)

            def banks_read(l, banks):
                for b in banks:
                    if before_scores[l][b]:
                        pe.wait_ge(drained[b], before_scores[l][b])

            def attention(l):
                for c in range(NC):
                    transposed_x(2 * l, c)
                    need_xT(2 * l, c)
                    for w in range(2):
                        project_qk(l, 0, c, w)
                for tp in range(TT // 2):
                    pt, done = claim("v", l, tp)
                    by_token(pt, lambda kd, t: xnT[:, kd, P * t:P * (t + 1)], lambda kd: wqkv[l][:, kd, 2 * D:3 * D],
                             (2 * tp, 2 * tp + 1), KD).then_inc(done, 1)
                banks_read(l, S_BANKS + O_BANKS)
                for kind, *key in first_scores():
                    if kind == "qk":
                        project_qk(l, 1, *key)
                    elif kind == "mt":
                        max_rows(l, 0)
                    else:
                        g, i, h, p = key
                        if i == TT - 1 and p == 0:
                            stack_ready(l, 0, h)
                        score_unit(l, 0, i, h, p, dict(score_parts(i))[p])
                banks_read(l, PROJ_BANKS)
                before = None
                for g in range(NG):
                    pe.wait_ge(m_loaded[g % NBUF], 16 * (1 + (g >= NBUF) + l * (1 + (g % NBUF + NBUF < NG))))
                    for kind, *key in group_order(g):
                        if kind == "st":
                            scores_t(l, g, *key)
                        elif kind == "pv":
                            j, c = key
                            if before:
                                weigh_values(l, *before, c)
                            if c == NC - 1:
                                before = (g, j)
                        elif kind == "mt":
                            max_rows(l, g + 1)
                        elif kind == "nm":
                            normalise(l, *key)
                        else:
                            _, i, h, p = key
                            if i == TT - 1 and p == 0:
                                stack_ready(l, g + 1, h)
                            score_unit(l, g + 1, i, h, p, dict(score_parts(i))[p])
                for c in range(NC):
                    weigh_values(l, *before, c)
                for c in range(NC):
                    normalise(l, NG - 1, c)
                pe.wait_ge(exp_done, tidx[l, NG - 1, TT - 1, HG - 1, NC - 1] + 1)
                pe.wait_ge(s_drained, sidx["nm", l, NG - 1, NC - 1] + 1)
                for c in range(NC):
                    for kd in range(KD):
                        pt, done = claim("yt", l, c, kd)
                        for i in range(TPC):
                            ins = pe.transpose(pt[:, P * i:P * (i + 1)], y[:, TPC * c + i, P * kd:P * (kd + 1)], ident[:])
                        ins.then_inc(done, 1)
                for tp in range(TT // 2):
                    for kd in range(KD):
                        in_sbuf("yt", l, 2 * tp // TPC, kd)
                    pt, done = claim("ao", l, tp)
                    by_token(pt, lambda kd, t: yT[:, kd, P * t:P * (t + 1)], lambda kd: wo[l][:, kd, :],
                             (2 * tp, 2 * tp + 1), KD).then_inc(done, 1)

            def first_ffn():
                for c in range(NC):
                    transposed_x(1, c)
                pt, done = claim("logit")
                for t in range(TT):
                    need_xT(1, t // TPC)
                    for kd in range(KD):
                        ins = pe.matmul(pt[:, E0 * t:E0 * (t + 1)], xnT[:, kd, P * t:P * (t + 1)], projw[:, kd, :],
                                        start=kd == 0, stop=kd == KD - 1)
                ins.then_inc(done, 1)
                for c in range(NC):
                    pt, done = claim("h1", c)
                    for kd in range(KD):
                        ins = pe.matmul(pt, win1[:, kd, :], xnT[:, kd, BANK * c:BANK * (c + 1)], start=kd == 0, stop=kd == KD - 1)
                    ins.then_inc(done, 1)
                pe.wait_ge(a_ready, 1)
                for c in range(NC):
                    pt, done = claim("at", c)
                    for i in range(TPC):
                        ins = pe.transpose(pt[0:E0, P * i:P * (i + 1)], zu[:, TPC * c + i, :], ident[:])
                    ins.then_inc(done, 1)
                for c in range(NC):
                    in_sbuf("at", c)
                    for n, name in enumerate(("g1", "g2")):
                        pt, done = claim(name, c)
                        pe.matmul(pt, c12[:, n, :], aT[:, BANK * c:BANK * (c + 1)], start=True, stop=True).then_inc(done, 1)

                def hidden(c, o):
                    pt, done = claim("hid", c, o)
                    pe.matmul(pt, wout1T[:, P * o:P * (o + 1)], z1[c], start=True, stop=True).then_inc(done, 1)

                for c in range(NC):
                    in_sbuf("h1", c)
                    acc, done = claim("z2", c)
                    lag = 3
                    for o in range(OC + lag):
                        if o < OC:
                            hidden(c, o)
                        if o >= lag:
                            in_sbuf("hid", c, o - lag)
                            ins = pe.matmul(acc, win2[:, o - lag, :], hsb[(o - lag) % 4], start=o == lag, stop=o == OC + lag - 1)
                            if o < OC + lag - 1:
                                ins.then_inc(h_used, 1)
                    ins.then_inc(done, 1)
                    in_sbuf("z2", c)
                    for tp in range(TPC // 2):
                        pt, done = claim("fo", c, tp)
                        by_token(pt, lambda kd, t: z2[c][:, P * t:P * (t + 1)], lambda kd: wout2T[:],
                                 (2 * tp, 2 * tp + 1), 1).then_inc(done, 1)

            def second_ffn():
                for c in range(NC):
                    transposed_x(3, c)
                pt, done = claim("route")
                for t in range(TT):
                    need_xT(3, t // TPC)
                    for kd in range(KD):
                        ins = pe.matmul(pt[:, NE * t:NE * (t + 1)], xnT[:, kd, P * t:P * (t + 1)], wr[:, kd, :],
                                        start=kd == 0, stop=kd == KD - 1)
                ins.then_inc(done, 1)

                def up_unit(e, c):
                    pt, done = claim("he", e, c)
                    for kd in range(KD):
                        ins = pe.matmul(pt, w1[:, e, kd, :], xnT[:, kd, BANK * c:BANK * (c + 1)], start=kd == 0, stop=kd == KD - 1)
                    ins.then_inc(done, 1)

                def down_unit(e, c):
                    in_sbuf("he", e, c)
                    for tp in range(TPC // 2):
                        pt, done = claim("eo", e, c, tp)
                        by_token(pt, lambda kd, t: hq[buffer_of(e, c)][:, P * t:P * (t + 1)], lambda kd: w2[:, e, :],
                                 (2 * tp, 2 * tp + 1), 1).then_inc(done, 1)

                def experts(which):
                    units = [(e, c) for e in which for c in range(NC)]
                    for u in range(len(units) + 1):
                        if u < len(units):
                            up_unit(*units[u])
                        if u:
                            down_unit(*units[u - 1])

                pe.wait_ge(gmax_ready, 1)
                pt, done = claim("any")
                pe.transpose(pt[0:1, 0:P], gmax[:], ident[:]).then_inc(done, 1)
                experts([NE])
                pe.wait_ge(flag_ready, 1)
                routed = pe.value_load(flag_i[:], min_val=0, max_val=1)
                with pe.If(routed > 0):
                    experts(range(NE))

            with pe.Fori(0, B) as b:
                begin_pass(pe, b)
                attention(0)
                first_ffn()
                attention(1)
                second_ffn()
                pe.drain().then_inc(part_done, 1)

        @block.scalar
        def _(act):
            unit = 0

            def setup_copy(dst, n=BANK):
                nonlocal unit
                act.wait_ge(w_full, unit + 1)
                src = bank[unit % 4][:, 0:n]
                if len(dst.shape) == 3:
                    src = src.rearrange("p (a n) -> p a n", a=dst.shape[1])
                act.activation(dst, src, ACT.Copy).then_inc(w_drained, 1)
                unit += 1

            for u in range(2):
                setup_copy(wout1T[:, BANK * u:BANK * (u + 1)])
            setup_copy(wout2T[:], D)
            for w in range(3):
                for u in range(4):
                    setup_copy(dT[:, w, 2 * u:2 * u + 2, :])
            for w in range(3):
                for odd in range(2):
                    act.wait_ge(w_full, unit + 1)
                    src = bank[unit % 4][:, 0:KD * D // 2].rearrange("p (k i d) -> p k i d", k=KD, d=DH)
                    dst = wqkv[1][:, :, D * w:D * (w + 1)].rearrange("p k (i o d) -> p k i o d", o=2, d=DH)[:, :, :, odd, :]
                    act.activation(dst, src, ACT.Copy).then_inc(w_drained, 1)
                    unit += 1
            act.drain().then_inc(part_done, 1)

            def copy_xT(name, s, c, kd):
                pt = arrived(act, name, s, c, kd)
                act.activation(xnT[:, kd, BANK * c:BANK * (c + 1)], pt, ACT.Copy).then_inc(read_out(name, s, c, kd), 1)

            def part0(l, u, m, c, w):
                dst = parts[:, m, w, 0, BANK * c:BANK * (c + 1)]
                if l == 0:
                    pt = arrived(act, "qk", l, m, c, w)
                    act.activation(dst, pt, ACT.Copy).then_inc(part0_ready, 1)
                else:
                    act.wait_ge(rope_ready, u + 1)
                    act.activation(dst, qs[u % 2], ACT.Copy).then_inc(part0_ready, 1)

            def copy_q(u, m, c, w):
                pt = arrived(act, "qk", 1, m, c, w)
                if u >= 2:
                    act.wait_ge(parts_ready, 8 + u - 1)
                act.activation(qf[u % 2], pt, ACT.Copy).then_inc(read_out("qk", 1, m, c, w), 1)

            def part1(l, u, m, c, w):
                act.wait_ge(rest_ready, 8 * l + u + 1)
                act.activation(parts[:, m, w, 1, BANK * c:BANK * (c + 1)], qr[u % 2], ACT.Copy).then_inc(part1_ready, 1)

            def split(l, m, c):
                units = [(4 * m + 2 * c + w, m, c, w) for w in range(2)]
                for u in units:
                    part0(l, *u)
                for u in units:
                    part1(l, *u)

            def split_rotated(m, c, w):
                u = 4 * m + 2 * c + w
                copy_q(u, m, c, w)
                part0(1, u, m, c, w)
                part1(1, u, m, c, w)

            def attention(l):
                for c in range(NC):
                    for kd in range(KD):
                        copy_xT("xt", 2 * l, c, kd)
                    if l == 0:
                        split(0, 0, c)
                    else:
                        for w in range(2):
                            split_rotated(0, c, w)
                for tp in range(TT // 2):
                    pt = arrived(act, "v", l, tp)
                    act.activation(vaug[:, 2 * tp:2 * tp + 2, :, 0:DH], pt.rearrange("p (t h d) -> p t h d", t=2, h=H),
                                   ACT.Copy).then_inc(read_out("v", l, tp), 1)
                for c in range(NC):
                    if l == 0:
                        split(0, 1, c)
                    else:
                        for w in range(2):
                            split_rotated(1, c, w)

                def copy_o(g):
                    act.wait_ge(pv_done, TT * (NG * l + g + 1))
                    if NG * l + g > 0:
                        key = ("nm", l, g - 1, NC - 1) if g else ("nm", l - 1, NG - 1, NC - 1)
                        act.wait_ge(s_drained, sidx[key] + 1)
                    for c in range(NC):
                        act.activation(oT[:, BANK * c:BANK * (c + 1)], o_bank[c], ACT.Copy).then_inc(o_drained, 1)

                for g in range(NG):
                    for j in range(TT):
                        step = TT * (NG * l + g) + j
                        if step >= 2:
                            act.wait_ge(pv_done, step - 1)
                        for h in range(HG):
                            for c in range(j // TPC, NC):
                                n = tidx[l, g, j, h, c]
                                a, z = query_range(j, c)
                                act.wait_ge(st_full, n + 1)
                                act.activation(probs[:, step % 2, h, a:z], st_bank[n % len(st_bank)][:, a - BANK * c:z - BANK * c],
                                               ACT.Exp, scale=SCALE).then_inc(exp_done, 1)
                        if g > 0 and j == 0:
                            copy_o(g - 1)
                copy_o(NG - 1)
                for c in range(NC):
                    for kd in range(KD):
                        copy_xT("yt", l, c, kd)

            def first_ffn():
                for c in range(NC):
                    for kd in range(KD):
                        copy_xT("xt", 1, c, kd)
                act.wait_ge(delta_ready, 1)
                act.activation(zt[:], zt[:], ACT.Sqrt).then_inc(sqrt_ready, 1)
                for c in range(NC):
                    pt = arrived(act, "at", c)
                    act.activation(aT[:, BANK * c:BANK * (c + 1)], pt[0:E0, :], ACT.Copy).then_inc(read_out("at", c), 1)
                for c in range(NC):
                    for n, name in enumerate(("g1", "g2")):
                        pt = arrived(act, name, c)
                        act.activation(gsb[2 * c + n], pt, ACT.Copy).then_inc(read_out(name, c), 1)
                for c in range(NC):
                    for o in range(OC):
                        pt = arrived(act, "hid", c, o)
                        n = OC * c + o
                        if o >= 4:
                            act.wait_ge(h_used, (OC - 1) * c + o - 3)
                        elif c:
                            bk, k = place["z2", c - 1]
                            act.wait_ge(full[bk], k + 1)
                        act.activation(hsb[n % 4], pt, ACT.Gelu).then_inc(read_out("hid", c, o), 1)

            def second_ffn():
                for c in range(NC):
                    for kd in range(KD):
                        copy_xT("xt", 3, c, kd)
                act.wait_ge(gap_ready, 1)
                act.activation(zsm[:, 1, :], zsm[:, 0, :], ACT.Exp).then_inc(egap_ready, 1)

                def experts(which):
                    for e in which:
                        for c in range(NC):
                            u = NC * (0 if e == NE else e + 1) + c
                            pt = arrived(act, "he", e, c)
                            if u >= 4:
                                act.wait_ge(hq_ready, u - 3)
                            act.activation(hr[buffer_of(e, c)], pt, ACT.Relu).then_inc(relu_ready, 1)

                experts([NE])
                act.wait_ge(flag_ready, 1)
                routed = act.value_load(flag_i[:], min_val=0, max_val=1)
                with act.If(routed > 0):
                    experts(range(NE))

            with act.Fori(0, B) as b:
                begin_pass(act, b)
                attention(0)
                first_ffn()
                attention(1)
                second_ffn()
                act.drain().then_inc(part_done, 1)

        @block.gpsimd
        def _(pool):
            n = 0

            def done(ins):
                nonlocal n
                n += 1
                ins.then_inc(act_chain, 1)
                pool.wait_ge(act_chain, n)

            done(pool.memset(ident[:], 0.0))
            done(pool.memset(ident_b[:], 0.0))
            done(pool.memset(mask_b[:], 0.0))
            done(pool.memset(neg_half[:], -0.5))
            for t in (ident, ident_b):
                done(pool.affine_select(out=t[:], in_=t[:], compare_op=ALU.not_equal, fill=1.0, base=0,
                                        pattern=[[-1, P]], channel_multiplier=1))
            pool.affine_select(out=mask_b[:], in_=mask_b[:], compare_op=ALU.is_ge, fill=NEG, base=0,
                               pattern=[[-1, P]], channel_multiplier=1).then_inc(w_const, 1)
            pool.drain().then_inc(part_done, 1)

            def inverse_root(s):
                for c in range(NC):
                    pool.wait_ge(ln_var, NC * s + c + 1)
                    tiles = slice(TPC * c, TPC * (c + 1))
                    pool.tensor_tensor(rstd[:, tiles], veps[:, tiles], neg_half[:, tiles], ALU.pow).then_inc(ln_rstd, 1)

            def attention(l):
                inverse_root(2 * l)
                if l:
                    for m in range(2):
                        for c in range(NC):
                            for w in range(2):
                                u = 4 * m + 2 * c + w
                                bk, k = place["qk", 1, m, c, w]
                                pool.wait_ge(drained[bk], k + 1)
                                cols = slice(BANK * c, BANK * (c + 1))
                                pool.tensor_tensor(qc[u % 2], qf[u % 2], cos[:, cols], ALU.mult).then_inc(rotated_ready, 1)
                                pool.wait_ge(swap_ready, u + 1)
                                pool.tensor_tensor(qs[u % 2], qs[u % 2], sin[:, cols], ALU.mult).then_inc(rotated_ready, 1)
                for step in range(TT * NG * l, TT * NG * (l + 1)):
                    j = step % TT
                    for h in range(HG):
                        pool.wait_ge(exp_done, tidx[l, step // TT % NG, j, h, j // TPC] + 1)
                        diag = probs[:, step % 2, h, P * j:P * (j + 1)]
                        pool.affine_select(out=diag, in_=diag, compare_op=ALU.is_ge, fill=0.0, base=0,
                                           pattern=[[1, P]], channel_multiplier=-1).then_inc(p_ready, 1)

            with pool.Fori(0, B) as b:
                begin_pass(pool, b)
                attention(0)
                inverse_root(1)
                pool.wait_ge(ent_var, 1)
                pool.tensor_tensor(zsm[:, 2, :], zsm[:, 1, :], neg_half[:], ALU.pow).then_inc(ent_rstd, 1)
                attention(1)
                inverse_root(3)
                pool.drain().then_inc(part_done, 1)

        @block.vector
        def _(dve):
            links = 0

            def link(ins):
                nonlocal links
                links += 1
                ins.then_inc(dve_chain, 1)
                dve.wait_ge(dve_chain, links)

            dve.memset(vaug[:], 1.0)
            dve.memset(mx[:], LOWEST)
            dve.wait_ge(w_drained, 21)
            for buf in range(NBUF):
                dve.memset(stk[ROWS_A:P, buf, 1, :, :], 1.0)
            for c in range(NC):
                dve.memset(o_bank[c], 0.0)
            dve.drain().then_inc(part_done, 1)

            def row_statistics(s, c, src):
                tiles = range(TPC * c, TPC * (c + 1))
                for t in tiles:
                    ins = dve.bn_stats(st6[:, t, :], src[:, t, :])
                link(ins)
                for t in tiles:
                    ins = dve.bn_aggr(mv[:, t, :], st6[:, t, :])
                link(ins)
                cs = slice(TPC * c, TPC * (c + 1))
                dve.tensor_scalar(veps[:, cs], mv[:, cs, 1], LN_EPS, None, ALU.add).then_inc(ln_var, 1)

            def normalised(s, c, src):
                dve.wait_ge(ln_rstd, NC * s + c + 1)
                for t in range(TPC * c, TPC * (c + 1)):
                    ins = dve.tensor_scalar(xn[:, t, :], src[:, t, :], mv[:, t, 0:1], rstd[:, t:t + 1],
                                            ALU.subtract, ALU.mult)
                ins.then_inc(xn_ready, 1)

            def rest(l, m, c, w):
                u = 4 * m + 2 * c + w
                part = parts[:, m, w, 0, BANK * c:BANK * (c + 1)]
                if l == 0:
                    dve.wait_ge(part0_ready, u + 1)
                    pt = arrived(dve, "qk", l, m, c, w)
                    if u >= 2:
                        dve.wait_ge(parts_ready, u - 1)
                    dve.tensor_tensor(qr[u % 2], pt, part, ALU.subtract).then_inc(rest_ready, 1)
                    bk, k = place["qk", l, m, c, w]
                    dve.wait_ge(rest_ready, u + 1)
                    dve.sem_inc(drained[bk], 1)
                else:
                    bk, k = place["qk", l, m, c, w]
                    dve.wait_ge(drained[bk], k + 1)
                    swap = [i ^ 1 for i in range(32)]
                    if u >= 2:
                        dve.wait_ge(parts_ready, 8 + u - 1)
                    dve.stream_shuffle(qs[u % 2], qf[u % 2], swap).then_inc(swap_ready, 1)
                    dve.wait_ge(rotated_ready, 2 * u + 2)
                    dve.tensor_tensor(qs[u % 2], qs[u % 2], qc[u % 2], ALU.add).then_inc(rope_ready, 1)
                    dve.wait_ge(part0_ready, 8 + u + 1)
                    dve.tensor_tensor(qr[u % 2], qs[u % 2], part, ALU.subtract).then_inc(rest_ready, 1)

            def part2(l, m, c, w):
                u = 4 * m + 2 * c + w
                dve.wait_ge(part1_ready, 8 * l + u + 1)
                cols = slice(BANK * c, BANK * (c + 1))
                dve.tensor_tensor(parts[:, m, w, 2, cols], qr[u % 2], parts[:, m, w, 1, cols], ALU.subtract).then_inc(parts_ready, 1)

            def maximum(l, g, i, h, p, width):
                n = sidx["s", l, g, i, h, p]
                dve.wait_ge(s_full, n + 1)
                dve.tensor_reduce(mx[:, h, i, p:p + 1], s_bank[n % len(S_BANKS)][:, 0:width], AX.X, ALU.max).then_inc(s_drained, 1)

            def split_max(l, g):
                n = sidx["mt", l, g]
                dve.wait_ge(s_drained, n)
                link(dve.tensor_reduce(negm[:], mx[:].rearrange("q h i p -> q (h i) p"), AX.X, ALU.max, negate=True))
                link(dve.tensor_copy(mparts[:, 0, :], negm[:]))
                link(dve.tensor_tensor(negr[:], negm[:], mparts[:, 0, :], ALU.subtract))
                link(dve.tensor_copy(mparts[:, 1, :], negr[:]))
                dve.tensor_tensor(mparts[:, 2, :], negr[:], mparts[:, 1, :], ALU.subtract).then_inc(mx_ready, 1)
                dve.wait_ge(s_full, n + 1)
                if NG * l + g:
                    loads = NG * l + g
                    before = (loads - 1) % NG
                    dve.wait_ge(m_loaded[before % NBUF], 16 * (1 + (before >= NBUF) + (loads > NG) * (1 + (before % NBUF + NBUF < NG))))
                rows = NP * HG * TT
                dve.tensor_copy(mT[0:rows, :], s_bank[n % len(S_BANKS)][0:rows, 0:P // 2].bitcast(BF16)).then_inc(s_drained, 1)

            def normalise(l, g, c):
                n = sidx["nm", l, g, c]
                dve.wait_ge(s_full, n + 1)
                dve.wait_ge(s_drained, n)
                src = s_bank[n % len(S_BANKS)].rearrange("q (t h v) -> q t h v", t=TPC, h=HG)
                link(dve.reciprocal(rec[:], src[:, :, :, DH]))
                dst = y[:, TPC * c:TPC * (c + 1), HG * DH * g:HG * DH * (g + 1)].rearrange("q t (h d) -> q t h d", h=HG)
                w = rec[:].rearrange("q t (h a) -> q t h a", a=1).broadcast_to([P, TPC, HG, DH])
                dve.tensor_tensor(dst, src[:, :, :, 0:DH], w, ALU.mult).then_inc(s_drained, 1)

            def add_to_x(tiles, pt, base, key):
                dve.tensor_tensor(x[:, tiles, :], pt.rearrange("p (t d) -> p t d", t=2), base[:, tiles, :], ALU.add)\
                    .then_inc(read_out(*key), 1)

            def settled(*keys):
                for key in keys:
                    bk, k = place[key]
                    dve.wait_ge(drained[bk], k + 1)

            def attention(l, src, pass_index):
                units = [(c, w) for c in range(NC) for w in range(2)]
                if l == 0:
                    for c in range(NC):
                        row_statistics(0, c, src)
                    for c in range(NC):
                        normalised(0, c, src)
                    for i, u in enumerate(units):
                        rest(0, 0, *u)
                        if i:
                            part2(0, 0, *units[i - 1])
                    part2(0, 0, *units[-1])
                else:
                    for c in range(NC):
                        normalised(2, c, src)
                    for u in units:
                        rest(1, 0, *u)
                        part2(1, 0, *u)
                held = []
                for kind, *key in first_scores():
                    if kind == "qk" and key[0] == 0:
                        rest(l, 1, *key)
                        part2(l, 1, *key)
                    elif kind == "qk":
                        held.append(key)
                    elif kind == "mt":
                        split_max(l, 0)
                    else:
                        g, i, h, p = key
                        if held and h >= 2 and i == TT - 1 and p == 0:
                            unit = held.pop(0)
                            rest(l, 1, *unit)
                            part2(l, 1, *unit)
                        maximum(l, 0, i, h, p, dict(score_parts(i))[p])
                for g in range(NG):
                    for kind, *key in group_order(g):
                        if kind == "mt":
                            split_max(l, g + 1)
                        elif kind == "nm":
                            normalise(l, *key)
                        elif kind == "s":
                            _, i, h, p = key
                            maximum(l, g + 1, i, h, p, dict(score_parts(i))[p])
                for c in range(NC):
                    normalise(l, NG - 1, c)
                if l == 0:
                    dve.wait_ge(stored, 16 * pass_index + 16)
                for c in range(NC):
                    pairs = range(TPC // 2 * c, TPC // 2 * (c + 1))
                    for tp in pairs:
                        pt = arrived(dve, "ao", l, tp)
                        add_to_x(slice(2 * tp, 2 * tp + 2), pt, src, ("ao", l, tp))
                    settled(*[("ao", l, tp) for tp in pairs])
                    row_statistics(2 * l + 1, c, x)
                for c in range(NC):
                    normalised(2 * l + 1, c, x)

            def entmax():
                def wide(v):
                    return v.rearrange("p (t a) -> p t a", a=1).broadcast_to([P, TT, E0])

                def every(v):
                    return v.rearrange("p (a k) -> p a k", a=1).broadcast_to([P, TT, E0])

                pt = arrived(dve, "logit")[:, 0:TT * E0].rearrange("p (t e) -> p t e", t=TT)
                link(dve.tensor_reduce(zsm[:, 0, :], pt, AX.X, ALU.add))
                link(dve.tensor_scalar(zsm[:, 0, :], zsm[:, 0, :], 1.0 / E0, None, ALU.mult))
                dve.tensor_tensor(zc[:], pt, wide(zsm[:, 0, :]), ALU.subtract).then_inc(read_out("logit"), 1)
                settled(("logit",))
                link(dve.tensor_tensor(zt[:], zc[:], zc[:], ALU.mult))
                link(dve.tensor_reduce(zsm[:, 1, :], zt[:], AX.X, ALU.add))
                ins = dve.tensor_scalar(zsm[:, 1, :], zsm[:, 1, :], 1.0 / E0, LN_EPS, ALU.mult, ALU.add)
                ins.then_inc(ent_var, 1)
                dve.wait_ge(ent_rstd, 1)
                link(dve.scalar_tensor_tensor(zc[:], zc[:], 0.5, wide(zsm[:, 2, :]), ALU.mult, ALU.mult))
                link(dve.tensor_reduce(zsm[:, 0, :], zc[:], AX.X, ALU.max))
                link(dve.tensor_tensor(zc[:], zc[:], wide(zsm[:, 0, :]), ALU.subtract))
                zs = cum[:, 0, 0:TT, :]
                for t in range(TT):
                    ins = dve.max(zs[:, t, 0:8], zc[:, t, :])
                link(ins)
                for t in range(TT):
                    ins = dve.match_replace(zt[:, t, :], zs[:, t, 0:8], zc[:, t, :], LOWEST)
                link(ins)
                for t in range(TT):
                    ins = dve.max(zs[:, t, 8:16], zt[:, t, :])
                link(ins)
                link(dve.tensor_tensor(cum[:, 0, TT:2 * TT, :], zs, zs, ALU.mult))
                a, nxt = cum[:, 0], (cum[:, 1], cum[:, 2])
                for r, s in enumerate((1, 2, 4, 8)):
                    z = nxt[r % 2]
                    dve.tensor_copy(z[:, :, 0:s], a[:, :, 0:s])
                    link(dve.tensor_tensor(z[:, :, s:E0], a[:, :, s:E0], a[:, :, 0:E0 - s], ALU.add))
                    a = z
                inv = kidx[:, 1, :].rearrange("p (a k) -> p a k", a=1).broadcast_to([P, 2 * TT, E0])
                m = cum[:, 1]
                link(dve.tensor_tensor(m, a, inv, ALU.mult))
                link(dve.tensor_tensor(zt[:], m[:, 0:TT, :], m[:, 0:TT, :], ALU.mult))
                link(dve.tensor_tensor(zt[:], zt[:], m[:, TT:2 * TT, :], ALU.subtract))
                link(dve.tensor_tensor(zt[:], zt[:], every(kidx[:, 1, :]), ALU.add))
                dve.tensor_scalar(zt[:], zt[:], 1e-34, None, ALU.max).then_inc(delta_ready, 1)
                dve.wait_ge(sqrt_ready, 1)
                tau = cum[:, 2, 0:TT, :]
                link(dve.tensor_tensor(tau, m[:, 0:TT, :], zt[:], ALU.subtract))
                link(dve.tensor_tensor(zu[:], tau, zs, ALU.is_le))
                link(dve.tensor_reduce(zsm[:, 3, :], zu[:], AX.X, ALU.add))
                link(dve.tensor_tensor(zu[:], every(kidx[:, 0, :]), wide(zsm[:, 3, :]), ALU.is_equal))
                link(dve.tensor_tensor(zu[:], zu[:], tau, ALU.mult))
                link(dve.tensor_reduce(zsm[:, 3, :], zu[:], AX.X, ALU.add))
                link(dve.tensor_tensor(zc[:], zc[:], wide(zsm[:, 3, :]), ALU.subtract))
                link(dve.tensor_scalar(zc[:], zc[:], 0.0, None, ALU.max))
                dve.tensor_tensor(zu[:], zc[:], zc[:], ALU.mult).then_inc(a_ready, 1)

            def gated(pt, bias, key, c, n, dst, src_key):
                settled((key, c))
                dve.scalar_tensor_tensor(dst, pt, bias[:, 0:1], gsb[2 * c + n], ALU.add, ALU.mult).then_inc(read_out(*src_key), 1)

            def first_ffn():
                entmax()
                for c in range(NC):
                    pt = arrived(dve, "h1", c)
                    gated(pt, bias1, "g1", c, 0, z1[c], ("h1", c))
                for c in range(NC):
                    pt = arrived(dve, "z2", c)
                    gated(pt, bias2, "g2", c, 1, z2[c], ("z2", c))
                    for tp in range(TPC // 2):
                        pt = arrived(dve, "fo", c, tp)
                        add_to_x(slice(TPC * c + 2 * tp, TPC * c + 2 * tp + 2), pt, x, ("fo", c, tp))
                    settled(*[("fo", c, tp) for tp in range(TPC // 2)])
                    row_statistics(2, c, x)

            def second_ffn():
                pt = arrived(dve, "route")[:, 0:TT * NE].rearrange("p (t e) -> p t e", t=TT)
                dve.tensor_copy(zc[:, :, 0:NE], pt).then_inc(read_out("route"), 1)
                settled(("route",))
                for t in range(TT):
                    ins = dve.max(zt[:, t, 0:8], zc[:, t, 0:NE])
                link(ins)
                dve.tensor_tensor(zsm[:, 0, :], zt[:, :, 1], zt[:, :, 0], ALU.subtract).then_inc(gap_ready, 1)
                dve.wait_ge(egap_ready, 1)
                link(dve.tensor_scalar(zsm[:, 1, :], zsm[:, 1, :], 1.0, None, ALU.add))
                link(dve.reciprocal(zsm[:, 2, :], zsm[:, 1, :]))
                link(dve.tensor_scalar(zsm[:, 2, :], zsm[:, 2, :], 1.0, None, ALU.is_ge))
                link(dve.tensor_tensor(gate[:], zc[:, :, 0:NE], zt[:, :, 0:1].broadcast_to([P, TT, NE]), ALU.is_ge))
                link(dve.tensor_tensor(gate[:], gate[:], zsm[:, 2, :].rearrange("p (t a) -> p t a", a=1)
                                       .broadcast_to([P, TT, NE]), ALU.mult))
                dve.tensor_reduce(gmax[:], gate[:].rearrange("p t e -> p (t e)"), AX.X, ALU.max).then_inc(gmax_ready, 1)

                def square(e, c):
                    u = NC * (0 if e == NE else e + 1) + c
                    dve.wait_ge(relu_ready, u + 1)
                    pt = arrived(dve, "he", e, c)
                    dve.scalar_tensor_tensor(hq[buffer_of(e, c)], pt, 0.0, hr[buffer_of(e, c)], ALU.max, ALU.mult)\
                        .then_inc(hq_ready, 1)
                    dve.wait_ge(hq_ready, u + 1)
                    dve.sem_inc(read_out("he", e, c), 1)

                def experts(which):
                    units = [(e, c) for e in which for c in range(NC)]
                    for u in range(len(units) + 1):
                        if u < len(units):
                            square(*units[u])
                        if not u:
                            continue
                        e, c = units[u - 1]
                        for tp in range(TPC // 2):
                            key = ("eo", e, c, tp)
                            pt = arrived(dve, *key)
                            t = TPC * c + 2 * tp
                            if e == NE:
                                add_to_x(slice(t, t + 2), pt, x, key)
                                continue
                            settled(("eo", e - 1 if e else NE, c, tp))
                            dve.scalar_tensor_tensor(x[:, t, :], pt[:, 0:D], gate[:, t, e:e + 1], x[:, t, :], ALU.mult, ALU.add)
                            dve.scalar_tensor_tensor(x[:, t + 1, :], pt[:, D:2 * D], gate[:, t + 1, e:e + 1], x[:, t + 1, :],
                                                     ALU.mult, ALU.add).then_inc(read_out(*key), 1)

                pt = arrived(dve, "any")
                link(dve.tensor_reduce(flag[:], pt[0:1, 0:P], AX.X, ALU.max))
                dve.tensor_copy(flag_i[:], flag[:]).then_inc(flag_ready, 1)
                experts([NE])
                dve.wait_ge(flag_ready, 1)
                routed = dve.value_load(flag_i[:], min_val=0, max_val=1)
                with dve.If(routed > 0):
                    experts(range(NE))
                dve.drain().then_inc(x_done, 1)

            with dve.Fori(0, B) as b:
                links = 0
                begin_pass(dve, b)
                dve.wait_ge(x_loaded, 16 * b + 16)
                attention(0, x_in, b)
                first_ffn()
                attention(1, x, b)
                second_ffn()
                dve.drain().then_inc(part_done, 1)


_INS = ['L0_attn_x', 'L0_attn_w_qkv', 'L0_attn_w_out', 'L0_ffn_proj', 'L0_ffn_C1', 'L0_ffn_Win1', 'L0_ffn_Wout1',
        'L0_ffn_C2', 'L0_ffn_Win2', 'L0_ffn_Wout2', 'L1_attn_Wq_down', 'L1_attn_Wk_down', 'L1_attn_Wv_down',
        'L1_attn_Wq_up_c', 'L1_attn_Wq_up_e', 'L1_attn_Wk_up_c', 'L1_attn_Wk_up_e', 'L1_attn_Wv_up', 'L1_attn_Wc',
        'L1_ffn_Ws1', 'L1_ffn_Ws2', 'L1_ffn_W1', 'L1_ffn_W2', 'L1_ffn_Wr']


def rope_tables():
    import numpy as np
    half = DH // 2
    inv = (1.0 / np.float32(10000.0) ** (np.arange(0, half, 2, dtype=np.float32) / np.float32(half))).astype(np.float32)
    freqs = np.arange(T, dtype=np.float32)[:, None] * inv[None, :]
    emb = np.concatenate((freqs, freqs), axis=-1).T
    cos = np.ones((DH, T), np.float32)
    sin = np.zeros((DH, T), np.float32)
    cos[half:] = np.cos(emb)
    sin[half:] = np.sin(emb)
    sin[half::2] *= -1.0
    return np.tile(cos, (MH, 1)), np.tile(sin, (MH, 1))


def kernel(**inputs):
    import numpy as np
    import concourse.bacc as bacc
    from concourse.bass_utils import run_bass_kernel_spmd

    nc = bacc.Bacc("TRN2", target_bir_lowering=False, num_devices=1)
    cos, sin = rope_tables()
    k = np.arange(1, E0 + 1, dtype=np.float32)
    arrays = {f"in_{name}": np.ascontiguousarray(inputs[name]) for name in _INS}
    arrays["cos_table"] = cos
    arrays["sin_table"] = sin
    arrays["k_table"] = np.ascontiguousarray(np.broadcast_to(np.stack([k, 1.0 / k]).astype(np.float32), (P, 2, E0)))
    args = [nc.dram_tensor(name, a.shape, mybir.dt.from_np(a.dtype), kind="ExternalInput").ap() for name, a in arrays.items()]
    out = nc.dram_tensor("out", (B, T, D), F32, kind="ExternalOutput").ap()
    transformer_kernel(nc, *args, out)
    r = run_bass_kernel_spmd(nc, [arrays], core_ids=[0])
    return r.results[0]["out"]
```

```python
import concourse.bass as bass
from concourse import mybir
from concourse.alu_op_type import AluOpType as ALU
from contextlib import ExitStack

F32 = mybir.dt.float32
BF16 = mybir.dt.bfloat16
ACT = mybir.ActivationFunctionType
AX = mybir.AxisListType

P = 128
BANK = 512
LN_EPS = 1e-5
NEG = -1.0e30
LOWEST = -3.0e38

B, T, D = 8, 1024, 256
H = 16
DH = D // H
TT = T // P
KD = D // P
NC = T // BANK
TPC = TT // NC
L = 64
E0, R, O = 16, 128, 1024
OC = O // P
NE, FE = 8, 128
HG = 4
NG = H // HG
MH = P // DH
SCALE = DH ** -0.5

NP = 3
ROWS_A = DH * 2 * NP
ROWS_S = ROWS_A + DH
ROWS = ROWS_S + NP
STACK_DMAS = 5
NBUF = 3

PBUF = 4
TURN = 4
AHEAD = (14, 20, 24)
SHARE = 10
LAG = 2
EARLY_BANKS = (0, 1, 2, 3, 4, 5)
PROJ_BANKS = (0, 1, 2)
S_BANKS = (3, 4, 5)
O_BANKS = (6, 7)
FFN_BANKS = (0, 1, 2, 3, 4)
H_BANK = 5
LN_TURN = {1: 0, 2: 1, 4: 2, 3: 3}
FOLD_LOADS = 2 + 3 + 2 * 5
HID_LAG = 3


def score_parts(i):
    return [(p, min(BANK, P * (i + 1) - BANK * p)) for p in range(NC) if P * (i + 1) > BANK * p]


def query_range(j, c):
    return max(P * j, BANK * c), BANK * (c + 1)


def key_tiles(c):
    return range(TPC * (c + 1))


def score_keys(g, c):
    tiles = list(reversed(range(TPC * c, TPC * (c + 1))))
    pairs = [(i, h) for h in range(HG) for i in tiles] if g == 0 else [(i, h) for i in tiles for h in range(HG)]
    return [("s", g, c, i, h, p) for i, h in pairs for p, _ in score_parts(i)]


def woven(main, others):
    def work(item):
        kind, *key = item
        if kind == "s":
            g, c, i, h, p = key
            return dict(score_parts(i))[p] + 60
        if kind == "st":
            g, c, j, h = key
            a, z = query_range(j, c)
            return z - a
        if kind == "pv":
            g, c, j = key
            a, z = query_range(j, c)
            return HG * (z - a)
        return {"v": 2000, "qk": 2000}.get(kind, 0)

    whole, part = sum(map(work, main)), sum(map(work, others))
    order, others, passed, given = [], list(others), 0, 0
    for item in main:
        while others and given * whole <= passed * part:
            order.append(others.pop(0))
            given += work(order[-1])
        order.append(item)
        passed += work(item)
    return order + others


def attention_order(l):
    units = [(g, c) for g in range(NG) for c in range(NC)]

    def scores(*which):
        items, turn = [], []
        for u in which:
            keys = score_keys(*u)
            items += keys[:TURN] + turn + keys[TURN:] + [("mx", *u)]
            turn = [("mt", *u)]
        return items, turn

    def steps(which):
        items = []
        for u in which:
            for j in key_tiles(u[1]):
                items += [("st", *u, j, h) for h in range(HG // 2)]
                held.append(("pv", *u, j))
                if len(held) > LAG:
                    items.append(held.pop(0))
                items += [("st", *u, j, h) for h in range(HG // 2, HG)]
                if u != units[0] and j == LAG - 1:
                    items.append(("o", *units[units.index(u) - 1]))
                if u == units[1] and j < len(late):
                    items += split(late[j], 1)
                if u != units[0] and j == LAG:
                    items.append(("nm", *units[units.index(u) - 1]))
                if u == units[-1]:
                    items += end.get(j, [])
        return items

    def split(stage, c, m=1):
        return [(stage, m, c, w) for w in range(2)]

    held = []
    end = {0: [("next",)] if l else [], LAG + 1: [("yt", 0)], LAG + 2: [("ao", 0)], TT - 2: [("rstd", 2 * l + 1, 0), ("norm", 2 * l + 1, 0)]}
    late = ("swap", "add", "rest", "last") if l else ("rest", "last")
    values = [("v", tp) for tp in range(TT // 2)]
    others = [("qk", 1, c, w) for c in range(NC) for w in range(2)]
    first, turn = scores(units[0])
    order = [] if l else [("xt", 0, 0)]
    order += [("qk", 0, 0, w) for w in range(2)] + split("swap", 0, 0) + values[:2]
    order += [("xt", 2 * l, 1)] + split("add", 0, 0) + split("rest", 0, 0) + [("qk", 0, 1, w) for w in range(2)]
    order += split("last", 0, 0)
    for stage in ("swap", "add", "rest", "last"):
        order += split(stage, 1, 0)
    order += woven(first, values[2:])
    second = score_keys(*units[1])
    order += second[:TURN] + turn + woven(second[TURN:AHEAD[0]], others) + split("swap", 0)
    order += woven(steps(units[:1]), second[AHEAD[0]:AHEAD[1]] + split("add", 0) + second[AHEAD[1]:AHEAD[2]] + split("rest", 0)
                   + second[AHEAD[2]:] + [("mx", *units[1])] + split("last", 0) + ([] if l else split("add", 1)))
    later, turn = scores(*units[2:])
    later = later[:TURN] + [("mt", *units[1])] + later[TURN:]
    lead = len(score_keys(*units[2])) + 2
    order += later[:lead]
    among, rest = steps(units[1:-2]), steps(units[-2:-1])
    order += woven(among + rest[:SHARE], later[lead:] + turn) + rest[SHARE:] + steps(units[-1:])
    return order + held + [("o", *units[-1]), ("nm", *units[-1])]


def first_ffn_order():
    def hidden(c, blocks):
        return [("hid", c, o) for o in blocks]

    blocks = range(OC + HID_LAG)
    return ([("xt", 1, 0), ("yt", 1), ("logit", 0), ("h1", 0), ("tau", 0), ("ao", 1), ("rstd", 1, 1), ("norm", 1, 1),
             ("at", 0), ("g", 0), ("z1", 0)]
            + hidden(0, blocks[:2]) + [("xt", 1, 1), ("logit", 1)] + hidden(0, blocks[2:OC]) + [("tau", 1)] + hidden(0, blocks[OC:])
            + [("z2", 0), ("h1", 1), ("at", 1), ("g", 1), ("z1", 1), ("fo", 0), ("rstd", 2, 0), ("norm", 2, 0)]
            + hidden(1, blocks) + [("z2", 1), ("xt", 2, 0), ("fo", 1), ("rstd", 2, 1), ("norm", 2, 1)])


def second_ffn_order():
    return [("xt", 3, 0), ("yt", 1), ("route", 0), ("ao", 1), ("rstd", 3, 1), ("up", NE, 0), ("norm", 3, 1), ("norm", 4, 0),
            ("down", NE, 0), ("xt", 3, 1), ("norm", 4, 1), ("up", NE, 1), ("route", 1), ("down", NE, 1), ("any",)]


PASS = [(l, *step) for l in range(2) for step in attention_order(l) + (second_ffn_order() if l else first_ffn_order())]
ROUTED = [(e, c) for e in range(NE) for c in range(NC)]


def plan_banks():
    place, used, before = {}, [0] * 8, {}
    banks, turn = EARLY_BANKS, 0

    def put(key, bank):
        place[key] = (bank, used[bank])
        used[bank] += 1

    def ring(*key):
        nonlocal turn
        put(key, banks[turn % len(banks)])
        turn += 1

    def expert_units(kind, e, c):
        if kind == "up":
            ring("he", e, c)
        else:
            for tp in range(TPC // 2):
                ring("eo", e, c, tp)

    last = (NG - 1, NC - 1)
    for l, kind, *key in PASS:
        if kind in ("s", "st") and (l, kind) not in before:
            before[l, kind] = list(used)
            banks, turn = (PROJ_BANKS if kind == "s" else S_BANKS), 0
        if kind == "nm" and tuple(key) == last:
            before[l, "nm"] = list(used)
            banks, turn = FFN_BANKS, 0
        if kind in ("xt", "yt"):
            if kind == "xt" and key == [2, 1]:
                banks, turn = EARLY_BANKS, 0
            for kd in range(KD):
                ring(kind, *(key if kind == "xt" else (l, *key)), kd)
        elif kind in ("qk", "v"):
            ring(kind, l, *key)
        elif kind in ("ao", "fo"):
            for tp in range(TPC // 2):
                ring(kind, l, *key, tp)
        elif kind == "h1":
            put(("h1", *key), H_BANK)
        elif kind == "g":
            ring("g1", *key)
            ring("g2", *key)
        elif kind == "hid" and key[1] < OC:
            ring("hid", *key)
        elif kind == "z2":
            put(("z2", *key), O_BANKS[key[0]])
        elif kind in ("logit", "at", "route"):
            ring(kind, *key)
        elif kind in ("up", "down"):
            expert_units(kind, *key)
        elif kind == "any":
            put(("any",), H_BANK)
    for u in range(len(ROUTED) + 1):
        if u < len(ROUTED):
            expert_units("up", *ROUTED[u])
        if u:
            expert_units("down", *ROUTED[u - 1])
    return place, before


def plan_scores():
    index, t_index, step_index, diagonal_index, unit_index = {}, {}, {}, {}, {}
    for l, kind, *key in PASS:
        if kind in ("s", "mt", "nm"):
            index[(kind, l, *key)] = len(index)
        elif kind == "st":
            g, c, j, h = key
            t_index[l, g, c, j, h] = len(t_index)
            if h == 0:
                step_index[l, g, c, j] = len(step_index)
                if j // TPC == c:
                    diagonal_index[l, g, c, j] = len(diagonal_index)
                if j == 0:
                    unit_index[l, g, c] = len(unit_index)
    return index, t_index, step_index, diagonal_index, unit_index


def transformer_kernel(nc, x_d, w_qkv_d, w_out_d, proj_d, c1_d, win1_d, wout1_d, c2_d, win2_d, wout2_d,
                       wqd_d, wkd_d, wvd_d, wquc_d, wque_d, wkuc_d, wkue_d, wvu_d, wc_d,
                       ws1_d, ws2_d, w1_d, w2_d, wr_d, cos_d, sin_d, kidx_d, out_d):
    place, filled_before = plan_banks()
    sidx, tidx, step_of, diagonal_of, unit_of = plan_scores()
    ctx = ExitStack()
    with ctx:
        def sb(name, shape, dt=F32):
            return ctx.enter_context(nc.sbuf_tensor(name, shape, dt))

        x_in = sb("x_in", [P, TT, D])
        x = sb("x", [P, TT, D])
        xn = sb("xn", [P, TT, D])
        xnT = sb("xnT", [P, KD, T])
        y, yT = xn, xnT
        parts = sb("parts", [P, 2, 2, NP, T], BF16)
        stk = sb("stk", [P, NBUF, 2, HG, T], BF16)
        probs = sb("probs", [P, PBUF, HG, BANK])
        vaug = sb("vaug", [P, TT, H, DH + 1])
        oT = sb("oT", [P, T])
        mx = sb("mx", [P, HG, TT, 2])
        negm = sb("negm", [P, TPC, HG])
        negr = sb("negr", [P, TPC, HG])
        mparts = sb("mparts", [P, TPC, NP, HG], BF16)
        mT = sb("mT", [NP * HG, BANK], BF16)
        rec = sb("rec", [P, TPC, HG])
        st6 = sb("st6", [P, TT, 6])
        stats = [(sb(f"mv{i}", [P, TT, 2]), sb(f"veps{i}", [P, TT]), sb(f"rstd{i}", [P, TT]))
                 for i in range(2)]
        neg_half = sb("neg_half", [P, TT])
        wqkv = [sb(f"wqkv{l}", [P, KD, 3 * D]) for l in range(2)]
        wo = [sb(f"wo{l}", [P, KD, D]) for l in range(2)]
        projw = sb("projw", [P, KD, E0])
        c12 = sb("c12", [E0, 2, R])
        win1 = sb("win1", [P, KD, R])
        bias1 = sb("bias1", [P, 1])
        wout1T = sb("wout1T", [R, O])
        win2 = sb("win2", [P, OC, R])
        bias2 = sb("bias2", [P, 1])
        wout2T = sb("wout2T", [R, D])
        wr = sb("wr", [P, KD, NE])
        w1 = sb("w1", [P, NE + 1, KD, FE])
        w2 = sb("w2", [P, NE + 1, D])
        cos = sb("cos", [P, T])
        sin = sb("sin", [P, T])
        ident = sb("ident", [P, P])
        ident_b = sb("ident_b", [P, P], BF16)
        mask_b = sb("mask_b", [P, P], BF16)
        kidx = sb("kidx", [P, 2, E0])
        zsm = sb("zsm", [P, 4, TT])
        zc = sb("zc", [P, TT, E0])
        zt = sb("zt", [P, TT, E0])
        zu = sb("zu", [P, TT, E0])
        cum = oT[:, 0:3 * 2 * TPC * E0].rearrange("p (a t k) -> p a t k", a=3, k=E0)
        gate = sb("gate", [P, TT, NE])
        gmax = sb("gmax", [P, 1])
        flag = sb("flag", [1, 1])
        flag_i = sb("flag_i", [1, 1], mybir.dt.int32)
        flat = probs[:, :, :, :].rearrange("p a h t -> p (a h t)")
        scratch = [flat[:, BANK * i:BANK * (i + 1)] for i in range(16)]
        spare = stk[:, NBUF - 1, 0].rearrange("p h t -> p (h t)").bitcast(F32)
        flat_x = xn[:].rearrange("p t d -> p (t d)")
        qf = scratch[0:2] + scratch[8:10] + [spare[:, BANK * i:BANK * (i + 1)] for i in range(4)]
        qs = scratch[2:4] + scratch[10:12] + [flat_x[:, BANK * (i % 2):BANK * (i % 2 + 1)] for i in range(4)]
        qc = scratch[14:16] + scratch[12:14] + [flat_x[:, BANK * (2 + i % 2):BANK * (3 + i % 2)] for i in range(4)]
        aT = flat[0:E0, 0:T]
        gsb = [scratch[2 + i] for i in range(4)]
        z1 = scratch[6:8]
        hsb = scratch[8:12]
        z2 = scratch[12:14]
        hr = scratch[0:4]
        hq = scratch[4:8]
        down = flat[:, 0:3 * KD * H * L].rearrange("p (w k n) -> p w k n", w=3, k=KD)
        dT = [stk[:, w, 0].rearrange("p h t -> p (h t)").bitcast(F32)[:, 0:H // 2 * D].rearrange("p (i d) -> p i d", d=D)
              for w in range(3)]
        stage = parts[:].rearrange("p m q n t -> p (m q n t)").bitcast(F32)
        ends = [0]

        def staged(blocks, width):
            ends.append(ends[-1] + blocks * width)
            return stage[:, ends[-2]:ends[-1]].rearrange("p (b n) -> p b n", b=blocks)

        wo1_s, wo2_s = staged(OC, R), staged(KD, R)
        up = staged(3, 2 * DH)

        ps = ctx.enter_context(nc.psum_tensor("ps", [P, 8 * BANK], F32))
        bank = [ps[:, BANK * b:BANK * (b + 1)] for b in range(8)]
        st_bank = [bank[b] for b in PROJ_BANKS]
        s_bank = [bank[b] for b in S_BANKS]
        o_bank = [bank[b] for b in O_BANKS]

        def sem(name):
            return ctx.enter_context(nc.semaphore(name))

        up_zeroed = sem("up_zeroed")
        fold_loaded = sem("fold_loaded")
        w_loaded = sem("w_loaded")
        w_const = sem("w_const")
        w_full = sem("w_full")
        w_drained = sem("w_drained")
        x_loaded = sem("x_loaded")
        stored = sem("stored")
        next_pass = sem("next_pass")
        first = part_done = sem("part_done")
        begun = sem("begun")
        full = [sem("full0")] + [sem(f"full{b}") for b in range(1, 8)]
        drained = [sem(f"drained{b}") for b in range(8)]
        ln_var = sem("ln_var")
        ln_rstd = sem("ln_rstd")
        xn_ready = sem("xn_ready")
        part0_ready = sem("part0_ready")
        rest_ready = sem("rest_ready")
        part1_ready = sem("part1_ready")
        parts_ready = sem("parts_ready")
        swap_ready = sem("swap_ready")
        cos_ready = sem("cos_ready")
        sin_ready = sem("sin_ready")
        gmax_ready = sem("gmax_ready")
        flag_ready = sem("flag_ready")
        rope_ready = sem("rope_ready")
        first_loaded = [[sem(f"first_loaded{c}_{h}") for h in range(HG)] for c in range(NC)]
        stk_loaded = [None] + [[sem(f"stk_loaded{g}_{h}") for h in range(HG)] for g in range(1, NG)]
        m_loaded = sem("m_loaded")
        s_full = sem("s_full")
        s_drained = sem("s_drained")
        mx_ready = sem("mx_ready")
        st_full = sem("st_full")
        exp_done = sem("exp_done")
        p_ready = sem("p_ready")
        pv_done = sem("pv_done")
        o_drained = sem("o_drained")
        ent_var = sem("ent_var")
        ent_rstd = sem("ent_rstd")
        delta_ready = sem("delta_ready")
        sqrt_ready = sem("sqrt_ready")
        a_ready = sem("a_ready")
        h_used = sem("h_used")
        gap_ready = sem("gap_ready")
        egap_ready = sem("egap_ready")
        relu_ready = sem("relu_ready")
        hq_ready = sem("hq_ready")
        x_done = sem("x_done")
        act_chain = sem("act_chain")
        last = dve_chain = sem("dve_chain")
        pass_sems = range(first.num, last.num + 1)

        def arrived(eng, *key):
            b, n = place[key]
            eng.wait_ge(full[b], n + 1)
            return bank[b]

        def begin_pass(eng, b):
            eng.wait_ge(next_pass, b + 1)
            eng.sem_inc(begun, 1)

        def buffer_of(e, c):
            return (NC * (0 if e == NE else e + 1) + c) % 4

        def read_out(*key):
            return drained[place[key][0]]

        block = ctx.enter_context(nc.Block())

        @block.sync
        def _(sp):
            half = DH // 2
            downs = [(wo1_s, wout1_d.rearrange("(o p) r -> p o r", p=P)),
                     (wo2_s, wout2_d.rearrange("(o p) r -> p o r", p=P))]
            downs += [(down[:, w], d.rearrange("(k p) n -> p k n", p=P)) for w, d in enumerate((wqd_d, wkd_d, wvd_d))]
            ups = []
            for odd in range(2):
                block = up[L * odd:L * (odd + 1), :, DH * odd:DH * (odd + 1)]
                ups += [(block[:, 0, 0:half], wquc_d), (block[:, 0, half:DH], wque_d),
                        (block[:, 1, 0:half], wkuc_d), (block[:, 1, half:DH], wkue_d), (block[:, 2], wvu_d)]
            loads = [
                (wqkv[0][:], w_qkv_d.rearrange("(k p) n -> p k n", p=P)),
                (wo[0][:], w_out_d.rearrange("(k p) n -> p k n", p=P)),
                (projw[:], proj_d.rearrange("(k p) n -> p k n", p=P)),
                (c12[:, 0], c1_d), (c12[:, 1], c2_d),
                (win1[:], win1_d[0:D, :].rearrange("(k p) r -> p k r", p=P)),
                (bias1[:], win1_d[D:D + 1, :].rearrange("a r -> r a")),
                (win2[:], win2_d[0:O, :].rearrange("(o p) r -> p o r", p=P)),
                (bias2[:], win2_d[O:O + 1, :].rearrange("a r -> r a")),
                (wo[1][:], wc_d.rearrange("(k p) n -> p k n", p=P)),
                (wr[:], wr_d.rearrange("(k p) n -> p k n", p=P)),
                (w1[:, NE], ws1_d.rearrange("(k p) f -> p k f", p=P)),
                (w2[:, NE], ws2_d),
                (cos[:], cos_d), (sin[:], sin_d), (kidx[:], kidx_d),
            ]
            for e in range(NE):
                loads.append((w1[:, e], w1_d[e].rearrange("(k p) f -> p k f", p=P)))
                loads.append((w2[:, e], w2_d[e]))
            for dst, src in downs:
                sp.dma_start(dst, src).then_inc(fold_loaded, 16)
            sp.wait_ge(up_zeroed, 1)
            for dst, src in ups:
                sp.dma_start(dst, src).then_inc(fold_loaded, 16)
            sp.dma_start(x_in[:], x_d[0].rearrange("(t p) d -> p t d", p=P)).then_inc(x_loaded, 16)
            for dst, src in loads:
                sp.dma_start(dst, src).then_inc(w_loaded, 16)
            sp.wait_ge(w_loaded, 16 * len(loads))
            sp.sem_inc(stored, 16)
            sp.wait_ge(part_done, 4)
            sp.sem_clear(pass_sems)
            sp.sem_inc(next_pass, 1)

            def load_head(l, g, h, cols, loaded):
                m, buf = g // 2, g % NBUF
                rows = slice(DH * ((g % 2) * HG + h), DH * ((g % 2) * HG + h + 1))
                ends = parts[rows, m, :, :, cols].rearrange("d w p t -> d (w p) t")[:, 0:2 * NP:2 * NP - 1, :]
                for t in range(2):
                    block = slice(DH * NP * t, DH * NP * (t + 1))
                    k = parts[rows, m, 1, t:t + 1, cols].broadcast_to([DH, NP, cols.stop - cols.start])
                    sp.dma_start(stk[block, buf, 0, h, cols], parts[rows, m, 0, :, cols]).then_inc(loaded, 16)
                    sp.dma_start(stk[block, buf, 1, h, cols], k).then_inc(loaded, 16)
                sp.dma_start(stk[ROWS_A:ROWS_S, buf, :, h, cols], ends).then_inc(loaded, 16)

            def load_first(l):
                if l:
                    sp.wait_ge(st_full, tidx[0, NG - 1, NC - 1, TT - 1, HG - 1] + 1)
                for c in range(NC):
                    sp.wait_ge(parts_ready, 8 * l + 2 * (c + 1))
                    for h in range(HG):
                        load_head(l, 0, h, slice(BANK * c, BANK * (c + 1)), first_loaded[c][h])

            def load_stack(l, g):
                sp.wait_ge(parts_ready, 8 * l + 4 * (g // 2 + 1))
                if NG * l + g >= NBUF:
                    done = NG * l + g - NBUF
                    sp.wait_ge(st_full, tidx[done // NG, done % NG, NC - 1, TT - 1, HG - 1] + 1)
                for h in range(HG):
                    load_head(l, g, h, slice(0, T), stk_loaded[g][h])

            def load_max(l, g, c):
                sp.wait_ge(s_drained, sidx["mt", l, g, c] + 1)
                sp.dma_start(stk[ROWS_S:ROWS, g % NBUF, 0, :, BANK * c:BANK * (c + 1)], mT[:]).then_inc(m_loaded, 16)

            with sp.Fori(0, B) as b:
                for l in range(2):
                    load_first(l)
                    load_max(l, 0, 0)
                    load_stack(l, 1)
                    load_max(l, 0, 1)
                    load_max(l, 1, 0)
                    load_stack(l, 2)
                    load_max(l, 1, 1)
                    load_max(l, 2, 0)
                    load_stack(l, 3)
                    load_max(l, 2, 1)
                    for c in range(NC):
                        load_max(l, 3, c)
                    if l == 0:
                        for c in range(NC):
                            for tp in range(TPC // 2):
                                bk, n = place["ao", 0, c, tp]
                                sp.wait_ge(drained[bk], n + 1)
                        sp.dma_start(x_in[:], x_d[(b + 1) % B].rearrange("(t p) d -> p t d", p=P)).then_inc(x_loaded, 16)
                sp.wait_ge(x_done, 1)
                sp.dma_start(out_d[b].rearrange("(t p) d -> p t d", p=P), x[:]).then_inc(stored, 16)
                sp.wait_ge(part_done, 4)
                sp.sem_clear(pass_sems)
                sp.sem_inc(next_pass, 1)
            sp.wait_ge(stored, 16 * (B + 1))
            sp.wait_ge(x_loaded, 16 * (B + 1))

        @block.tensor
        def _(pe):
            def claim(*key):
                b, n = place[key]
                if n:
                    pe.wait_ge(drained[b], n)
                return bank[b], full[b]

            def in_sbuf(*key):
                b, n = place[key]
                pe.wait_ge(drained[b], n + 1)

            pe.wait_ge(w_const, 1)
            pe.wait_ge(fold_loaded, 16 * FOLD_LOADS)
            unit = 0

            def setup_bank():
                nonlocal unit
                if unit >= 4:
                    pe.wait_ge(w_drained, unit - 3)
                unit += 1
                return bank[(unit - 1) % 4]

            for u in range(2):
                pt = setup_bank()
                for i in range(4):
                    ins = pe.transpose(pt[:, P * i:P * (i + 1)], wo1_s[:, 4 * u + i, :], ident[:])
                ins.then_inc(w_full, 1)
            pt = setup_bank()
            for i in range(KD):
                ins = pe.transpose(pt[:, P * i:P * (i + 1)], wo2_s[:, i, :], ident[:])
            ins.then_inc(w_full, 1)
            for w in range(3):
                for u in range(4):
                    pt = setup_bank()
                    for i in range(4):
                        blk = 2 * u + i // KD
                        ins = pe.transpose(pt[:, P * i:P * (i + 1)], down[:, w, i % KD, P * blk:P * (blk + 1)], ident[:])
                    ins.then_inc(w_full, 1)
            for w in range(3):
                pe.wait_ge(w_drained, 3 + 4 * (w + 1))
                pt = setup_bank()
                for kd in range(KD):
                    for i in range(H // 2):
                        col = D * kd + 2 * DH * i
                        ins = pe.matmul(pt[:, col:col + 2 * DH], dT[w][:, i, P * kd:P * (kd + 1)], up[:, w, :],
                                        start=True, stop=True)
                ins.then_inc(w_full, 1)
            pe.drain().then_inc(part_done, 1)

            def transposed_x(s, c):
                if s:
                    pe.wait_ge(xn_ready, NC * (s - 1) + c + 1)
                for kd in range(KD):
                    pt, done = claim("xt", s, c, kd)
                    for i in range(TPC):
                        ins = pe.transpose(pt[:, P * i:P * (i + 1)], xn[:, TPC * c + i, P * kd:P * (kd + 1)], ident[:])
                    ins.then_inc(done, 1)

            def need_xT(s, c):
                for kd in range(KD):
                    in_sbuf("xt", s, c, kd)

            def project_qk(l, m, c, w):
                pt, done = claim("qk", l, m, c, w)
                for kd in range(KD):
                    ins = pe.matmul(pt, wqkv[l][:, kd, D * w + P * m:D * w + P * (m + 1)],
                                    xnT[:, kd, BANK * c:BANK * (c + 1)], start=kd == 0, stop=kd == KD - 1)
                ins.then_inc(done, 1)

            def by_token(pt, left, right, tiles, n_k):
                for i, t in enumerate(tiles):
                    for kd in range(n_k):
                        ins = pe.matmul(pt[:, D * i:D * (i + 1)], left(kd, t), right(kd), start=kd == 0, stop=kd == n_k - 1)
                return ins

            def score_unit(l, g, c, i, h, p, width):
                n, buf = sidx["s", l, g, c, i, h, p], g % NBUF
                if n >= len(S_BANKS):
                    pe.wait_ge(s_drained, n - len(S_BANKS) + 1)
                out = s_bank[n % len(S_BANKS)][:, 0:width]
                lhsT = stk[0:ROWS_S, buf, 0, h, P * i:P * (i + 1)]
                diagonal = BANK * p + width == P * (i + 1)
                ins = pe.matmul(out, lhsT, stk[0:ROWS_S, buf, 1, h, BANK * p:BANK * p + width], start=True, stop=not diagonal)
                if diagonal:
                    ins = pe.matmul(out[:, width - P:width], ident_b[:], mask_b[:], start=False, stop=True)
                ins.then_inc(s_full, 1)

            def score(l, g, c, i, h, p):
                if g == 0 and i == TPC * (c + 1) - 1 and p == 0:
                    pe.wait_ge(first_loaded[c][h], STACK_DMAS * 16 * (l + 1))
                elif g and i == TPC - 1:
                    pe.wait_ge(stk_loaded[g][h], STACK_DMAS * 16 * (l + 1))
                score_unit(l, g, c, i, h, p, dict(score_parts(i))[p])

            def max_rows(l, g, c):
                n = sidx["mt", l, g, c]
                pe.wait_ge(s_drained, n - len(S_BANKS) + 1)
                pe.wait_ge(mx_ready, unit_of[l, g, c] + 1)
                rows = s_bank[n % len(S_BANKS)][0:NP * HG, 0:BANK // 2].bitcast(BF16)
                for i in range(TPC):
                    ins = pe.transpose(rows[:, P * i:P * (i + 1)], mparts[:, i].rearrange("q p h -> q (p h)"), ident_b[:])
                ins.then_inc(s_full, 1)

            def normalise(l, g, c):
                n = sidx["nm", l, g, c]
                pe.wait_ge(s_drained, n - len(S_BANKS) + 1)
                if (g, c) == (NG - 1, NC - 1):
                    b = S_BANKS[n % len(S_BANKS)]
                    pe.wait_ge(drained[b], filled_before[l, "nm"][b])
                pe.wait_ge(o_drained, unit_of[l, g, c] + 1)
                for i in range(TPC):
                    t = TPC * c + i
                    ins = pe.transpose(s_bank[n % len(S_BANKS)][:, P * i:P * (i + 1)], oT[:, P * t:P * (t + 1)], ident[:])
                ins.then_inc(s_full, 1)

            def scores_t(l, g, c, j, h):
                n, buf = tidx[l, g, c, j, h], g % NBUF
                if j == 0 and h == 0:
                    pe.wait_ge(m_loaded, 16 * (unit_of[l, g, c] + 1))
                if n >= len(st_bank):
                    pe.wait_ge(exp_done, n - len(st_bank) + 1)
                a, z = query_range(j, c)
                pe.matmul(st_bank[n % len(st_bank)][:, a - BANK * c:z - BANK * c], stk[0:ROWS, buf, 1, h, P * j:P * (j + 1)],
                          stk[0:ROWS, buf, 0, h, a:z], start=True, stop=True).then_inc(st_full, 1)

            def weigh_values(l, g, c, j):
                if j // TPC == c:
                    pe.wait_ge(p_ready, HG * (diagonal_of[l, g, c, j] + 1))
                else:
                    pe.wait_ge(exp_done, tidx[l, g, c, j, HG - 1] + 1)
                if j == 0 and unit_of[l, g, c] >= NC:
                    pe.wait_ge(o_drained, unit_of[l, g, c] - NC + 1)
                a, z = query_range(j, c)
                for h in range(HG):
                    ins = pe.matmul(o_bank[c][32 * h:32 * h + DH + 1, a - BANK * c:z - BANK * c],
                                    vaug[:, j, HG * g + h, :], probs[:, step_of[l, g, c, j] % PBUF, h, a - BANK * c:z - BANK * c],
                                    start=j == 0, stop=j == TPC * (c + 1) - 1)
                ins.then_inc(pv_done, 1)

            def banks_read(l, kind, banks):
                for b in banks:
                    if filled_before[l, kind][b]:
                        pe.wait_ge(drained[b], filled_before[l, kind][b])

            def values(l, tp):
                need_xT(2 * l, 2 * tp // TPC)
                pt, done = claim("v", l, tp)
                by_token(pt, lambda kd, t: xnT[:, kd, P * t:P * (t + 1)], lambda kd: wqkv[l][:, kd, 2 * D:3 * D],
                         (2 * tp, 2 * tp + 1), KD).then_inc(done, 1)

            def transposed_y(l, c):
                if c == 0:
                    pe.wait_ge(s_drained, sidx["nm", l, NG - 1, 0] + 1)
                else:
                    pe.wait_ge(s_drained, sidx["nm", l, NG - 1, c] + 1)
                for kd in range(KD):
                    pt, done = claim("yt", l, c, kd)
                    for i in range(TPC):
                        ins = pe.transpose(pt[:, P * i:P * (i + 1)], y[:, TPC * c + i, P * kd:P * (kd + 1)], ident[:])
                    ins.then_inc(done, 1)

            def project_y(l, c):
                for kd in range(KD):
                    in_sbuf("yt", l, c, kd)
                for tp in range(TPC // 2):
                    pt, done = claim("ao", l, c, tp)
                    t = TPC * c + 2 * tp
                    by_token(pt, lambda kd, t: yT[:, kd, P * t:P * (t + 1)], lambda kd: wo[l][:, kd, :], (t, t + 1), KD)\
                        .then_inc(done, 1)

            def small_product(name, s, c, w, width):
                need_xT(s, c)
                pt, done = claim(name, c)
                for i in range(TPC):
                    t = TPC * c + i
                    for kd in range(KD):
                        ins = pe.matmul(pt[:, width * i:width * (i + 1)], xnT[:, kd, P * t:P * (t + 1)], w[:, kd, :],
                                        start=kd == 0, stop=kd == KD - 1)
                ins.then_inc(done, 1)

            def first_product(c):
                pt, done = claim("h1", c)
                for kd in range(KD):
                    ins = pe.matmul(pt, win1[:, kd, :], xnT[:, kd, BANK * c:BANK * (c + 1)], start=kd == 0, stop=kd == KD - 1)
                ins.then_inc(done, 1)

            def transposed_a(c):
                pe.wait_ge(a_ready, c + 1)
                pt, done = claim("at", c)
                for i in range(TPC):
                    ins = pe.transpose(pt[0:E0, P * i:P * (i + 1)], zu[:, TPC * c + i, :], ident[:])
                ins.then_inc(done, 1)

            def gates(c):
                in_sbuf("at", c)
                for n, name in enumerate(("g1", "g2")):
                    pt, done = claim(name, c)
                    pe.matmul(pt, c12[:, n, :], aT[:, BANK * c:BANK * (c + 1)], start=True, stop=True).then_inc(done, 1)

            def hidden(c, o):
                if o == 0:
                    in_sbuf("h1", c)
                if o < OC:
                    pt, done = claim("hid", c, o)
                    pe.matmul(pt, wout1T[:, P * o:P * (o + 1)], z1[c], start=True, stop=True).then_inc(done, 1)
                if o >= HID_LAG:
                    k = o - HID_LAG
                    acc, done = claim("z2", c)
                    in_sbuf("hid", c, k)
                    ins = pe.matmul(acc, win2[:, k, :], hsb[k % 4], start=k == 0, stop=k == OC - 1)
                    ins.then_inc(h_used if k < OC - 1 else done, 1)

            def last_product(c):
                in_sbuf("z2", c)
                for tp in range(TPC // 2):
                    pt, done = claim("fo", 0, c, tp)
                    by_token(pt, lambda kd, t: z2[c][:, P * t:P * (t + 1)], lambda kd: wout2T[:], (2 * tp, 2 * tp + 1), 1)\
                        .then_inc(done, 1)

            def expert_up(e, c):
                need_xT(3, c)
                pt, done = claim("he", e, c)
                for kd in range(KD):
                    ins = pe.matmul(pt, w1[:, e, kd, :], xnT[:, kd, BANK * c:BANK * (c + 1)], start=kd == 0, stop=kd == KD - 1)
                ins.then_inc(done, 1)

            def expert_down(e, c):
                in_sbuf("he", e, c)
                for tp in range(TPC // 2):
                    pt, done = claim("eo", e, c, tp)
                    by_token(pt, lambda kd, t: hq[buffer_of(e, c)][:, P * t:P * (t + 1)], lambda kd: w2[:, e, :],
                             (2 * tp, 2 * tp + 1), 1).then_inc(done, 1)

            def largest_gate():
                pe.wait_ge(gmax_ready, 1)
                pt, done = claim("any")
                pe.transpose(pt[0:1, 0:P], gmax[:], ident[:]).then_inc(done, 1)

            def whole_pass():
                first = set()
                for l, kind, *key in PASS:
                    if kind in ("s", "st") and (l, kind) not in first:
                        banks_read(l, kind, S_BANKS + O_BANKS if kind == "s" else PROJ_BANKS)
                        first.add((l, kind))
                    if kind == "xt":
                        if key == [2 * l + 1, 0]:
                            pe.wait_ge(exp_done, tidx[l, NG - 1, NC - 1, TT - 1, HG - 1] + 1)
                        transposed_x(*key)
                    elif kind == "qk":
                        need_xT(2 * l, key[1])
                        project_qk(l, *key)
                    elif kind == "v":
                        values(l, *key)
                    elif kind == "s":
                        score(l, *key)
                    elif kind == "mt":
                        max_rows(l, *key)
                    elif kind == "st":
                        scores_t(l, *key)
                    elif kind == "pv":
                        if key[2] == 0 and key[0] == 0:
                            for tp in range(TT // 2):
                                in_sbuf("v", l, tp)
                        weigh_values(l, *key)
                    elif kind == "nm":
                        normalise(l, *key)
                    elif kind == "yt":
                        transposed_y(l, *key)
                    elif kind == "ao":
                        project_y(l, *key)
                    elif kind == "logit":
                        small_product("logit", 1, *key, projw, E0)
                    elif kind == "h1":
                        first_product(*key)
                    elif kind == "at":
                        transposed_a(*key)
                    elif kind == "g":
                        gates(*key)
                    elif kind == "hid":
                        hidden(*key)
                    elif kind == "fo":
                        last_product(*key)
                    elif kind == "route":
                        small_product("route", 3, *key, wr, NE)
                    elif kind == "up":
                        expert_up(*key)
                    elif kind == "down":
                        expert_down(*key)
                    elif kind == "any":
                        largest_gate()

            with pe.Fori(0, B) as b:
                begin_pass(pe, b)
                whole_pass()
                pe.wait_ge(flag_ready, 1)
                routed = pe.value_load(flag_i[:], min_val=0, max_val=1)
                with pe.If(routed > 0):
                    for u in range(len(ROUTED) + 1):
                        if u < len(ROUTED):
                            expert_up(*ROUTED[u])
                        if u:
                            expert_down(*ROUTED[u - 1])
                pe.drain().then_inc(part_done, 1)

        @block.scalar
        def _(act):
            unit = 0

            def setup_copy(dst, n=BANK):
                nonlocal unit
                act.wait_ge(w_full, unit + 1)
                src = bank[unit % 4][:, 0:n]
                if len(dst.shape) == 3:
                    src = src.rearrange("p (a n) -> p a n", a=dst.shape[1])
                act.activation(dst, src, ACT.Copy).then_inc(w_drained, 1)
                unit += 1

            for u in range(2):
                setup_copy(wout1T[:, BANK * u:BANK * (u + 1)])
            setup_copy(wout2T[:], D)
            for w in range(3):
                for u in range(4):
                    setup_copy(dT[w][:, 2 * u:2 * u + 2, :])
            for w in range(3):
                setup_copy(wqkv[1][:, :, D * w:D * (w + 1)])
            act.drain().then_inc(part_done, 1)

            def copy_xT(name, s, c, kd):
                pt = arrived(act, name, s, c, kd)
                act.activation(xnT[:, kd, BANK * c:BANK * (c + 1)], pt, ACT.Copy).then_inc(read_out(name, s, c, kd), 1)

            def copy_q(l, m, c, w):
                u = 4 * m + 2 * c + w
                pt = arrived(act, "qk", l, m, c, w)
                act.activation(qf[u], pt, ACT.Copy).then_inc(read_out("qk", l, m, c, w), 1)

            def part0(l, m, c, w):
                u = 4 * m + 2 * c + w
                bk, k = place["qk", l, m, c, w]
                if l == 0 and m == 0:
                    src = arrived(act, "qk", l, m, c, w)
                elif l == 0:
                    src = qf[u]
                    act.wait_ge(drained[bk], k + 1)
                else:
                    src = qs[u]
                    act.wait_ge(rope_ready, u + 1)
                act.activation(parts[:, m, w, 0, BANK * c:BANK * (c + 1)], src, ACT.Copy).then_inc(part0_ready, 1)

            def part1(l, m, c, w):
                u = 4 * m + 2 * c + w
                act.wait_ge(rest_ready, 8 * l + u + 1)
                act.activation(parts[:, m, w, 1, BANK * c:BANK * (c + 1)], qf[u], ACT.Copy).then_inc(part1_ready, 1)

            def copy_v(l, tp):
                pt = arrived(act, "v", l, tp)
                act.activation(vaug[:, 2 * tp:2 * tp + 2, :, 0:DH], pt.rearrange("p (t h d) -> p t h d", t=2, h=H),
                               ACT.Copy).then_inc(read_out("v", l, tp), 1)

            def weights(l, g, c, j, h):
                step, n = step_of[l, g, c, j], tidx[l, g, c, j, h]
                if h == 0 and step >= PBUF:
                    act.wait_ge(pv_done, step - PBUF + 1)
                a, z = query_range(j, c)
                act.wait_ge(st_full, n + 1)
                act.activation(probs[:, step % PBUF, h, a - BANK * c:z - BANK * c], st_bank[n % len(st_bank)][:, a - BANK * c:z - BANK * c],
                               ACT.Exp, scale=SCALE).then_inc(exp_done, 1)

            def copy_o(l, g, c):
                u = unit_of[l, g, c]
                act.wait_ge(pv_done, step_of[l, g, c, TPC * (c + 1) - 1] + 1)
                if u >= NC:
                    key = ("nm", l, g - 1, c) if g else ("nm", l - 1, NG - 1, c)
                    act.wait_ge(s_drained, sidx[key] + 1)
                act.activation(oT[:, BANK * c:BANK * (c + 1)], o_bank[c], ACT.Copy).then_inc(o_drained, 1)

            def gelu(c, o):
                if o >= OC:
                    return
                pt = arrived(act, "hid", c, o)
                n = OC * c + o
                if o >= 4:
                    act.wait_ge(h_used, (OC - 1) * c + o - 3)
                elif c:
                    bk, k = place["z2", c - 1]
                    act.wait_ge(full[bk], k + 1)
                act.activation(hsb[n % 4], pt, ACT.Gelu).then_inc(read_out("hid", c, o), 1)

            def relu(e, c):
                u = NC * (0 if e == NE else e + 1) + c
                pt = arrived(act, "he", e, c)
                if u >= 4:
                    act.wait_ge(hq_ready, u - 3)
                act.activation(hr[buffer_of(e, c)], pt, ACT.Relu).then_inc(relu_ready, 1)

            def whole_pass():
                for l, kind, *key in PASS:
                    if kind == "xt":
                        for kd in range(KD):
                            copy_xT("xt", *key, kd)
                    elif kind == "yt":
                        for kd in range(KD):
                            copy_xT("yt", l, *key, kd)
                    elif kind == "v":
                        copy_v(l, *key)
                    elif kind == "qk" and (l or key[0]):
                        copy_q(l, *key)
                    elif kind == "add":
                        part0(l, *key)
                    elif kind == "rest":
                        part1(l, *key)
                    elif kind == "st":
                        weights(l, *key)
                    elif kind == "o":
                        copy_o(l, *key)
                    elif kind == "tau":
                        c, = key
                        cs = slice(TPC * c, TPC * (c + 1))
                        act.wait_ge(delta_ready, c + 1)
                        act.activation(zt[:, cs, :], zt[:, cs, :], ACT.Sqrt).then_inc(sqrt_ready, 1)
                    elif kind == "at":
                        c, = key
                        pt = arrived(act, "at", c)
                        act.activation(aT[:, BANK * c:BANK * (c + 1)], pt[0:E0, :], ACT.Copy).then_inc(read_out("at", c), 1)
                    elif kind == "g":
                        c, = key
                        for n, name in enumerate(("g1", "g2")):
                            pt = arrived(act, name, c)
                            act.activation(gsb[2 * c + n], pt, ACT.Copy).then_inc(read_out(name, c), 1)
                    elif kind == "hid":
                        gelu(*key)
                    elif kind == "route":
                        c, = key
                        cs = slice(TPC * c, TPC * (c + 1))
                        act.wait_ge(gap_ready, c + 1)
                        act.activation(zsm[:, 1, cs], zsm[:, 0, cs], ACT.Exp).then_inc(egap_ready, 1)
                    elif kind == "up":
                        relu(*key)

            with act.Fori(0, B) as b:
                begin_pass(act, b)
                whole_pass()
                act.wait_ge(flag_ready, 1)
                routed = act.value_load(flag_i[:], min_val=0, max_val=1)
                with act.If(routed > 0):
                    for u in ROUTED:
                        relu(*u)
                act.drain().then_inc(part_done, 1)

        @block.gpsimd
        def _(pool):
            n = 0

            def done(ins):
                nonlocal n
                n += 1
                ins.then_inc(act_chain, 1)
                pool.wait_ge(act_chain, n)

            done(pool.memset(ident[:], 0.0))
            done(pool.memset(ident_b[:], 0.0))
            done(pool.memset(mask_b[:], 0.0))
            done(pool.memset(neg_half[:], -0.5))
            for t in (ident, ident_b):
                done(pool.affine_select(out=t[:], in_=t[:], compare_op=ALU.not_equal, fill=1.0, base=0,
                                        pattern=[[-1, P]], channel_multiplier=1))
            pool.affine_select(out=mask_b[:], in_=mask_b[:], compare_op=ALU.is_ge, fill=NEG, base=0,
                               pattern=[[-1, P]], channel_multiplier=1).then_inc(w_const, 1)

            def inverse_root(n, c, src=0):
                mv, veps, rstd = stats[src]
                pool.wait_ge(ln_var, NC * n + c + 1)
                tiles = slice(TPC * c, TPC * (c + 1))
                pool.tensor_tensor(rstd[:, tiles], veps[:, tiles], neg_half[:, tiles], ALU.pow).then_inc(ln_rstd, 1)

            for c in range(NC):
                inverse_root(0, c, 1)
            pool.drain().then_inc(part_done, 1)

            def rotated(m, c, w):
                u = 4 * m + 2 * c + w
                bk, k = place["qk", 1, m, c, w]
                pool.wait_ge(drained[bk], k + 1)
                if u >= 6:
                    pool.wait_ge(rope_ready, u - 1)
                cols = slice(BANK * c, BANK * (c + 1))
                pool.tensor_tensor(qc[u], qf[u], cos[:, cols], ALU.mult).then_inc(cos_ready, 1)
                if m:
                    pool.wait_ge(swap_ready, u + 1)
                    pool.tensor_tensor(qs[u], qs[u], sin[:, cols], ALU.mult).then_inc(sin_ready, 1)

            def mask(l, g, c, j, h):
                pool.wait_ge(exp_done, tidx[l, g, c, j, h] + 1)
                diag = probs[:, step_of[l, g, c, j] % PBUF, h, P * j - BANK * c:P * (j + 1) - BANK * c]
                pool.affine_select(out=diag, in_=diag, compare_op=ALU.is_ge, fill=0.0, base=0,
                                   pattern=[[1, P]], channel_multiplier=-1).then_inc(p_ready, 1)

            def entmax_power(c):
                cs = slice(TPC * c, TPC * (c + 1))
                pool.wait_ge(ent_var, c + 1)
                pool.tensor_tensor(zsm[:, 2, cs], zsm[:, 1, cs], neg_half[:, cs], ALU.pow).then_inc(ent_rstd, 1)

            with pool.Fori(0, B) as b:
                begin_pass(pool, b)
                for l, kind, *key in PASS:
                    if kind == "swap" and l:
                        rotated(*key)
                    elif kind == "st" and key[2] // TPC == key[1]:
                        mask(l, *key)
                    elif kind == "rstd":
                        inverse_root(LN_TURN[key[0]], key[1])
                    elif kind == "next":
                        for c in range(NC):
                            inverse_root(LN_TURN[4], c, 1)
                    elif kind == "logit":
                        entmax_power(*key)
                pool.drain().then_inc(part_done, 1)

        @block.vector
        def _(dve):
            links = 0

            def link(ins):
                nonlocal links
                links += 1
                ins.then_inc(dve_chain, 1)
                dve.wait_ge(dve_chain, links)

            dve.memset(up, 0.0).then_inc(up_zeroed, 1)
            dve.memset(vaug[:], 1.0)
            dve.memset(mx[:], LOWEST)
            for buf in range(NBUF):
                dve.memset(stk[ROWS_A:P, buf, 1, :, :], 1.0)
            for c in range(NC):
                dve.memset(o_bank[c], 0.0)

            def row_statistics(c, src):
                mv, veps, rstd = stats[src is x_in]
                tiles = range(TPC * c, TPC * (c + 1))
                for t in tiles:
                    ins = dve.bn_stats(st6[:, t, :], src[:, t, :])
                link(ins)
                for t in tiles:
                    ins = dve.bn_aggr(mv[:, t, :], st6[:, t, :])
                link(ins)
                cs = slice(TPC * c, TPC * (c + 1))
                dve.tensor_scalar(veps[:, cs], mv[:, cs, 1], LN_EPS, None, ALU.add).then_inc(ln_var, 1)

            def normalised(n, c, src):
                mv, veps, rstd = stats[src is x_in]
                dve.wait_ge(ln_rstd, NC * n + c + 1)
                for t in range(TPC * c, TPC * (c + 1)):
                    ins = dve.tensor_scalar(xn[:, t, :], src[:, t, :], mv[:, t, 0:1], rstd[:, t:t + 1],
                                            ALU.subtract, ALU.mult)
                ins.then_inc(xn_ready, 1)

            dve.wait_ge(x_loaded, 16)
            for c in range(NC):
                row_statistics(c, x_in)
            for c in range(NC):
                normalised(0, c, x_in)
            dve.drain().then_inc(part_done, 1)

            def swap_pairs(l, m, c, w):
                if l == 0:
                    return
                u = 4 * m + 2 * c + w
                bk, k = place["qk", l, m, c, w]
                dve.wait_ge(drained[bk], k + 1)
                if u >= 6:
                    dve.wait_ge(rest_ready, 8 + u - 1)
                dve.stream_shuffle(qs[u], qf[u], [i ^ 1 for i in range(32)]).then_inc(swap_ready, 1)
                if m == 0:
                    dve.wait_ge(swap_ready, u + 1)
                    dve.tensor_tensor(qs[u], qs[u], sin[:, BANK * c:BANK * (c + 1)], ALU.mult).then_inc(sin_ready, 1)

            def rotate(l, m, c, w):
                if l == 0:
                    return
                u = 4 * m + 2 * c + w
                dve.wait_ge(cos_ready, u + 1)
                dve.wait_ge(sin_ready, u + 1)
                dve.tensor_tensor(qs[u], qs[u], qc[u], ALU.add).then_inc(rope_ready, 1)

            def rest(l, m, c, w):
                u = 4 * m + 2 * c + w
                bk, k = place["qk", l, m, c, w]
                src = qs[u] if l else qf[u]
                dve.wait_ge(part0_ready, 8 * l + u + 1)
                if l == 0 and m == 0:
                    src = arrived(dve, "qk", l, m, c, w)
                dve.tensor_tensor(qf[u], src, parts[:, m, w, 0, BANK * c:BANK * (c + 1)], ALU.subtract).then_inc(rest_ready, 1)
                if l == 0 and m == 0:
                    dve.wait_ge(rest_ready, u + 1)
                    dve.sem_inc(drained[bk], 1)

            def part2(l, m, c, w):
                u = 4 * m + 2 * c + w
                dve.wait_ge(part1_ready, 8 * l + u + 1)
                cols = slice(BANK * c, BANK * (c + 1))
                dve.tensor_tensor(parts[:, m, w, 2, cols], qf[u], parts[:, m, w, 1, cols], ALU.subtract).then_inc(parts_ready, 1)

            def maximum(l, g, c, i, h, p, width):
                n = sidx["s", l, g, c, i, h, p]
                dve.wait_ge(s_full, n + 1)
                dve.tensor_reduce(mx[:, h, i, p:p + 1], s_bank[n % len(S_BANKS)][:, 0:width], AX.X, ALU.max).then_inc(s_drained, 1)

            def split_max(l, g, c):
                dve.wait_ge(s_drained, sidx["s", l, *score_keys(g, c)[-1][1:]] + 1)
                tiles = mx[:, :, TPC * c:TPC * (c + 1), :]
                link(dve.tensor_reduce(negm[:].rearrange("q i h -> q h i"), tiles, AX.X, ALU.max, negate=True))
                link(dve.tensor_copy(mparts[:, :, 0], negm[:]))
                link(dve.tensor_tensor(negr[:], negm[:], mparts[:, :, 0], ALU.subtract))
                link(dve.tensor_copy(mparts[:, :, 1], negr[:]))
                dve.tensor_tensor(mparts[:, :, 2], negr[:], mparts[:, :, 1], ALU.subtract).then_inc(mx_ready, 1)

            def max_rows(l, g, c):
                n = sidx["mt", l, g, c]
                dve.wait_ge(s_full, n + 1)
                if unit_of[l, g, c]:
                    dve.wait_ge(m_loaded, 16 * unit_of[l, g, c])
                rows = s_bank[n % len(S_BANKS)][0:NP * HG, 0:BANK // 2].bitcast(BF16)
                dve.tensor_copy(mT[:], rows).then_inc(s_drained, 1)

            def normalise(l, g, c):
                n = sidx["nm", l, g, c]
                dve.wait_ge(s_full, n + 1)
                dve.wait_ge(s_drained, n)
                src = s_bank[n % len(S_BANKS)].rearrange("q (t h v) -> q t h v", t=TPC, h=HG)
                link(dve.reciprocal(rec[:], src[:, :, :, DH]))
                dst = y[:, TPC * c:TPC * (c + 1), HG * DH * g:HG * DH * (g + 1)].rearrange("q t (h d) -> q t h d", h=HG)
                w = rec[:].rearrange("q t (h a) -> q t h a", a=1).broadcast_to([P, TPC, HG, DH])
                dve.tensor_tensor(dst, src[:, :, :, 0:DH], w, ALU.mult).then_inc(s_drained, 1)

            def add_to_x(tiles, pt, base, key):
                dve.tensor_tensor(x[:, tiles, :], pt.rearrange("p (t d) -> p t d", t=2), base[:, tiles, :], ALU.add)\
                    .then_inc(read_out(*key), 1)

            def settled(*keys):
                for key in keys:
                    bk, k = place[key]
                    dve.wait_ge(drained[bk], k + 1)

            def attention_residual(l, c):
                for tp in range(TPC // 2):
                    t = TPC * c + 2 * tp
                    pt = arrived(dve, "ao", l, c, tp)
                    add_to_x(slice(t, t + 2), pt, x if l else x_in, ("ao", l, c, tp))
                settled(*[("ao", l, c, tp) for tp in range(TPC // 2)])
                row_statistics(c, x)

            def wide(v):
                return v.rearrange("p (t a) -> p t a", a=1).broadcast_to([P, TPC, E0])

            def every(v):
                return v.rearrange("p (a k) -> p a k", a=1).broadcast_to([P, TPC, E0])

            def sorted_logits(c):
                cs = slice(TPC * c, TPC * (c + 1))
                zc_, zt_, zsm_ = zc[:, cs, :], zt[:, cs, :], zsm[:, :, cs]
                pt = arrived(dve, "logit", c)[:, 0:TPC * E0].rearrange("p (t e) -> p t e", t=TPC)
                link(dve.tensor_reduce(zsm_[:, 0, :], pt, AX.X, ALU.add))
                link(dve.tensor_scalar(zsm_[:, 0, :], zsm_[:, 0, :], 1.0 / E0, None, ALU.mult))
                dve.tensor_tensor(zc_, pt, wide(zsm_[:, 0, :]), ALU.subtract).then_inc(read_out("logit", c), 1)
                settled(("logit", c))
                link(dve.tensor_tensor(zt_, zc_, zc_, ALU.mult))
                link(dve.tensor_reduce(zsm_[:, 1, :], zt_, AX.X, ALU.add))
                ins = dve.tensor_scalar(zsm_[:, 1, :], zsm_[:, 1, :], 1.0 / E0, LN_EPS, ALU.mult, ALU.add)
                ins.then_inc(ent_var, 1)
                dve.wait_ge(ent_rstd, c + 1)
                link(dve.scalar_tensor_tensor(zc_, zc_, 0.5, wide(zsm_[:, 2, :]), ALU.mult, ALU.mult))
                link(dve.tensor_reduce(zsm_[:, 0, :], zc_, AX.X, ALU.max))
                link(dve.tensor_tensor(zc_, zc_, wide(zsm_[:, 0, :]), ALU.subtract))
                zs = cum[:, 0, 0:TPC, :]
                for t in range(TPC):
                    ins = dve.max(zs[:, t, 0:8], zc_[:, t, :])
                link(ins)
                for t in range(TPC):
                    ins = dve.match_replace(zt_[:, t, :], zs[:, t, 0:8], zc_[:, t, :], LOWEST)
                link(ins)
                for t in range(TPC):
                    ins = dve.max(zs[:, t, 8:16], zt_[:, t, :])
                link(ins)
                link(dve.tensor_tensor(cum[:, 0, TPC:2 * TPC, :], zs, zs, ALU.mult))
                a, nxt = cum[:, 0], (cum[:, 1], cum[:, 2])
                for r, s in enumerate((1, 2, 4, 8)):
                    z = nxt[r % 2]
                    dve.tensor_copy(z[:, :, 0:s], a[:, :, 0:s])
                    link(dve.tensor_tensor(z[:, :, s:E0], a[:, :, s:E0], a[:, :, 0:E0 - s], ALU.add))
                    a = z
                inv = kidx[:, 1, :].rearrange("p (a k) -> p a k", a=1).broadcast_to([P, 2 * TPC, E0])
                m = cum[:, 1]
                link(dve.tensor_tensor(m, a, inv, ALU.mult))
                link(dve.tensor_tensor(zt_, m[:, 0:TPC, :], m[:, 0:TPC, :], ALU.mult))
                link(dve.tensor_tensor(zt_, zt_, m[:, TPC:2 * TPC, :], ALU.subtract))
                link(dve.tensor_tensor(zt_, zt_, every(kidx[:, 1, :]), ALU.add))
                dve.tensor_scalar(zt_, zt_, 1e-34, None, ALU.max).then_inc(delta_ready, 1)

            def entmax(c):
                cs = slice(TPC * c, TPC * (c + 1))
                zc_, zt_, zu_, zsm_ = zc[:, cs, :], zt[:, cs, :], zu[:, cs, :], zsm[:, :, cs]
                m, zs = cum[:, 1], cum[:, 0, 0:TPC, :]
                dve.wait_ge(sqrt_ready, c + 1)
                tau = cum[:, 2, 0:TPC, :]
                link(dve.tensor_tensor(tau, m[:, 0:TPC, :], zt_, ALU.subtract))
                link(dve.tensor_tensor(zu_, tau, zs, ALU.is_le))
                link(dve.tensor_reduce(zsm_[:, 3, :], zu_, AX.X, ALU.add))
                link(dve.tensor_tensor(zu_, every(kidx[:, 0, :]), wide(zsm_[:, 3, :]), ALU.is_equal))
                link(dve.tensor_tensor(zu_, zu_, tau, ALU.mult))
                link(dve.tensor_reduce(zsm_[:, 3, :], zu_, AX.X, ALU.add))
                link(dve.tensor_tensor(zc_, zc_, wide(zsm_[:, 3, :]), ALU.subtract))
                link(dve.tensor_scalar(zc_, zc_, 0.0, None, ALU.max))
                dve.tensor_tensor(zu_, zc_, zc_, ALU.mult).then_inc(a_ready, 1)

            def gated(pt, bias, key, c, n, dst, src_key):
                settled((key, c))
                dve.scalar_tensor_tensor(dst, pt, bias[:, 0:1], gsb[2 * c + n], ALU.add, ALU.mult).then_inc(read_out(*src_key), 1)

            def ffn_residual(c):
                for tp in range(TPC // 2):
                    pt = arrived(dve, "fo", 0, c, tp)
                    add_to_x(slice(TPC * c + 2 * tp, TPC * c + 2 * tp + 2), pt, x, ("fo", 0, c, tp))
                settled(*[("fo", 0, c, tp) for tp in range(TPC // 2)])
                row_statistics(c, x)

            def router(c):
                cs = slice(TPC * c, TPC * (c + 1))
                pt = arrived(dve, "route", c)[:, 0:TPC * NE].rearrange("p (t e) -> p t e", t=TPC)
                dve.tensor_copy(zc[:, cs, 0:NE], pt).then_inc(read_out("route", c), 1)
                settled(("route", c))
                for t in range(TPC * c, TPC * (c + 1)):
                    ins = dve.max(zt[:, t, 0:8], zc[:, t, 0:NE])
                link(ins)
                dve.tensor_tensor(zsm[:, 0, cs], zt[:, cs, 1], zt[:, cs, 0], ALU.subtract).then_inc(gap_ready, 1)
                dve.wait_ge(egap_ready, c + 1)
                link(dve.tensor_scalar(zsm[:, 1, cs], zsm[:, 1, cs], 1.0, None, ALU.add))
                link(dve.reciprocal(zsm[:, 2, cs], zsm[:, 1, cs]))
                link(dve.tensor_scalar(zsm[:, 2, cs], zsm[:, 2, cs], 1.0, None, ALU.is_ge))
                link(dve.tensor_tensor(gate[:, cs], zc[:, cs, 0:NE], zt[:, cs, 0:1].broadcast_to([P, TPC, NE]), ALU.is_ge))
                link(dve.tensor_tensor(gate[:, cs], gate[:, cs], zsm[:, 2, cs].rearrange("p (t a) -> p t a", a=1)
                                       .broadcast_to([P, TPC, NE]), ALU.mult))
                if c == NC - 1:
                    dve.tensor_reduce(gmax[:], gate[:].rearrange("p t e -> p (t e)"), AX.X, ALU.max).then_inc(gmax_ready, 1)

            def square(e, c):
                u = NC * (0 if e == NE else e + 1) + c
                dve.wait_ge(relu_ready, u + 1)
                pt = arrived(dve, "he", e, c)
                dve.scalar_tensor_tensor(hq[buffer_of(e, c)], pt, 0.0, hr[buffer_of(e, c)], ALU.max, ALU.mult)\
                    .then_inc(hq_ready, 1)
                dve.wait_ge(hq_ready, u + 1)
                dve.sem_inc(read_out("he", e, c), 1)

            def add_expert(e, c):
                for tp in range(TPC // 2):
                    key = ("eo", e, c, tp)
                    pt = arrived(dve, *key)
                    t = TPC * c + 2 * tp
                    if e == NE:
                        add_to_x(slice(t, t + 2), pt, x, key)
                        continue
                    settled(("eo", e - 1 if e else NE, c, tp))
                    dve.scalar_tensor_tensor(x[:, t, :], pt[:, 0:D], gate[:, t, e:e + 1], x[:, t, :], ALU.mult, ALU.add)
                    dve.scalar_tensor_tensor(x[:, t + 1, :], pt[:, D:2 * D], gate[:, t + 1, e:e + 1], x[:, t + 1, :],
                                             ALU.mult, ALU.add).then_inc(read_out(*key), 1)

            def any_routed():
                pt = arrived(dve, "any")
                link(dve.tensor_reduce(flag[:], pt[0:1, 0:P], AX.X, ALU.max))
                dve.tensor_copy(flag_i[:], flag[:]).then_inc(flag_ready, 1)

            def whole_pass(pass_index):
                for l, kind, *key in PASS:
                    if kind == "s":
                        maximum(l, *key, dict(score_parts(key[2]))[key[4]])
                    elif kind == "mx":
                        split_max(l, *key)
                    elif kind == "mt":
                        max_rows(l, *key)
                    elif kind == "nm":
                        normalise(l, *key)
                    elif kind == "swap":
                        swap_pairs(l, *key)
                    elif kind == "add":
                        rotate(l, *key)
                    elif kind == "rest":
                        rest(l, *key)
                    elif kind == "last":
                        part2(l, *key)
                    elif kind == "ao":
                        if l == 0 and key == [0]:
                            dve.wait_ge(stored, 16 * pass_index + 16)
                        attention_residual(l, *key)
                    elif kind == "norm":
                        if key[0] == 4:
                            settled(*[("xt", 3, key[1], kd) for kd in range(KD)])
                        normalised(LN_TURN[key[0]], key[1], x if key[0] < 4 else x_in)
                    elif kind == "next":
                        dve.wait_ge(x_loaded, 16 * pass_index + 32)
                        for c in range(NC):
                            row_statistics(c, x_in)
                    elif kind == "logit":
                        sorted_logits(*key)
                    elif kind == "tau":
                        entmax(*key)
                    elif kind == "z1":
                        c, = key
                        pt = arrived(dve, "h1", c)
                        gated(pt, bias1, "g1", c, 0, z1[c], ("h1", c))
                    elif kind == "z2":
                        c, = key
                        pt = arrived(dve, "z2", c)
                        gated(pt, bias2, "g2", c, 1, z2[c], ("z2", c))
                    elif kind == "fo":
                        ffn_residual(*key)
                    elif kind == "route":
                        router(*key)
                    elif kind == "up":
                        square(*key)
                    elif kind == "down":
                        add_expert(*key)
                    elif kind == "any":
                        any_routed()

            with dve.Fori(0, B) as b:
                links = 0
                begin_pass(dve, b)
                whole_pass(b)
                dve.wait_ge(flag_ready, 1)
                routed = dve.value_load(flag_i[:], min_val=0, max_val=1)
                with dve.If(routed > 0):
                    for u in range(len(ROUTED) + 1):
                        if u < len(ROUTED):
                            square(*ROUTED[u])
                        if u:
                            add_expert(*ROUTED[u - 1])
                dve.drain().then_inc(x_done, 1)
                dve.drain().then_inc(part_done, 1)


_INS = ['L0_attn_x', 'L0_attn_w_qkv', 'L0_attn_w_out', 'L0_ffn_proj', 'L0_ffn_C1', 'L0_ffn_Win1', 'L0_ffn_Wout1',
        'L0_ffn_C2', 'L0_ffn_Win2', 'L0_ffn_Wout2', 'L1_attn_Wq_down', 'L1_attn_Wk_down', 'L1_attn_Wv_down',
        'L1_attn_Wq_up_c', 'L1_attn_Wq_up_e', 'L1_attn_Wk_up_c', 'L1_attn_Wk_up_e', 'L1_attn_Wv_up', 'L1_attn_Wc',
        'L1_ffn_Ws1', 'L1_ffn_Ws2', 'L1_ffn_W1', 'L1_ffn_W2', 'L1_ffn_Wr']


def rope_tables():
    import numpy as np
    half = DH // 2
    inv = (1.0 / np.float32(10000.0) ** (np.arange(0, half, 2, dtype=np.float32) / np.float32(half))).astype(np.float32)
    freqs = np.arange(T, dtype=np.float32)[:, None] * inv[None, :]
    emb = np.concatenate((freqs, freqs), axis=-1).T
    cos = np.ones((DH, T), np.float32)
    sin = np.zeros((DH, T), np.float32)
    cos[half:] = np.cos(emb)
    sin[half:] = np.sin(emb)
    sin[half::2] *= -1.0
    return np.tile(cos, (MH, 1)), np.tile(sin, (MH, 1))


def kernel(**inputs):
    import numpy as np
    import concourse.bacc as bacc
    from concourse.bass_utils import run_bass_kernel_spmd

    nc = bacc.Bacc("TRN2", target_bir_lowering=False, num_devices=1)
    cos, sin = rope_tables()
    k = np.arange(1, E0 + 1, dtype=np.float32)
    arrays = {f"in_{name}": np.ascontiguousarray(inputs[name]) for name in _INS}
    arrays["cos_table"] = cos
    arrays["sin_table"] = sin
    arrays["k_table"] = np.ascontiguousarray(np.broadcast_to(np.stack([k, 1.0 / k]).astype(np.float32), (P, 2, E0)))
    args = [nc.dram_tensor(name, a.shape, mybir.dt.from_np(a.dtype), kind="ExternalInput").ap() for name, a in arrays.items()]
    out = nc.dram_tensor("out", (B, T, D), F32, kind="ExternalOutput").ap()
    transformer_kernel(nc, *args, out)
    r = run_bass_kernel_spmd(nc, [arrays], core_ids=[0])
    return r.results[0]["out"]
```
